# Optimizing a Trainium2 kernel written in Bass

```python
import numpy as np
import jax
import jax.numpy as jnp

def _softmax(x, axis=-1):
    return jax.nn.softmax(x, axis=axis)

def _gelu(x):
    return jax.nn.gelu(x, approximate=True)

def _silu(x):
    return jax.nn.silu(x)

def _sigmoid(x):
    return jax.nn.sigmoid(x)

def _layernorm(x, axis=-1, eps=1e-05):
    m = jnp.mean(x, axis=axis, keepdims=True)
    v = jnp.var(x, axis=axis, keepdims=True)
    return (x - m) / jnp.sqrt(v + eps)

def _scatter_add(tgt, idx, src, axis=0):
    return tgt.at[idx].add(src)

def _segment_sum(src, seg, n):
    return jax.ops.segment_sum(src, seg, n)
kernel_name = 'mk_adaln_ffn_d2_seqx_r8_31f2a5'

def setup_inputs(seed: int=0):
    np.random.seed(seed)
    _w = jnp.asarray

    def _rec_inputs():
        import jax
        import jax.numpy as jnp
        _rk = jax.random.key(seed)
        x = -0.000125 + 0.9999 * jax.random.normal(jax.random.fold_in(_rk, 1), (4, 256, 256), jnp.float32)
        _lenS = 256 - jax.random.randint(jax.random.fold_in(_rk, 7), (4,), 0, max(1, 256 // 4) + 1, jnp.int32)
        _lenS2 = 256 - jax.random.randint(jax.random.fold_in(_rk, 8), (4,), 0, max(1, 256 // 4) + 1, jnp.int32)
        fside_BxSxS_0 = -1.52775e-05 + 0.999936 * jax.random.normal(jax.random.fold_in(_rk, 11), (4, 256, 256), jnp.float32)
        cond_512 = -5.03954e-05 + 1.00559 * jax.random.normal(jax.random.fold_in(_rk, 12), (4, 64), jnp.float32)
        return (x, fside_BxSxS_0, cond_512)
    x, fside_BxSxS_0, cond_512 = _rec_inputs()

    def _L0_cond_setup():
        import jax, jax.numpy as jnp
        from jax import lax
        import numpy as np
        B, T, C, TD = (8, 256, 256, 64)

        def _bi_wkv(r, k, v, w, u, time_emb):
            tf = jax.nn.sigmoid(jnp.sum(time_emb, axis=-1))[:, None, None]
            decay = jnp.exp(-jnp.exp(w.astype(jnp.float32)))[None, :] * (0.5 + 0.5 * tf[:, :, 0])
            kf = k.astype(jnp.float32)
            vf = v.astype(jnp.float32)
            ek = jnp.exp(jnp.minimum(kf, 30.0))
            ekv = ek * vf

            def step(carry, x):
                a, b = carry
                ekv_t, ek_t = x
                a = a * decay + ekv_t
                b = b * decay + ek_t
                return ((a, b), (a, b))
            ekv_t = jnp.swapaxes(ekv, 0, 1)
            ek_t = jnp.swapaxes(ek, 0, 1)
            init = (jnp.zeros_like(decay), jnp.zeros_like(decay))
            _, (nf, df) = lax.scan(step, init, (ekv_t, ek_t))
            _, (nb, db) = lax.scan(step, init, (ekv_t, ek_t), reverse=True)
            nf = jnp.swapaxes(nf, 0, 1)
            df = jnp.swapaxes(df, 0, 1)
            nb = jnp.swapaxes(nb, 0, 1)
            db = jnp.swapaxes(db, 0, 1)
            euk = jnp.exp(jnp.minimum(u.astype(jnp.float32)[None, None, :] + kf, 30.0))
            num = nf + nb - ekv + euk * vf
            den = df + db - ek + euk
            base = jax.nn.sigmoid(r.astype(jnp.float32)) * (num / jnp.maximum(den, 1e-08))
            out = base * (0.8 + 0.2 * tf)
            return out.astype(r.dtype)
        key = jax.random.key(seed)
        ks = jax.random.split(key, 6)
        return {'r': jax.random.normal(ks[0], (B, T, C), dtype=jnp.float32), 'k': jax.random.normal(ks[1], (B, T, C), dtype=jnp.float32), 'v': jax.random.normal(ks[2], (B, T, C), dtype=jnp.float32), 'w': jax.random.normal(ks[3], (C,), dtype=jnp.float32), 'u': jax.random.normal(ks[4], (C,), dtype=jnp.float32), 'time_emb': jax.random.normal(ks[5], (B, TD), dtype=jnp.float32)}
    _L0_cond_all = _L0_cond_setup()
    _L0_cond_in = {k: v for k, v in _L0_cond_all.items() if k in ('w', 'u')}
    del _L0_cond_all

    def _L0_ffn_setup():
        import jax, jax.numpy as jnp
        import numpy as np
        import math
        B, S, D = (2, 128, 256)
        H, KVH, HD = (16, 4, 128)
        E, K, FF = (8, 2, 896)
        EPS = 1e-05
        ROPE_BASE = 1000000.0

        def rmsnorm(x, w, eps=EPS):
            xf = x.astype(jnp.float32)
            var = jnp.mean(xf * xf, axis=-1, keepdims=True)
            return (xf * jax.lax.rsqrt(var + eps)).astype(x.dtype) * w

        def apply_rope(x, cos, sin):
            x1 = x[..., 0::2]
            x2 = x[..., 1::2]
            r1 = x1 * cos - x2 * sin
            r2 = x1 * sin + x2 * cos
            return jnp.stack([r1, r2], axis=-1).reshape(x.shape)
        key = jax.random.key(seed)
        ks = jax.random.split(key, 12)
        sc = 0.02
        inp = {'x': jax.random.normal(ks[0], (B, S, D), jnp.float32), 'ln_w': jnp.ones((D,), jnp.float32), 'ff_ln_w': jnp.ones((D,), jnp.float32), 'wq': jax.random.normal(ks[1], (D, H * HD), jnp.float32) * sc, 'wk': jax.random.normal(ks[2], (D, KVH * HD), jnp.float32) * sc, 'wv': jax.random.normal(ks[3], (D, KVH * HD), jnp.float32) * sc, 'wo': jax.random.normal(ks[4], (H * HD, D), jnp.float32) * sc, 'gate_w': jax.random.normal(ks[5], (D, E), jnp.float32) * sc, 'w1': jax.random.normal(ks[6], (E, D, FF), jnp.float32) * sc, 'w3': jax.random.normal(ks[7], (E, D, FF), jnp.float32) * sc, 'w2': jax.random.normal(ks[8], (E, FF, D), jnp.float32) * sc}
        return inp
    _L0_ffn_all = _L0_ffn_setup()
    _L0_ffn_in = {k: v for k, v in _L0_ffn_all.items() if k in ('ln_w', 'ff_ln_w', 'wq', 'wk', 'wv', 'wo', 'gate_w', 'w1', 'w3', 'w2')}
    del _L0_ffn_all

    def _L1_cond_setup():
        import jax, jax.numpy as jnp
        from jax import lax
        import numpy as np
        B, T, C, TD = (8, 256, 256, 64)

        def _bi_wkv(r, k, v, w, u, time_emb):
            tf = jax.nn.sigmoid(jnp.sum(time_emb, axis=-1))[:, None, None]
            decay = jnp.exp(-jnp.exp(w.astype(jnp.float32)))[None, :] * (0.5 + 0.5 * tf[:, :, 0])
            kf = k.astype(jnp.float32)
            vf = v.astype(jnp.float32)
            ek = jnp.exp(jnp.minimum(kf, 30.0))
            ekv = ek * vf

            def step(carry, x):
                a, b = carry
                ekv_t, ek_t = x
                a = a * decay + ekv_t
                b = b * decay + ek_t
                return ((a, b), (a, b))
            ekv_t = jnp.swapaxes(ekv, 0, 1)
            ek_t = jnp.swapaxes(ek, 0, 1)
            init = (jnp.zeros_like(decay), jnp.zeros_like(decay))
            _, (nf, df) = lax.scan(step, init, (ekv_t, ek_t))
            _, (nb, db) = lax.scan(step, init, (ekv_t, ek_t), reverse=True)
            nf = jnp.swapaxes(nf, 0, 1)
            df = jnp.swapaxes(df, 0, 1)
            nb = jnp.swapaxes(nb, 0, 1)
            db = jnp.swapaxes(db, 0, 1)
            euk = jnp.exp(jnp.minimum(u.astype(jnp.float32)[None, None, :] + kf, 30.0))
            num = nf + nb - ekv + euk * vf
            den = df + db - ek + euk
            base = jax.nn.sigmoid(r.astype(jnp.float32)) * (num / jnp.maximum(den, 1e-08))
            out = base * (0.8 + 0.2 * tf)
            return out.astype(r.dtype)
        key = jax.random.key(seed)
        ks = jax.random.split(key, 6)
        return {'r': jax.random.normal(ks[0], (B, T, C), dtype=jnp.float32), 'k': jax.random.normal(ks[1], (B, T, C), dtype=jnp.float32), 'v': jax.random.normal(ks[2], (B, T, C), dtype=jnp.float32), 'w': jax.random.normal(ks[3], (C,), dtype=jnp.float32), 'u': jax.random.normal(ks[4], (C,), dtype=jnp.float32), 'time_emb': jax.random.normal(ks[5], (B, TD), dtype=jnp.float32)}
    _L1_cond_all = _L1_cond_setup()
    _L1_cond_in = {k: v for k, v in _L1_cond_all.items() if k in ('w', 'u')}
    del _L1_cond_all

    def _L1_ffn_setup():
        import jax, jax.numpy as jnp
        import numpy as np
        FP8_MAX = 448.0
        GLOBAL_DIV = 448.0 * 6.0

        def _fp8(x):
            return x.astype(jnp.float8_e4m3fn).astype(jnp.float32)

        def _reorder_quantize_x(x, idx):
            scale = jnp.max(jnp.abs(x)) / GLOBAL_DIV
            xr = (x / scale)[:, idx]
            scale_x = jnp.max(jnp.abs(xr), axis=1, keepdims=True) / FP8_MAX
            qx = _fp8(xr / scale_x)
            return (qx, scale_x, scale)

        def _qlinear(qx, scale_x, scale, W, idx, out_idx=None):
            Wr = W[:, idx]
            w_scale = jnp.max(jnp.abs(Wr), axis=1, keepdims=True) / FP8_MAX
            qw = _fp8(Wr / w_scale)
            y = qx * scale_x @ (qw * w_scale).T * scale
            if out_idx is not None:
                y = y[:, out_idx]
            return y
        key = jax.random.key(seed)
        ks = jax.random.split(key, 6)
        B, S, H, I = (2, 128, 256, 704)
        return {'x': jax.random.normal(ks[0], (B, S, H), jnp.float32), 'w_gate': jax.random.normal(ks[1], (I, H), jnp.float32) * 0.02, 'w_up': jax.random.normal(ks[2], (I, H), jnp.float32) * 0.02, 'w_down': jax.random.normal(ks[3], (H, I), jnp.float32) * 0.02, 'up_reorder_index': jax.random.permutation(ks[4], jnp.arange(H, dtype=jnp.int64)), 'down_reorder_index': jax.random.permutation(ks[5], jnp.arange(I, dtype=jnp.int64))}
    _L1_ffn_all = _L1_ffn_setup()
    _L1_ffn_in = {k: v for k, v in _L1_ffn_all.items() if k in ('w_gate', 'w_up', 'w_down', 'up_reorder_index', 'down_reorder_index')}
    del _L1_ffn_all
    return {'x': x, 'fside_BxSxS_0': fside_BxSxS_0, 'cond_512': cond_512, 'L0_cond_w': _L0_cond_in['w'], 'L0_cond_u': _L0_cond_in['u'], 'L0_ffn_ln_w': _L0_ffn_in['ln_w'], 'L0_ffn_ff_ln_w': _L0_ffn_in['ff_ln_w'], 'L0_ffn_wq': _L0_ffn_in['wq'], 'L0_ffn_wk': _L0_ffn_in['wk'], 'L0_ffn_wv': _L0_ffn_in['wv'], 'L0_ffn_wo': _L0_ffn_in['wo'], 'L0_ffn_gate_w': _L0_ffn_in['gate_w'], 'L0_ffn_w1': _L0_ffn_in['w1'], 'L0_ffn_w3': _L0_ffn_in['w3'], 'L0_ffn_w2': _L0_ffn_in['w2'], 'L1_cond_w': _L1_cond_in['w'], 'L1_cond_u': _L1_cond_in['u'], 'L1_ffn_w_gate': _L1_ffn_in['w_gate'], 'L1_ffn_w_up': _L1_ffn_in['w_up'], 'L1_ffn_w_down': _L1_ffn_in['w_down'], 'L1_ffn_up_reorder_index': _L1_ffn_in['up_reorder_index'], 'L1_ffn_down_reorder_index': _L1_ffn_in['down_reorder_index']}

def reference(x, fside_BxSxS_0, cond_512, L0_cond_w, L0_cond_u, L0_ffn_ln_w, L0_ffn_ff_ln_w, L0_ffn_wq, L0_ffn_wk, L0_ffn_wv, L0_ffn_wo, L0_ffn_gate_w, L0_ffn_w1, L0_ffn_w3, L0_ffn_w2, L1_cond_w, L1_cond_u, L1_ffn_w_gate, L1_ffn_w_up, L1_ffn_w_down, L1_ffn_up_reorder_index, L1_ffn_down_reorder_index):
    import jax
    import jax.numpy as jnp

    def _L0_cond_ref(r, k, v, w, u, time_emb):
        import jax, jax.numpy as jnp
        from jax import lax
        import numpy as np
        B, T, C, TD = (8, 256, 256, 64)

        def _bi_wkv(r, k, v, w, u, time_emb):
            tf = jax.nn.sigmoid(jnp.sum(time_emb, axis=-1))[:, None, None]
            decay = jnp.exp(-jnp.exp(w.astype(jnp.float32)))[None, :] * (0.5 + 0.5 * tf[:, :, 0])
            kf = k.astype(jnp.float32)
            vf = v.astype(jnp.float32)
            ek = jnp.exp(jnp.minimum(kf, 30.0))
            ekv = ek * vf

            def step(carry, x):
                a, b = carry
                ekv_t, ek_t = x
                a = a * decay + ekv_t
                b = b * decay + ek_t
                return ((a, b), (a, b))
            ekv_t = jnp.swapaxes(ekv, 0, 1)
            ek_t = jnp.swapaxes(ek, 0, 1)
            init = (jnp.zeros_like(decay), jnp.zeros_like(decay))
            _, (nf, df) = lax.scan(step, init, (ekv_t, ek_t))
            _, (nb, db) = lax.scan(step, init, (ekv_t, ek_t), reverse=True)
            nf = jnp.swapaxes(nf, 0, 1)
            df = jnp.swapaxes(df, 0, 1)
            nb = jnp.swapaxes(nb, 0, 1)
            db = jnp.swapaxes(db, 0, 1)
            euk = jnp.exp(jnp.minimum(u.astype(jnp.float32)[None, None, :] + kf, 30.0))
            num = nf + nb - ekv + euk * vf
            den = df + db - ek + euk
            base = jax.nn.sigmoid(r.astype(jnp.float32)) * (num / jnp.maximum(den, 1e-08))
            out = base * (0.8 + 0.2 * tf)
            return out.astype(r.dtype)
        return _bi_wkv(r, k, v, w, u, time_emb)

    def _L0_ffn_ref(x, ln_w, ff_ln_w, wq, wk, wv, wo, gate_w, w1, w3, w2):
        import jax, jax.numpy as jnp
        import numpy as np
        import math
        B, S, D = (2, 128, 256)
        H, KVH, HD = (16, 4, 128)
        E, K, FF = (8, 2, 896)
        EPS = 1e-05
        ROPE_BASE = 1000000.0

        def rmsnorm(x, w, eps=EPS):
            xf = x.astype(jnp.float32)
            var = jnp.mean(xf * xf, axis=-1, keepdims=True)
            return (xf * jax.lax.rsqrt(var + eps)).astype(x.dtype) * w

        def apply_rope(x, cos, sin):
            x1 = x[..., 0::2]
            x2 = x[..., 1::2]
            r1 = x1 * cos - x2 * sin
            r2 = x1 * sin + x2 * cos
            return jnp.stack([r1, r2], axis=-1).reshape(x.shape)
        Bx, Sx, Dx = x.shape
        residual = x
        h = rmsnorm(x, ln_w)
        q = (h @ wq).reshape(Bx, Sx, H, HD)
        k = (h @ wk).reshape(Bx, Sx, KVH, HD)
        v = (h @ wv).reshape(Bx, Sx, KVH, HD)
        pos = jnp.arange(Sx, dtype=jnp.float32)
        inv_freq = ROPE_BASE ** (-jnp.arange(0, HD, 2, dtype=jnp.float32) / HD)
        ang = pos[:, None] * inv_freq[None, :]
        cos = jnp.cos(ang)[None, :, None, :]
        sin = jnp.sin(ang)[None, :, None, :]
        q = apply_rope(q, cos, sin)
        k = apply_rope(k, cos, sin)
        rep = H // KVH
        k = jnp.repeat(k, rep, axis=2)
        v = jnp.repeat(v, rep, axis=2)
        scores = jnp.einsum('bqhd,bkhd->bhqk', q, k) / math.sqrt(HD)
        causal = jnp.tril(jnp.ones((Sx, Sx), dtype=bool))
        scores = jnp.where(causal[None, None], scores, jnp.finfo(scores.dtype).min)
        attn = jax.nn.softmax(scores, axis=-1)
        o = jnp.einsum('bhqk,bkhd->bqhd', attn, v).reshape(Bx, Sx, H * HD)
        x = o @ wo + residual
        residual = x
        h = rmsnorm(x, ff_ln_w)
        ht = h.reshape(-1, Dx)
        logits = ht @ gate_w
        top_vals, top_idx = jax.lax.top_k(logits, K)
        gates = jax.nn.softmax(top_vals, axis=-1)
        out = jnp.zeros_like(ht)
        for e in range(E):
            we = jnp.sum(gates * (top_idx == e), axis=-1)
            ye = jax.nn.silu(ht @ w1[e]) * (ht @ w3[e]) @ w2[e]
            out = out + we[:, None] * ye
        return out.reshape(Bx, Sx, Dx) + residual

    def _L1_cond_ref(r, k, v, w, u, time_emb):
        import jax, jax.numpy as jnp
        from jax import lax
        import numpy as np
        B, T, C, TD = (8, 256, 256, 64)

        def _bi_wkv(r, k, v, w, u, time_emb):
            tf = jax.nn.sigmoid(jnp.sum(time_emb, axis=-1))[:, None, None]
            decay = jnp.exp(-jnp.exp(w.astype(jnp.float32)))[None, :] * (0.5 + 0.5 * tf[:, :, 0])
            kf = k.astype(jnp.float32)
            vf = v.astype(jnp.float32)
            ek = jnp.exp(jnp.minimum(kf, 30.0))
            ekv = ek * vf

            def step(carry, x):
                a, b = carry
                ekv_t, ek_t = x
                a = a * decay + ekv_t
                b = b * decay + ek_t
                return ((a, b), (a, b))
            ekv_t = jnp.swapaxes(ekv, 0, 1)
            ek_t = jnp.swapaxes(ek, 0, 1)
            init = (jnp.zeros_like(decay), jnp.zeros_like(decay))
            _, (nf, df) = lax.scan(step, init, (ekv_t, ek_t))
            _, (nb, db) = lax.scan(step, init, (ekv_t, ek_t), reverse=True)
            nf = jnp.swapaxes(nf, 0, 1)
            df = jnp.swapaxes(df, 0, 1)
            nb = jnp.swapaxes(nb, 0, 1)
            db = jnp.swapaxes(db, 0, 1)
            euk = jnp.exp(jnp.minimum(u.astype(jnp.float32)[None, None, :] + kf, 30.0))
            num = nf + nb - ekv + euk * vf
            den = df + db - ek + euk
            base = jax.nn.sigmoid(r.astype(jnp.float32)) * (num / jnp.maximum(den, 1e-08))
            out = base * (0.8 + 0.2 * tf)
            return out.astype(r.dtype)
        return _bi_wkv(r, k, v, w, u, time_emb)

    def _L1_ffn_ref(x, w_gate, w_up, w_down, up_reorder_index, down_reorder_index):
        import jax, jax.numpy as jnp
        import numpy as np
        FP8_MAX = 448.0
        GLOBAL_DIV = 448.0 * 6.0

        def _fp8(x):
            return x.astype(jnp.float8_e4m3fn).astype(jnp.float32)

        def _reorder_quantize_x(x, idx):
            scale = jnp.max(jnp.abs(x)) / GLOBAL_DIV
            xr = (x / scale)[:, idx]
            scale_x = jnp.max(jnp.abs(xr), axis=1, keepdims=True) / FP8_MAX
            qx = _fp8(xr / scale_x)
            return (qx, scale_x, scale)

        def _qlinear(qx, scale_x, scale, W, idx, out_idx=None):
            Wr = W[:, idx]
            w_scale = jnp.max(jnp.abs(Wr), axis=1, keepdims=True) / FP8_MAX
            qw = _fp8(Wr / w_scale)
            y = qx * scale_x @ (qw * w_scale).T * scale
            if out_idx is not None:
                y = y[:, out_idx]
            return y
        B, S, H = x.shape
        xf = x.reshape(B * S, H)
        qx, sx, sc = _reorder_quantize_x(xf, up_reorder_index)
        g = _qlinear(qx, sx, sc, w_gate, up_reorder_index, out_idx=down_reorder_index)
        u = _qlinear(qx, sx, sc, w_up, up_reorder_index, out_idx=down_reorder_index)
        t = jax.nn.silu(g) * u
        qt, st, sct = _reorder_quantize_x(t, down_reorder_index)
        y = _qlinear(qt, st, sct, w_down, down_reorder_index)
        return y.reshape(B, S, H)
    x = x + _L0_ffn_ref(_L0_cond_ref(x, fside_BxSxS_0, fside_BxSxS_0, L0_cond_w, L0_cond_u, cond_512), L0_ffn_ln_w, L0_ffn_ff_ln_w, L0_ffn_wq, L0_ffn_wk, L0_ffn_wv, L0_ffn_wo, L0_ffn_gate_w, L0_ffn_w1, L0_ffn_w3, L0_ffn_w2)
    x = x + _L1_ffn_ref(_L1_cond_ref(x, fside_BxSxS_0, fside_BxSxS_0, L1_cond_w, L1_cond_u, cond_512), L1_ffn_w_gate, L1_ffn_w_up, L1_ffn_w_down, L1_ffn_up_reorder_index, L1_ffn_down_reorder_index)
    return x

_drawn_inputs = setup_inputs


def setup_inputs(seed=0):
    import zlib

    import numpy as np

    out = dict(_drawn_inputs(seed))
    spreads = {'L0_ffn_ln_w': (1.0, 0.2), 'L0_ffn_ff_ln_w': (1.0, 0.6)}
    factors = {'L0_ffn_wq': 8.0,
     'L0_ffn_wk': 8.0,
     'L0_ffn_gate_w': 3.428,
     'L0_ffn_w1': 2.96,
     'L0_ffn_w3': 2.893,
     'L0_ffn_w2': 2.913,
     'L1_cond_w': 8.0,
     'L1_cond_u': 8.0,
     'L1_ffn_w_gate': 7.967,
     'L1_ffn_w_up': 7.911,
     'L1_ffn_w_down': 7.779}
    for name, (base, spread) in spreads.items():
        noise = np.random.default_rng([zlib.crc32(name.encode()), seed]).standard_normal(out[name].shape)
        drawn = base * np.exp(spread * noise) if base else spread * noise
        out[name] = jnp.asarray(drawn.astype(out[name].dtype))
    for name, factor in factors.items():
        out[name] = (out[name] * factor).astype(out[name].dtype)
    return out
```

```python
import numpy as np
import concourse.bass as bass
from concourse import mybir
from contextlib import ExitStack

F32 = mybir.dt.float32
F16 = mybir.dt.float16
BF16 = mybir.dt.bfloat16
I32 = mybir.dt.int32
U32 = mybir.dt.uint32
ALU = mybir.AluOpType
ACT = mybir.ActivationFunctionType
AX = mybir.AxisListType

P = 128
B, S, D = 4, 256, 256
TT = S // P
NT = B * TT
C = D // P
H, KVH, HD = 16, 4, 128
NE, FF = 8, 896
FC = FF // P
FA, FB = 4 * P, FF - 4 * P
MT = 2 * B * S // P + NE - 1
SLOTS = MT * P
WEXP = C * FF * 2 + FC * D
RING = 3
INTER = 704
IQ = 88
NI = INTER // IQ
IH = INTER // 2
WS = 64.0
EPS = 1e-5
QKV = (H + 2 * KVH) * HD
PAIR = 2 * S
KU = 2 * KVH
QU = 2 * H
SCALE = float(HD) ** -0.5
BLK = 3 * P
FP8_MAX = 448.0
MAGIC = 1.5 * 2.0 ** 20
FP8_LEAST = 2.0 ** -6


def constants():
    pos = np.arange(S, dtype=np.float32)
    inv = np.float32(1e6) ** (-np.arange(0, HD, 2, dtype=np.float32) / np.float32(HD))
    ang = (pos[:, None] * inv[None, :].astype(np.float32)).astype(np.float32)
    cos, sin = np.cos(ang).T, np.sin(ang).T
    rope = np.stack([np.concatenate([cos, cos]), np.concatenate([-sin, sin])], 1) / WS
    diag = np.where(np.arange(P)[None, :] > np.arange(P)[:, None], -1e38, 0.0)
    mask = np.concatenate([diag, np.zeros((P, P)), diag], 1)
    before = (np.arange(P)[:, None] < np.arange(P)[None, :]).astype(np.float32)
    iota = np.tile(np.arange(NE, dtype=np.float32), (P, 1))
    tiles = np.tile(np.arange(MT, dtype=np.float32), (P, 1))
    consts = np.concatenate([np.eye(P), mask, before, np.ones((P, P)), iota, tiles, rope.reshape(P, -1)], 1)
    return np.ascontiguousarray(consts, dtype=np.float32)


def build(nc, t, out, dbg=None):
    ctx = ExitStack()
    with ctx:
        def sb(name, shape, dt=F32):
            return ctx.enter_context(nc.sbuf_tensor(name, shape, dt))

        def sem(name):
            return ctx.enter_context(nc.semaphore(name))

        def cut(region, offset, count, dt=F32):
            v = region[:, offset:offset + count]
            return v if dt == F32 else v.bitcast(dt)

        CN = P + BLK + P + P + NE + MT + 2 * S
        con = sb("con", [P, CN])
        ident = con[:, 0:P]
        mask = con[:, P:P + BLK]
        before = con[:, P + BLK:2 * P + BLK]
        ones = con[:, 2 * P + BLK:3 * P + BLK]
        o = 3 * P + BLK
        iota_e = con[:, o:o + NE]
        iota_t = con[:, o + NE:o + NE + MT]
        o += NE + MT
        rope_cos = con[:, o:o + S]
        rope_sin = con[:, o + S:o + 2 * S]

        stage_words = C * QKV
        wreg = sb("wreg", [P, RING * WEXP + 512])
        stage = cut(wreg, 0, stage_words).rearrange("p (c n) -> p c n", c=C)
        stage_wo = cut(wreg, 0, H * D).rearrange("p (h n) -> p h n", h=H)
        qkv16 = cut(wreg, stage_words, C * QKV, F16).rearrange("p (s c n) -> p s c n", s=2, c=C)
        wo16 = cut(wreg, 2 * stage_words, H * D, F16).rearrange("p (s h n) -> p s h n", s=2, h=H)

        AW = 4096 + 4096 + 2048 + 8192
        areg = sb("areg", [P, AW])
        kT = cut(areg, 0, 4096, F16).rearrange("p (s h n) -> p s h n", s=2, h=KVH)
        v16 = cut(areg, 4096, 4096, F16).rearrange("p (s i n) -> p s i n", s=2, i=NT)
        hT = cut(areg, 8192, 2048, F16).rearrange("p (s c n) -> p s c n", s=2, c=C)
        oT = cut(areg, 10240, 8192, F16).rearrange("p (s h n) -> p s h n", s=2, h=H)
        E = cut(areg, 0, 4096).rearrange("p (b k n) -> p b k n", b=B, k=2)
        fT = cut(areg, 4096, 2048).rearrange("p (b n) -> p b n", b=B)
        f_tok = cut(areg, 6144, 2048).rearrange("p (b i n) -> p b i n", b=B, i=TT)
        fwd = cut(areg, 10240, 1024).rearrange("p (k n) -> p k n", k=2)
        bwd = cut(areg, 11264, 1024).rearrange("p (k n) -> p k n", k=2)
        U = cut(areg, 12288, 1024).rearrange("p (k n) -> p k n", k=2)
        rat = cut(areg, 13312, 512)
        kmin = cut(areg, 13824, 512)
        xn = cut(areg, 14336, 512)
        sg = cut(areg, 14848, 2048).rearrange("p (b n) -> p b n", b=B)
        x_tok = cut(areg, 16896, 1536)
        x_in = sb("x_in", [P, B, TT * D])
        xs = cut(areg, 0, 2 * D).rearrange("p (k n) -> p k n", k=2)
        xsT = cut(areg, 512, 2 * D).rearrange("p (k n) -> p k n", k=2)
        eh = cut(areg, 1024, FF)
        hh = cut(areg, 1920, FF)
        hhT = cut(areg, 2816, FF).rearrange("p (c n) -> p c n", c=FC)
        ysb = cut(areg, 3712, 2 * D).rearrange("p (k n) -> p k n", k=2)
        h2 = cut(areg, 4224, NT * D).rearrange("p (i n) -> p i n", i=NT)
        h2T = cut(areg, 6272, 2 * D).rearrange("p (k n) -> p k n", k=2)
        y1 = cut(areg, 6784, 2 * D).rearrange("p (k n) -> p k n", k=2)
        y2 = cut(areg, 7296, 2 * D).rearrange("p (k n) -> p k n", k=2)
        xq = cut(areg, 7808, 5 * D).rearrange("p (k n) -> p k n", k=5)
        qx = cut(areg, 9088, D // 2, BF16)
        qxT = cut(areg, 9216, D // 2, BF16).rearrange("p (c n) -> p c n", c=C)
        gw = cut(areg, 9344, 5 * INTER).rearrange("p (k n) -> p k n", k=5)
        qt = cut(areg, 12864, INTER // 2, BF16)
        qtT = cut(areg, 13216, NI * P // 2, BF16).rearrange("p (c n) -> p c n", c=NI)
        yo = cut(areg, 13728, 2 * D).rearrange("p (k n) -> p k n", k=2)

        x0 = sb("x0", [P, NT, D])
        ratio1 = sb("ratio1", [P, NT, D])
        x1 = x0
        wln = sb("wln", [P, C])
        ffln = sb("ffln", [P, D])
        wu = sb("wu", [P, 4, C])
        cond = sb("cond", [P, B, 64])
        tf = sb("tf", [P, 8, B])
        dec = sb("dec", [P, 3, 2, C])
        decay = sb("decay", [P, 2, C, B])
        gate_w = sb("gate_w", [P, C, NE])
        small = sb("small", [P, 64])

        q16 = sb("q16", [P, 2, 2, PAIR], F16)
        t1 = sb("t1", [P, PAIR])
        t2 = sb("t2", [P, PAIR])
        qr = sb("qr", [P, 2, PAIR])
        pr = sb("pr", [P, 2, 2, BLK])
        pT = sb("pT", [P, 2, 2, 2, BLK], F16)
        mx = sb("mx", [P, 2, 2, 4])
        sums = sb("sums", [P, 2, 2, 4])
        nhalf = sb("nhalf", [P, 4])
        ssq = sb("ssq", [P, 4, NT])

        srow = cut(areg, 14240, 2 * INTER + D)
        q1w = cut(areg, 15904, C * INTER, BF16).rearrange("p (m c n) -> p m c n", m=2, c=C)
        q1d = cut(areg, 17312, NI * D // 2, BF16).rearrange("p (c n) -> p c n", c=NI)
        rows = cut(wreg, 2 * WEXP, 2048)
        grid = cut(wreg, 2 * WEXP + 2048, 2048)
        rq = cut(wreg, 2 * WEXP + 4096, 1024, BF16)
        wmax = sb("wmax", [P, 3, NI])
        winv = sb("winv", [P, 3, NI])
        wscale = sb("wscale", [P, 3, NI])
        diag = sb("diag", [P, P])
        didx = sb("didx", [IQ, NI], I32)

        pb = [ctx.enter_context(nc.psum_tensor(f"pb{i}", [P, 512], F32)) for i in range(2)]
        sc2 = ctx.enter_context(nc.psum_tensor("sc2", [P, 2, 512], F32))
        pt2 = ctx.enter_context(nc.psum_tensor("pt2", [P, 2, 512], F32))
        po = ctx.enter_context(nc.psum_tensor("po", [P, 512], F32))
        pw = ctx.enter_context(nc.psum_tensor("pw", [P, 512], F32))
        gat = cut(wreg, 2 * WEXP + 5120, NI * IQ)

        rt = sb("rt", [P, 14, NT * NE])
        lg, M1, M2, MK, tots, pos, prod = (rt[:, k, :] for k in range(7))
        m8 = rt[:, 7, :]
        i8 = rt[:, 8, :].bitcast(U32)
        car = rt[:, 9:11, :].rearrange("p a n -> p (a n)")[:, 0:(NT + 1) * NE]
        idf = rt[:, 11, 0:2 * NT]
        gts = rt[:, 12, :].rearrange("p (k n) -> p k n", n=NT)
        ex8 = rt[:, 13, :].rearrange("p (k n) -> p k n", n=NE)
        exi = sb("exi", [P, 2, NE], I32)
        slotf = sb("slotf", [P, 2, NT])
        sloti = sb("sloti", [P, 2, NT], I32)
        cmp = sb("cmp", [P, MT * NE])
        tmap = sb("tmap", [P, 2, MT])
        tmi = sb("tmi", [1, MT], I32)
        endi = sb("endi", [1, NE], I32)
        identb = sb("identb", [P, P], BF16)
        rs = sb("rs", [P, 10, NT])

        xs_dram = nc.dram_tensor("xs_dram", (SLOTS, D), F32).ap()
        ys_dram = nc.dram_tensor("ys_dram", (SLOTS, D), F32).ap()

        names = """con_in par_in qkv_in wo_in didx_in gatew_in upw_in downw_in zero_out scatter_out
            fT_done fT_copied kmin_ready ek_ready tfsum tf_exp dec_exp sg_exp ku_ready uexp_ready u_ready u_used
            ratT_ready rat_done x0_ready ssq_ready rstd_ready xn_ready hTp_done hi_done hlo_done ms_done act_link dve_link pool_link
            qkvhi_done qkvlo_done wohi_done wolo_done
            proj_done rope_done radd_done qhi_done qlo_done v_done vhi_done vlo_done
            score_done max_done nmax_done exp_done recip_done norm_done pT_done pThi_done pTlo_done
            av_done ohi_done olo_done wo_done x1a_done
            ssq2_ready rstd2_ready h2_ready h2T_done h2T_copied gate_done lg_ready d_ready ge_ready mk_ready rank_done slots_ready tmap_ready
            rq_ready rqT_done rq_copied diag_ready diag_used srow_done prep_dve
            w_ready tiles_done xs_free xT_done xT_copied upa_done upb_done expa_done expb_done silua_done silub_done
            hT_done hT_copied down_done y_copied moe_link
            comb_in x1_ready sgx_ready qx_ready qxT_done qxT_copied gu_done g_ready ge1_ready gu_read qt_ready qtT_done qtT_copied dn_done yo_ready out_done
            dve_paused pool_paused identb_ready rows_in gate_tile yo_read sx_ready act2_link g1_ready""".split()
        s = {n: sem(n) for n in names}
        s_f = [sem(f"f_in{b}") for b in range(B)]
        s_x = [sem(f"x_in{b}") for b in range(B)]
        s_w = [sem(f"w_in{k}") for k in range(RING)]
        s_xs = [sem(f"xs_in{k}") for k in range(2)]
        s_y = [sem(f"y_out{k}") for k in range(2)]
        s_g = [sem(f"gather_in{k}") for k in range(2)]
        s_o = [sem(f"out_out{k}") for k in range(2)]

        block = ctx.enter_context(nc.Block())

        def tokens(a, b):
            return a[b].rearrange("(i p) d -> p i d", p=P)

        def load_expert(eng, e):
            base = (e % RING) * WEXP
            n = C * FF
            eng.dma_start(wreg[:, base:base + n].rearrange("p (c n) -> p c n", c=C),
                          t["L0_ffn_w1"][e].rearrange("(c p) n -> p c n", p=P)).then_inc(s_w[e % RING], 16)
            eng.dma_start(wreg[:, base + n:base + 2 * n].rearrange("p (c n) -> p c n", c=C),
                          t["L0_ffn_w3"][e].rearrange("(c p) n -> p c n", p=P)).then_inc(s_w[e % RING], 16)
            eng.dma_start(wreg[:, base + 2 * n:base + WEXP].rearrange("p (c n) -> p c n", c=FC),
                          t["L0_ffn_w2"][e].rearrange("(c p) n -> p c n", p=P)).then_inc(s_w[e % RING], 16)

        @block.sync
        def _(sp):
            sp.dma_start(con[:, :], t["consts"]).then_inc(s["con_in"], 16)
            for b in range(B):
                sp.dma_start(f_tok[:, b], tokens(t["fside_BxSxS_0"], b)).then_inc(s_f[b], 16)
            with nc.allow_non_contiguous_dma(reason="short vectors, one element a partition"):
                for k, n in enumerate(("L0_cond_w", "L0_cond_u", "L1_cond_w", "L1_cond_u")):
                    sp.dma_start(wu[:, k], t[n].rearrange("(c p) -> p c", p=P)).then_inc(s["par_in"], 16)
                sp.dma_start(wln[:, :], t["L0_ffn_ln_w"].rearrange("(c p) -> p c", p=P)).then_inc(s["par_in"], 16)
                sp.dma_start(didx[:, :], t["L1_ffn_down_reorder_index"].rearrange("(c p) -> p c", p=IQ))\
                    .then_inc(s["didx_in"], 16)
            sp.dma_start(cond[:, :, :], t["cond_512"].rearrange("(a b) n -> a b n", a=1).to_broadcast([P, B, 64]))\
                .then_inc(s["par_in"], 16)
            sp.dma_start(ffln[:, :], t["L0_ffn_ff_ln_w"].rearrange("(a n) -> a n", a=1).to_broadcast([P, D]))\
                .then_inc(s["par_in"], 16)
            sp.dma_start(gate_w[:, :, :], t["L0_ffn_gate_w"].rearrange("(c p) n -> p c n", p=P))\
                .then_inc(s["par_in"], 16)
            for b in range(B):
                sp.dma_start(x_in[:, b].rearrange("p (i d) -> p i d", i=TT), tokens(t["x"], b)).then_inc(s_x[b], 16)
            at = 0
            for n, w in (("L0_ffn_wq", H * HD), ("L0_ffn_wk", KVH * HD), ("L0_ffn_wv", KVH * HD)):
                sp.dma_start(stage[:, :, at:at + w], t[n].rearrange("(c p) n -> p c n", p=P)).then_inc(s["qkv_in"], 16)
                at += w
            sp.wait_ge(s["ms_done"], 1)
            sp.dma_start(xs_dram.rearrange("(t p) n -> p t n", p=P),
                         t2[:, 0:D].rearrange("p (a n) -> p a n", a=1).to_broadcast([P, MT, D])).then_inc(s["zero_out"], 16)
            sp.wait_ge(s["qkvhi_done"], 1)
            sp.wait_ge(s["qkvlo_done"], 1)
            sp.dma_start(stage_wo, t["L0_ffn_wo"].rearrange("(h p) n -> p h n", p=P)).then_inc(s["wo_in"], 16)
            sp.wait_ge(s["wohi_done"], 1)
            sp.wait_ge(s["wolo_done"], 1)
            load_expert(sp, 0)
            sp.wait_ge(s["wo_done"], NT)
            load_expert(sp, 1)
            sp.wait_ge(s["diag_used"], 3)
            sp.wait_ge(s["rqT_done"], 4)
            load_expert(sp, 2)
            sp.wait_ge(s["tmap_ready"], 1)
            for e in range(NE):
                if e >= RING:
                    last = sp.value_load(endi[0:1, e - RING:e - RING + 1], min_val=1, max_val=MT + 1)
                    sp.wait_ge(s["down_done"], last)
                    load_expert(sp, e)
                sp.wait_ge(s_w[e % RING], 48 * (e // RING + 1))
                sp.sem_inc(s["w_ready"], 1)
            for i in range(NT):
                sp.wait_ge(s["yo_ready"], i + 1)
                sp.dma_start(out.rearrange("b s d -> (b s) d")[i * P:(i + 1) * P, :], yo[:, i % 2]).then_inc(s_o[i % 2], 16)
            for k in range(2):
                sp.wait_ge(s_o[k], 16 * NT // 2)

        def attention_steps(eng, step, middle):
            for u in range(3):
                step(u, u % 2)
            with eng.Fori(0, H // 2) as i:
                step(i * 2 + 3, 1)
                step(i * 2 + 4, 0)
            middle()
            with eng.Fori(0, H // 2 - 2) as i:
                step(i * 2 + H + 3, 1)
                step(i * 2 + H + 4, 0)
            for u in range(QU - 1, QU + 3):
                step(u, u % 2)

        @block.tensor
        def _(pe):
            pe.wait_ge(s["con_in"], 16)
            for b in range(B):
                pe.wait_ge(s_f[b], 16)
                if b >= 2:
                    pe.wait_ge(s["fT_copied"], b - 1)
                for c in range(C):
                    for i in range(TT):
                        last = nc.tensor.transpose(pb[b % 2][:, c * S + i * P:c * S + (i + 1) * P],
                                                   f_tok[:, b, i, c * P:(c + 1) * P], ident)
                last.then_inc(s["fT_done"], 1)

            def ratio_transposes(n):
                pe.wait_ge(s["ratT_ready"], n + 1)
                if n >= 2:
                    pe.wait_ge(s["x0_ready"], n - 1)
                for i in range(TT):
                    for c in range(C):
                        last = nc.tensor.transpose(sc2[:, n % 2, i * D + c * P:i * D + (c + 1) * P],
                                                   rat[:, c * S + i * P:c * S + (i + 1) * P], ident)
                last.then_inc(s["rat_done"], 1)

            for b in range(B):
                ratio_transposes(b)
                pe.wait_ge(s["xn_ready"], b + 1)
                if b >= 2:
                    pe.wait_ge(s["hlo_done"], b - 1)
                for c in range(C):
                    for i in range(TT):
                        last = nc.tensor.transpose(pt2[:, b % 2, c * S + i * P:c * S + (i + 1) * P],
                                                   xn[:, i * D + c * P:i * D + (c + 1) * P], ident)
                last.then_inc(s["hTp_done"], 1)
            for n in range(B, 2 * B):
                ratio_transposes(n)

            def split_products(bank, w, m, first=True, final=True):
                order = ((0, 0), (0, 1), (1, 0))
                for k, (a, b) in enumerate(order):
                    last = nc.tensor.matmul(bank, w(a), m(b), start=first and k == 0, stop=final and k == 2)
                return last

            def proj(n, bank, col, pair):
                for c in range(C):
                    last = split_products(bank[:, :], lambda a: qkv16[:, a, c, bass.ds(col, HD)],
                                          lambda a: hT[:, a, c, bass.ds(pair * PAIR, PAIR)], c == 0, c == C - 1)
                last.then_inc(s["proj_done"], 1)

            pe.wait_ge(s["hlo_done"], B)
            pe.wait_ge(s["hi_done"], B)
            pe.wait_ge(s["qkvhi_done"], 1)
            pe.wait_ge(s["qkvlo_done"], 1)
            pe.wait_ge(s["fT_copied"], B)
            for n in range(KU):
                if n >= 2:
                    pe.wait_ge(s["rope_done"], n - 1)
                proj(n, pb[n % 2], H * HD + (n % KVH) * HD, n // KVH)
            for i in range(NT):
                bank = (po, pw)[i % 2]
                if i >= 2:
                    pe.wait_ge(s["vlo_done"], i - 1)
                for c in range(C):
                    last = split_products(bank[:, :], lambda a: hT[:, a, c, i * P:(i + 1) * P],
                                          lambda a: qkv16[:, a, c, (H + KVH) * HD:QKV], c == 0, c == C - 1)
                last.then_inc(s["v_done"], 1)

            def scores(u):
                pe.wait_ge(s["qlo_done"], KU + u + 1)
                if not isinstance(u, int) or u >= 1:
                    pe.wait_ge(s["max_done"], u)
                kv, pair = (u % H) // (H // KVH), u // H
                buf = par[0]
                for b in range(2):
                    for qb in range(2):
                        o, w = (0, P) if qb == 0 else (P, 2 * P)
                        last = split_products(sc2[:, b, o:o + w],
                                              lambda a: q16[:, buf, a, b * S + qb * P:b * S + (qb + 1) * P],
                                              lambda a: kT[:, a, bass.ds(kv, 1), bass.ds(pair * PAIR + b * S, w)]
                                              .rearrange("p a n -> p (a n)"))
                last.then_inc(s["score_done"], 1)

            def prob_transposes(u):
                pe.wait_ge(s["norm_done"], u + 1)
                if not isinstance(u, int) or u >= 1:
                    pe.wait_ge(s["pTlo_done"], u)
                for b in range(2):
                    for k in range(3):
                        last = nc.tensor.transpose(pt2[:, b, k * P:(k + 1) * P], pr[:, par[0], b, k * P:(k + 1) * P], ident)
                last.then_inc(s["pT_done"], 1)

            def weighted_values(u):
                pe.wait_ge(s["pTlo_done"], u + 1)
                if not isinstance(u, int) or u >= 1:
                    pe.wait_ge(s["olo_done"], u)
                kv, pair = (u % H) // (H // KVH), u // H
                buf = par[0]
                for b in range(2):
                    for kb in range(2):
                        o, w = (0, S) if kb == 0 else (2 * P, P)
                        last = split_products(po[:, b * S + kb * P:b * S + kb * P + w],
                                              lambda a: v16[:, a, bass.ds(pair * 4 + b * TT + kb, 1), bass.ds(kv * HD, HD)]
                                              .rearrange("p a n -> p (a n)"),
                                              lambda a: pT[:, buf, a, b, o:o + w], kb == 0, kb == 1)
                last.then_inc(s["av_done"], 1)

            def project_out(pair):
                pe.wait_ge(s["olo_done"], (pair + 1) * H)
                pe.wait_ge(s["wohi_done"], 1)
                pe.wait_ge(s["wolo_done"], 1)
                for i in range(4):
                    n = 4 * pair + i
                    if n >= 1:
                        pe.wait_ge(s["x1a_done"], n)
                    for h in range(H):
                        last = split_products(pw[:, 0:D], lambda a: oT[:, a, h, i * P:(i + 1) * P],
                                              lambda a: wo16[:, a, h, :], h == 0, h == H - 1)
                    last.then_inc(s["wo_done"], 1)

            par = [0]

            def step(u, parity):
                fixed = isinstance(u, int)
                if not fixed or u < QU:
                    pe.wait_ge(s["rope_done"], KU + u - 1)
                    proj(None, pb[parity], (u % H) * HD, u // H)
                if not fixed or 1 <= u < QU + 1:
                    par[0] = 1 - parity
                    scores(u - 1)
                if not fixed or 2 <= u < QU + 2:
                    par[0] = parity
                    prob_transposes(u - 2)
                if not fixed or u >= 3:
                    par[0] = 1 - parity
                    weighted_values(u - 3)

            pe.wait_ge(s["vlo_done"], NT)
            pe.wait_ge(s["x0_ready"], 2 * B)
            attention_steps(pe, step, lambda: project_out(0))
            project_out(1)

            for i in range(NT):
                pe.wait_ge(s["h2_ready"], i + 1)
                if i >= 2:
                    pe.wait_ge(s["h2T_copied"], i - 1)
                for c in range(C):
                    last = nc.tensor.transpose(pb[i % 2][:, c * P:(c + 1) * P], h2[:, i, c * P:(c + 1) * P], ident)
                last.then_inc(s["h2T_done"], 1)
                pe.wait_ge(s["h2T_copied"], i + 1)
                for c in range(C):
                    last = nc.tensor.matmul(po[:, i * NE:(i + 1) * NE], h2T[:, i % 2, c * P:(c + 1) * P], gate_w[:, c, :],
                                            start=c == 0, stop=c == C - 1)
                last.then_inc(s["gate_tile"], 1)
            pe.wait_ge(s["mk_ready"], 1)
            nc.tensor.matmul(po[:, 128:128 + NT * NE], before, MK, start=True, stop=True)
            nc.tensor.matmul(po[:, 256:256 + NT * NE], ones, MK, start=True, stop=True).then_inc(s["rank_done"], 1)

            for m in range(2):
                pe.wait_ge(s["rq_ready"], m + 1)
                pe.wait_ge(s["identb_ready"], 1)
                if m == 0:
                    pe.wait_ge(s["h2T_copied"], NT)
                else:
                    pe.wait_ge(s["rq_copied"], 1)
                    pe.wait_ge(s["srow_done"], 1)
                for kc in range(C):
                    for c in range(NI):
                        last = nc.tensor.transpose(pb[kc][:, :].bitcast(BF16)[:, c * IQ:(c + 1) * IQ],
                                                   rq[0:IQ, c * D + kc * P:c * D + (kc + 1) * P], identb[0:IQ, 0:IQ])
                last.then_inc(s["rqT_done"], 1)
                pe.wait_ge(s["diag_ready"], m + 1)
                for k in range(2):
                    last = nc.tensor.matmul(pt2[:, k, 0:IH], ones[0:IQ, :], gat[0:IQ, k * IH:(k + 1) * IH], start=True, stop=True)
                last.then_inc(s["diag_used"], 1)
            pe.wait_ge(s["rq_ready"], 3)
            pe.wait_ge(s["rq_copied"], 2)
            pe.wait_ge(s["srow_done"], 2)
            for hc in range(C):
                for c in range(NI):
                    last = nc.tensor.transpose(pb[hc][0:IQ, :].bitcast(BF16)[:, c * P:(c + 1) * P],
                                               rq[:, hc * INTER + c * IQ:hc * INTER + (c + 1) * IQ], identb[:, :])
                last.then_inc(s["rqT_done"], 1)
            pe.wait_ge(s["diag_ready"], 3)
            nc.tensor.matmul(pt2[:, 0, 0:D], ones, gat[:, 0:D], start=True, stop=True).then_inc(s["diag_used"], 1)
            pe.wait_ge(s["rq_copied"], 3)
            pe.wait_ge(s["srow_done"], 3)

            def x_transposes(n, parity):
                pe.wait_ge(s_xs[parity], 16 * (n // 2 + 1))
                if not isinstance(n, int) or n >= 1:
                    pe.wait_ge(s["xT_copied"], n)
                for c in range(C):
                    last = nc.tensor.transpose(po[:, c * P:(c + 1) * P], xs[:, parity, c * P:(c + 1) * P], ident)
                last.then_inc(s["xT_done"], 1)

            def up(n, parity, base, part):
                lo, w = (0, FA) if part == 0 else (FA, FB)
                for m in range(2):
                    bank = (pb[m] if part == 0 else sc2[:, m])[:, 0:w]
                    for c in range(C):
                        last = nc.tensor.matmul(bank, xsT[:, parity, c * P:(c + 1) * P],
                                                wreg[:, bass.ds(base + (m * C + c) * FF + lo, w)], start=c == 0, stop=c == C - 1)
                last.then_inc(s["upa_done" if part == 0 else "upb_done"], 1)

            def h_transposes(n):
                pe.wait_ge(s["silub_done"], n + 1)
                if not isinstance(n, int) or n >= 1:
                    pe.wait_ge(s["hT_copied"], n)
                for c in range(FC):
                    last = nc.tensor.transpose(pt2[:, c // 4, c % 4 * P:(c % 4 + 1) * P], hh[:, c * P:(c + 1) * P], ident)
                last.then_inc(s["hT_done"], 1)

            def down(n, base):
                pe.wait_ge(s["hT_copied"], n + 1)
                if not isinstance(n, int) or n >= 1:
                    pe.wait_ge(s["y_copied"], n)
                for c in range(FC):
                    last = nc.tensor.matmul(pw[:, 0:D], hhT[:, c, :], wreg[:, bass.ds(base + 2 * C * FF + c * D, D)],
                                            start=c == 0, stop=c == FC - 1)
                last.then_inc(s["down_done"], 1)

            pe.wait_ge(s["tmap_ready"], 1)
            pe.sem_inc(s["down_done"], 1)
            x_transposes(0, 0)

            def tile_base(n):
                e = pe.value_load(tmi[0:1, bass.ds(n, 1)], min_val=0, max_val=NE - 1)
                return e, (e % RING) * WEXP

            def tile_step(n, parity):
                fixed = isinstance(n, int)
                if not fixed or n < MT:
                    e, base = tile_base(n)
                    pe.wait_ge(s["w_ready"], e + 1)
                    pe.wait_ge(s["xT_copied"], n + 1)
                    if not fixed or n >= 1:
                        pe.wait_ge(s["silua_done"], n)
                    up(n, parity, base, 0)
                if not fixed or n >= 1:
                    h_transposes(n - 1)
                if not fixed or n < MT:
                    if not fixed or n + 1 < MT:
                        x_transposes(n + 1, 1 - parity)
                    up(n, parity, base, 1)
                if not fixed or n >= 1:
                    down(n - 1, tile_base(n - 1)[1])

            tile_step(0, 0)
            with pe.Fori(0, (MT - 3) // 2) as i:
                tile_step(i * 2 + 1, 1)
                tile_step(i * 2 + 2, 0)
            for n in range(MT - 2, MT + 1):
                tile_step(n, n % 2)

            def quantised_transposes(i):
                pe.wait_ge(s["qx_ready"], i + 1)
                if i >= 1:
                    pe.wait_ge(s["qxT_copied"], i)
                else:
                    pe.wait_ge(s["xT_copied"], MT)
                for c in range(C):
                    last = nc.tensor.transpose(po[:, :].bitcast(BF16)[:, c * P:(c + 1) * P], qx[:, c * P:(c + 1) * P], identb[:, :])
                last.then_inc(s["qxT_done"], 1)

            def gate_up(i):
                pe.wait_ge(s["qxT_copied"], i + 1)
                if i >= 1:
                    pe.wait_ge(s["g1_ready"], i)
                else:
                    pe.wait_ge(s["silub_done"], MT)
                for m in range(2):
                    for k in range(2):
                        bank = (pb[k] if m == 0 else sc2[:, k])[:, 0:IH]
                        for c in range(C):
                            last = nc.tensor.matmul(bank, qxT[:, c, :], q1w[:, m, c, k * IH:(k + 1) * IH],
                                                    start=c == 0, stop=c == C - 1)
                last.then_inc(s["gu_done"], 1)

            def inner_transposes(i):
                pe.wait_ge(s["qt_ready"], i + 1)
                if i >= 1:
                    pe.wait_ge(s["qtT_copied"], i)
                else:
                    pe.wait_ge(s["hT_copied"], MT)
                for c in range(NI):
                    last = nc.tensor.transpose(pt2[0:IQ, 0, :].bitcast(BF16)[:, c * P:(c + 1) * P], qt[:, c * IQ:(c + 1) * IQ], identb[:, :])
                last.then_inc(s["qtT_done"], 1)

            def down_quantised(i):
                pe.wait_ge(s["qtT_copied"], i + 1)
                if i >= 1:
                    pe.wait_ge(s["yo_read"], i)
                else:
                    pe.wait_ge(s["y_copied"], MT)
                for c in range(NI):
                    last = nc.tensor.matmul(pw[:, 0:D], qtT[0:IQ, c, :], q1d[0:IQ, c, :], start=c == 0, stop=c == NI - 1)
                last.then_inc(s["dn_done"], 1)

            for i in range(NT + 1):
                if i < NT:
                    quantised_transposes(i)
                    gate_up(i)
                if i >= 1:
                    inner_transposes(i - 1)
                    down_quantised(i - 1)

        @block.scalar
        def _(act):
            links = [0]

            def link(ins):
                links[0] += 1
                ins.then_inc(s["act_link"], 1)
                act.wait_ge(s["act_link"], links[0])

            act.wait_ge(s["tfsum"], 1)
            nc.scalar.activation(tf[:, 1, :], tf[:, 0, :], ACT.Exp, scale=-1.0).then_inc(s["tf_exp"], 1)
            link(nc.scalar.activation(dec[:, 0, :, :], wu[:, 0:4:2, :], ACT.Exp))
            nc.scalar.activation(dec[:, 1, :, :], dec[:, 0, :, :], ACT.Exp, scale=-1.0).then_inc(s["dec_exp"], 1)
            for b in range(B):
                act.wait_ge(s["fT_done"], b + 1)
                nc.scalar.copy(fT[:, b, :], pb[b % 2][:, :]).then_inc(s["fT_copied"], 1)
                act.wait_ge(s["kmin_ready"], b + 1)
                nc.scalar.activation(E[:, b, 1, :], kmin, ACT.Exp).then_inc(s["ek_ready"], 1)
                act.wait_ge(s_x[b], 16)
                nc.scalar.activation(sg[:, b, :], x_in[:, b, :], ACT.Exp, scale=-1.0).then_inc(s["sg_exp"], 1)
            act.wait_ge(s["qkv_in"], 48)
            for c in range(C):
                for q in range(2):
                    nc.scalar.activation(qkv16[:, 0, c, 0:20 * HD].rearrange("p (h q i) -> p h q i", q=2, i=HD // 2)[:, :, q, :],
                                         stage[:, c, q:20 * HD:2].rearrange("p (h i) -> p h i", i=HD // 2), ACT.Copy, scale=WS)
            nc.scalar.activation(qkv16[:, 0, :, 20 * HD:], stage[:, :, 20 * HD:], ACT.Copy, scale=WS).then_inc(s["qkvhi_done"], 1)

            def batch_hidden(b):
                act.wait_ge(s["x0_ready"], b + 1)
                for i in range(TT):
                    last = nc.scalar.activation(t1[:, i * D:(i + 1) * D], x0[:, b * TT + i, :], ACT.Square,
                                                accum_out=ssq[:, 0, b * TT + i:b * TT + i + 1])
                last.then_inc(s["ssq_ready"], 1)
                act.wait_ge(s["hTp_done"], b + 1)
                for c in range(C):
                    last = nc.scalar.activation(hT[:, 0, c, b * S:(b + 1) * S], pt2[:, b % 2, c * S:(c + 1) * S],
                                                ACT.Copy, scale=wln[:, c:c + 1])
                last.then_inc(s["hi_done"], 1)

            for n in range(2 * B):
                act.wait_ge(s["ku_ready"], n + 1)
                nc.scalar.activation(U[:, 1, :], U[:, 1, :], ACT.Exp).then_inc(s["uexp_ready"], 1)
                if n == 0:
                    act.wait_ge(s["par_in"], 16 * 8)
                if n < B:
                    batch_hidden(n)
            act.wait_ge(s["wo_in"], 16)
            nc.scalar.activation(wo16[:, 0], stage_wo, ACT.Copy, scale=WS).then_inc(s["wohi_done"], 1)

            def high_part(u, parity):
                act.wait_ge(s["radd_done"], KU + u + 1)
                if not isinstance(u, int) or u >= 2:
                    act.wait_ge(s["score_done"], u - 1)
                nc.scalar.copy(q16[:, parity, 0, :], qr[:, parity, :]).then_inc(s["qhi_done"], 1)

            def exponentials(u, parity):
                act.wait_ge(s["nmax_done"], u + 1)
                for b in range(2):
                    for qb in range(2):
                        o, w = (0, P) if qb == 0 else (P, 2 * P)
                        k = 2 * b + qb
                        last = nc.scalar.activation(pr[:, parity, b, o:o + w], pr[:, parity, b, o:o + w], ACT.Exp,
                                                    bias=mx[:, parity, 1, k:k + 1], scale=SCALE,
                                                    accum_out=sums[:, parity, 0, k:k + 1])
                last.then_inc(s["exp_done"], 1)

            def pT_high(u, parity):
                act.wait_ge(s["pT_done"], u + 1)
                if not isinstance(u, int) or u >= 2:
                    act.wait_ge(s["av_done"], u - 1)
                nc.scalar.copy(pT[:, parity, 0], pt2[:, :, 0:BLK]).then_inc(s["pThi_done"], 1)

            def o_high(u):
                act.wait_ge(s["av_done"], u + 1)
                nc.scalar.copy(oT[:, 0, bass.ds(u % H, 1), :].rearrange("p a n -> p (a n)"), po[:, :]).then_inc(s["ohi_done"], 1)

            for n in range(KU):
                act.wait_ge(s["radd_done"], n + 1)
                nc.scalar.copy(kT[:, 0, n % KVH, n // KVH * PAIR:(n // KVH + 1) * PAIR], qr[:, n % 2, :]).then_inc(s["qhi_done"], 1)
            for i in range(NT):
                act.wait_ge(s["v_done"], i + 1)
                nc.scalar.copy(v16[:, 0, i, :], (po, pw)[i % 2][:, :]).then_inc(s["vhi_done"], 1)

            def step(u, parity):
                fixed = isinstance(u, int)
                if not fixed or u < QU:
                    high_part(u, parity)
                if not fixed or 1 <= u < QU + 1:
                    exponentials(u - 1, 1 - parity)
                if not fixed or 2 <= u < QU + 2:
                    pT_high(u - 2, parity)
                if not fixed or u >= 3:
                    o_high(u - 3)

            attention_steps(act, step, lambda: act.wait_ge(s["wo_done"], NT // 2))

            act.wait_ge(s["x1a_done"], NT)
            for i in range(NT):
                nc.scalar.activation(h2[:, i, :], x0[:, i, :], ACT.Square, accum_out=ssq[:, 0, i:i + 1]).then_inc(s["ssq2_ready"], 1)
            for i in range(NT):
                act.wait_ge(s["h2T_done"], i + 1)
                if i >= 2:
                    act.wait_ge(s["gate_tile"], i - 1)
                nc.scalar.copy(h2T[:, i % 2, :], pb[i % 2][:, 0:D]).then_inc(s["h2T_copied"], 1)
            act.wait_ge(s["d_ready"], 1)
            nc.scalar.activation(gts[:, :, 1], gts[:, :, 0], ACT.Exp).then_inc(s["ge_ready"], 1)

            for m in range(2):
                act.wait_ge(s["rqT_done"], m + 1)
                for kc in range(C):
                    last = nc.scalar.copy(q1w[:, m, kc, :], pb[kc][:, :].bitcast(BF16)[:, 0:INTER])
                last.then_inc(s["rq_copied"], 1)
                act.wait_ge(s["diag_used"], m + 1)
                nc.scalar.copy(srow[:, m * INTER:(m + 1) * INTER].rearrange("p (k n) -> p k n", k=2), pt2[:, :, 0:IH])\
                    .then_inc(s["srow_done"], 1)
            act.wait_ge(s["rqT_done"], 4)
            for hc in range(C):
                last = nc.scalar.copy(q1d[0:IQ, :, hc * P:(hc + 1) * P],
                                      pb[hc][0:IQ, :].bitcast(BF16).rearrange("p (c n) -> p c n", c=NI))
            last.then_inc(s["rq_copied"], 1)
            act.wait_ge(s["diag_used"], 3)
            nc.scalar.copy(srow[:, 2 * INTER:], pt2[:, 0, 0:D]).then_inc(s["srow_done"], 1)

            def load_rows(n, parity):
                act.dma_start(xs[:, parity, :], xs_dram[bass.ds(n * P, P), :]).then_inc(s_xs[parity], 16)

            def copy_xT(n, parity):
                act.wait_ge(s["xT_done"], n + 1)
                if not isinstance(n, int) or n >= 2:
                    act.wait_ge(s["upb_done"], n - 1)
                nc.scalar.copy(xsT[:, parity, :], po[:, 0:D]).then_inc(s["xT_copied"], 1)

            act.wait_ge(s["scatter_out"], 16 * 2 * NT)
            load_rows(0, 0)
            load_rows(1, 1)
            copy_xT(0, 0)

            def tile_step(n, parity):
                fixed = isinstance(n, int)
                if not fixed or n < MT:
                    act.wait_ge(s["upa_done"], n + 1)
                    if not fixed or n >= 1:
                        act.wait_ge(s["silub_done"], n)
                    nc.scalar.activation(eh[:, 0:FA], pb[0][:, :], ACT.Exp, scale=-1.0).then_inc(s["expa_done"], 1)
                if not fixed or n >= 1:
                    act.wait_ge(s["hT_done"], n)
                    if not fixed or n >= 2:
                        act.wait_ge(s["down_done"], n)
                    nc.scalar.copy(hhT[:, 0:4, :], pt2[:, 0, :].rearrange("p (c n) -> p c n", c=4))
                    nc.scalar.copy(hhT[:, 4:FC, :], pt2[:, 1, 0:FB].rearrange("p (c n) -> p c n", c=FC - 4)).then_inc(s["hT_copied"], 1)
                if not fixed or n + 1 < MT:
                    copy_xT(n + 1, 1 - parity)
                if not fixed or n + 2 < MT:
                    load_rows(n + 2, parity)
                if not fixed or n < MT:
                    act.wait_ge(s["upb_done"], n + 1)
                    nc.scalar.activation(eh[:, FA:FF], sc2[:, 0, 0:FB], ACT.Exp, scale=-1.0).then_inc(s["expb_done"], 1)
                if not fixed or n >= 1:
                    act.wait_ge(s["down_done"], n + 1)
                    if not fixed or n >= 3:
                        act.wait_ge(s_y[1 - parity], 16 * ((n - 1) // 2))
                    nc.scalar.copy(ysb[:, 1 - parity, :], pw[:, 0:D]).then_inc(s["y_copied"], 1)
                    act.wait_ge(s["y_copied"], n)
                    act.dma_start(ys_dram[bass.ds((n - 1) * P, P), :], ysb[:, 1 - parity, :]).then_inc(s_y[1 - parity], 16)

            for n in range(3):
                tile_step(n, n % 2)
            with act.Fori(0, (MT - 5) // 2) as i:
                tile_step(i * 2 + 3, 1)
                tile_step(i * 2 + 4, 0)
            for n in range(MT - 2, MT + 1):
                tile_step(n, n % 2)

            for i in range(NT + 1):
                if i < NT:
                    act.wait_ge(s["x1_ready"], i + 1)
                    nc.scalar.activation(xq[:, 0, :], x1[:, i, :], ACT.Exp, scale=-1.0).then_inc(s["sgx_ready"], 1)
                    act.wait_ge(s["qxT_done"], i + 1)
                    if i >= 1:
                        act.wait_ge(s["gu_done"], i)
                    nc.scalar.copy(qxT[:, :, :], po[:, 0:P].bitcast(BF16).rearrange("p (c n) -> p c n", c=C)).then_inc(s["qxT_copied"], 1)
                if i >= 1:
                    act.wait_ge(s["g1_ready"], i)
                    nc.scalar.activation(gw[:, 2, :], gw[:, 0, :], ACT.Exp, scale=rs[:, 4, i - 1:i]).then_inc(s["ge1_ready"], 1)
                    act.wait_ge(s["qtT_done"], i)
                    if i >= 2:
                        act.wait_ge(s["dn_done"], i - 1)
                    nc.scalar.copy(qtT[0:IQ, :, :], pt2[0:IQ, 0, :].bitcast(BF16).rearrange("p (c n) -> p c n", c=NI)).then_inc(s["qtT_copied"], 1)

        @block.vector
        def _(dve):
            links = [0]
            V = nc.vector

            def link(ins):
                links[0] += 1
                ins.then_inc(s["dve_link"], 1)
                dve.wait_ge(s["dve_link"], links[0])

            dve.wait_ge(s["par_in"], 16 * 8)
            V.tensor_reduce(out=tf[:, 0, :], in_=cond[:, :, :], axis=AX.X, op=ALU.add).then_inc(s["tfsum"], 1)
            dve.wait_ge(s["tf_exp"], 1)
            link(V.tensor_scalar(tf[:, 2, :], tf[:, 1, :], 1.0, None, ALU.add))
            link(V.reciprocal(tf[:, 3, :], tf[:, 2, :]))
            V.tensor_scalar(tf[:, 4, :], tf[:, 3, :], 0.5, 0.5, ALU.mult, ALU.add)
            link(V.tensor_scalar(tf[:, 5, :], tf[:, 3, :], 0.2, 0.8, ALU.mult, ALU.add))
            dve.wait_ge(s["dec_exp"], 1)
            for l in range(2):
                for c in range(C):
                    last = V.tensor_scalar(decay[:, l, c, :], tf[:, 4, :], dec[:, 1, l, c:c + 1], None, ALU.mult)
            link(last)

            for b in range(B):
                dve.wait_ge(s["fT_copied"], b + 1)
                V.tensor_scalar(kmin, fT[:, b, :], 30.0, None, ALU.min).then_inc(s["kmin_ready"], 1)
                dve.wait_ge(s["ek_ready"], b + 1)
                link(V.tensor_tensor(E[:, b, 0, :], E[:, b, 1, :], fT[:, b, :], ALU.mult))

            def mixing_ratio(l, b):
                n = l * B + b
                for c in range(C):
                    a = decay[:, l, c, b:b + 1].to_broadcast([P, S])
                    for k in range(2):
                        src = E[:, b, k, c * S:(c + 1) * S]
                        V.tensor_tensor_scan(out=fwd[:, k, c * S:(c + 1) * S], data0=a, data1=src, initial=0.0,
                                             op0=ALU.mult, op1=ALU.add)
                        last = V.tensor_tensor_scan(out=bwd[:, k, c * S:(c + 1) * S][:, ::-1], data0=a, data1=src[:, ::-1],
                                                    initial=0.0, op0=ALU.mult, op1=ALU.add)
                link(last)
                link(V.tensor_tensor(fwd[:, :, :], fwd[:, :, :], bwd[:, :, :], ALU.add))
                link(V.tensor_tensor(fwd[:, :, :], fwd[:, :, :], E[:, b, :, :], ALU.subtract))
                dve.wait_ge(s["u_ready"], n + 1)
                last = V.tensor_tensor(fwd[:, :, :], fwd[:, :, :], U[:, :, :], ALU.add)
                last.then_inc(s["u_used"], 1)
                dve.wait_ge(s["u_used"], n + 1)
                link(V.tensor_scalar(fwd[:, 1, :], fwd[:, 1, :], 1e-8, None, ALU.max))
                link(V.reciprocal(bwd[:, 1, :], fwd[:, 1, :]))
                if n >= 1:
                    dve.wait_ge(s["rat_done"], n)
                V.scalar_tensor_tensor(rat, fwd[:, 0, :], tf[:, 5, b:b + 1], bwd[:, 1, :], ALU.mult, ALU.mult)\
                    .then_inc(s["ratT_ready"], 1)

            for b in range(B):
                mixing_ratio(0, b)
                dve.wait_ge(s["sg_exp"], b + 1)
                link(V.tensor_scalar(sg[:, b, :], sg[:, b, :], 1.0, None, ALU.add))
                link(V.reciprocal(sg[:, b, :], sg[:, b, :]))
                dve.wait_ge(s["rat_done"], b + 1)
                V.tensor_tensor(x0[:, TT * b:TT * (b + 1), :].rearrange("p i n -> p (i n)"), sc2[:, b % 2, :], sg[:, b, :], ALU.mult)\
                    .then_inc(s["x0_ready"], 1)
                dve.wait_ge(s["x0_ready"], b + 1)
                dve.wait_ge(s["rstd_ready"], b + 1)
                if b >= 1:
                    dve.wait_ge(s["hTp_done"], b)
                for i in range(TT):
                    k = b * TT + i
                    last = V.tensor_scalar(xn[:, i * D:(i + 1) * D], x0[:, k, :], ssq[:, 2, k:k + 1], None, ALU.mult)
                last.then_inc(s["xn_ready"], 1)
                dve.wait_ge(s["hi_done"], b + 1)
                for c in range(C):
                    last = V.scalar_tensor_tensor(hT[:, 1, c, b * S:(b + 1) * S], pt2[:, b % 2, c * S:(c + 1) * S], wln[:, c:c + 1],
                                                  hT[:, 0, c, b * S:(b + 1) * S], ALU.mult, ALU.subtract)
                last.then_inc(s["hlo_done"], 1)
            dve.wait_ge(s["qkvhi_done"], 1)
            for c in range(C):
                for q in range(2):
                    def lanes(a):
                        return qkv16[:, a, c, 0:20 * HD].rearrange("p (h q i) -> p h q i", q=2, i=HD // 2)[:, :, q, :]
                    V.scalar_tensor_tensor(lanes(1), stage[:, c, q:20 * HD:2].rearrange("p (h i) -> p h i", i=HD // 2), WS,
                                           lanes(0), ALU.mult, ALU.subtract)
            V.scalar_tensor_tensor(qkv16[:, 1, :, 20 * HD:], stage[:, :, 20 * HD:], WS, qkv16[:, 0, :, 20 * HD:],
                                   ALU.mult, ALU.subtract).then_inc(s["qkvlo_done"], 1)
            for b in range(B):
                mixing_ratio(1, b)
                dve.wait_ge(s["rat_done"], B + b + 1)
                V.tensor_copy(ratio1[:, TT * b:TT * (b + 1), :].rearrange("p i n -> p (i n)"), sc2[:, b % 2, :]).then_inc(s["x0_ready"], 1)
            dve.wait_ge(s["wohi_done"], 1)
            V.scalar_tensor_tensor(wo16[:, 1], stage_wo, WS, wo16[:, 0], ALU.mult, ALU.subtract).then_inc(s["wolo_done"], 1)

            dve.wait_ge(s["zero_out"], 16)
            HH = HD // 2

            def rope(n, parity):
                dve.wait_ge(s["proj_done"], n + 1)
                if not isinstance(n, int) or n >= 1:
                    dve.wait_ge(s["radd_done"], n)
                bank = pb[parity][:, :].rearrange("p (b n) -> p b n", b=2)
                t1v, t2v = (x[:, :].rearrange("p (b n) -> p b n", b=2) for x in (t1, t2))
                cosv = rope_cos.rearrange("p (a n) -> p a n", a=1)
                sinv = rope_sin.rearrange("p (a n) -> p a n", a=1)
                V.tensor_tensor(t1v, bank, cosv.to_broadcast([P, 2, S]), ALU.mult)
                V.tensor_tensor(t2v[0:HH], bank[HH:HD], sinv[0:HH].to_broadcast([HH, 2, S]), ALU.mult)
                V.tensor_tensor(t2v[HH:HD], bank[0:HH], sinv[HH:HD].to_broadcast([HH, 2, S]), ALU.mult).then_inc(s["rope_done"], 1)

            for n in range(KU):
                rope(n, n % 2)
            for i in range(NT):
                dve.wait_ge(s["vhi_done"], i + 1)
                V.tensor_tensor(v16[:, 1, i, :], (po, pw)[i % 2][:, :], v16[:, 0, i, :], ALU.subtract).then_inc(s["vlo_done"], 1)

            def recip(u, parity):
                dve.wait_ge(s["exp_done"], u + 1)
                V.reciprocal(sums[:, parity, 1, :], sums[:, parity, 0, :]).then_inc(s["recip_done"], 1)

            def row_max(u, parity):
                dve.wait_ge(s["score_done"], u + 1)
                if not isinstance(u, int) or u >= 2:
                    dve.wait_ge(s["pT_done"], u - 1)
                dve.sem_inc(s["dve_paused"], 1)
                for b in range(2):
                    for qb in range(2):
                        o, w = (0, P) if qb == 0 else (P, 2 * P)
                        k = 2 * b + qb
                        last = V.tensor_tensor_reduce(out=pr[:, parity, b, o:o + w], in0=sc2[:, b, o:o + w], in1=mask[:, o:o + w],
                                                      scale=1.0, scalar=-3e38, op0=ALU.add, op1=ALU.max,
                                                      accum_out=mx[:, parity, 0, k:k + 1])
                last.then_inc(s["max_done"], 1)
                dve.wait_ge(s["max_done"], u + 1)
                V.tensor_scalar(mx[:, parity, 1, :], mx[:, parity, 0, :], -SCALE, None, ALU.mult).then_inc(s["nmax_done"], 1)

            def pT_low(u, parity):
                dve.wait_ge(s["pThi_done"], u + 1)
                V.tensor_tensor(pT[:, parity, 1], pt2[:, :, 0:BLK], pT[:, parity, 0], ALU.subtract).then_inc(s["pTlo_done"], 1)

            def o_low(u):
                dve.wait_ge(s["ohi_done"], u + 1)
                V.tensor_tensor(oT[:, 1, bass.ds(u % H, 1), :].rearrange("p a n -> p (a n)"), po[:, :],
                                oT[:, 0, bass.ds(u % H, 1), :].rearrange("p a n -> p (a n)"), ALU.subtract).then_inc(s["olo_done"], 1)

            def step(u, parity):
                fixed = isinstance(u, int)
                if not fixed or 2 <= u < QU + 2:
                    recip(u - 2, parity)
                if not fixed or u < QU:
                    rope(KU + u, parity)
                if not fixed or 1 <= u < QU + 1:
                    row_max(u - 1, 1 - parity)
                if not fixed or 2 <= u < QU + 2:
                    pT_low(u - 2, parity)
                if not fixed or u >= 3:
                    o_low(u - 3)

            def residual(pair):
                for n in range(4 * pair, 4 * pair + 4):
                    dve.wait_ge(s["wo_done"], n + 1)
                    V.scalar_tensor_tensor(x0[:, n, :], pw[:, 0:D], 1.0 / (WS * WS), x0[:, n, :],
                                           ALU.mult, ALU.add).then_inc(s["x1a_done"], 1)

            attention_steps(dve, step, lambda: residual(0))
            residual(1)

            for i in range(NT):
                dve.wait_ge(s["rstd2_ready"], i + 1)
                V.scalar_tensor_tensor(h2[:, i, :], x0[:, i, :], ssq[:, 2, i:i + 1], ffln[:, :], ALU.mult, ALU.mult)\
                    .then_inc(s["h2_ready"], 1)
            dve.wait_ge(s["gate_tile"], NT)
            link(V.tensor_copy(lg, po[:, 0:NT * NE]))
            for i in range(NT):
                last = V.max(m8[:, i * NE:(i + 1) * NE], lg[:, i * NE:(i + 1) * NE])
            link(last)
            for i in range(NT):
                last = V.max_index(i8[:, i * NE:(i + 1) * NE], m8[:, i * NE:(i + 1) * NE], lg[:, i * NE:(i + 1) * NE])
            link(last)

            def te(x):
                return x.rearrange("p (i e) -> p i e", e=NE)

            m8v = te(m8)
            idfv = idf.rearrange("p (i k) -> p i k", k=2)
            iota = iota_e.rearrange("p (a e) -> p a e", a=1).to_broadcast([P, NT, NE])
            link(V.tensor_copy(idfv, i8.rearrange("p (i e) -> p i e", e=NE)[:, :, 0:2]))
            V.tensor_tensor(te(M1), iota, idfv[:, :, 0:1].to_broadcast([P, NT, NE]), ALU.is_equal)
            V.tensor_tensor(te(M2), iota, idfv[:, :, 1:2].to_broadcast([P, NT, NE]), ALU.is_equal)
            link(V.tensor_tensor(gts[:, :, 0], m8v[:, :, 1], m8v[:, :, 0], ALU.subtract))
            V.tensor_tensor(MK, M1, M2, ALU.add).then_inc(s["mk_ready"], 1)
            V.memset(car[:, 0:NE], 0.0).then_inc(s["d_ready"], 1)
            dve.wait_ge(s["ge_ready"], 1)
            link(V.tensor_scalar(gts[:, :, 2], gts[:, :, 1], 1.0, None, ALU.add))
            link(V.reciprocal(gts[:, :, 3], gts[:, :, 2]))
            link(V.tensor_tensor(gts[:, :, 4], gts[:, :, 3], gts[:, :, 1], ALU.mult))
            dve.wait_ge(s["rank_done"], 1)
            link(V.tensor_copy(tots, po[:, 256:256 + NT * NE]))
            for i in range(NT):
                link(V.tensor_tensor(car[:, (i + 1) * NE:(i + 2) * NE], car[:, i * NE:(i + 1) * NE], tots[:, i * NE:(i + 1) * NE], ALU.add))
            link(V.tensor_scalar(exi[:, 0, :], car[:, NT * NE:], float(P - 1), None, ALU.add))
            link(V.tensor_scalar(exi[:, 1, :], exi[:, 0, :], 7, None, ALU.logical_shift_right))
            link(V.tensor_copy(ex8[:, 1, :], exi[:, 1, :]))
            link(V.tensor_tensor_scan(out=ex8[:, 2, :], data0=ones[:, 0:NE], data1=ex8[:, 1, :], initial=0.0, op0=ALU.mult, op1=ALU.add))
            link(V.tensor_tensor(ex8[:, 3, :], ex8[:, 2, :], ex8[:, 1, :], ALU.subtract))
            link(V.tensor_scalar(ex8[:, 4, :], ex8[:, 3, :], float(P), None, ALU.mult))
            link(V.tensor_tensor(pos, po[:, 128:128 + NT * NE], car[:, 0:NT * NE], ALU.add))
            link(V.tensor_tensor(te(pos), te(pos), ex8[:, 4:5, :].to_broadcast([P, NT, NE]), ALU.add))
            for k, M in enumerate((M1, M2)):
                link(V.tensor_tensor(prod, pos, M, ALU.mult))
                link(V.tensor_reduce(out=slotf[:, k, :], in_=te(prod), axis=AX.X, op=ALU.add))
            V.tensor_copy(sloti[:, :, :], slotf[:, :, :]).then_inc(s["slots_ready"], 1)
            cmpv = cmp[:, :].rearrange("p (t e) -> p t e", e=NE)
            link(V.tensor_tensor(cmpv, ex8[:, 2:3, :].to_broadcast([P, MT, NE]),
                                 iota_t.rearrange("p (t a) -> p t a", a=1).to_broadcast([P, MT, NE]), ALU.is_le))
            link(V.tensor_reduce(out=tmap[:, 0, :], in_=cmpv, axis=AX.X, op=ALU.add))
            link(V.tensor_scalar(tmi[0:1, :], tmap[0:1, 0, :], float(NE - 1), None, ALU.min))
            V.tensor_scalar(endi[0:1, :], ex8[0:1, 2, :], 1.0, None, ALU.add).then_inc(s["tmap_ready"], 1)

            V.tensor_copy(identb[:, :], ident).then_inc(s["identb_ready"], 1)

            def round_e4m3(dst, v, g):
                link(V.tensor_scalar(g.bitcast(I32), v.bitcast(I32), 0x7F800000, None, ALU.bitwise_and))
                link(V.tensor_scalar(g, g, FP8_LEAST, MAGIC, ALU.max, ALU.mult))
                link(V.tensor_tensor(v, v, g, ALU.add))
                return V.tensor_tensor(dst, v, g, ALU.subtract)

            for m in range(3):
                q, k, n = (IQ, NI, D) if m < 2 else (P, C, INTER)
                dve.wait_ge(s["rows_in"], (16 * NI, 32 * NI, 32 * NI + 16)[m])
                r = rows[0:q, 0:k * n]
                r3 = r.rearrange("p (k n) -> p k n", k=k)
                link(V.tensor_reduce(out=wmax[0:q, m, 0:k], in_=r3, axis=AX.X, op=ALU.max, apply_absolute_value=True))
                link(V.reciprocal(winv[0:q, m, 0:k], wmax[0:q, m, 0:k]))
                V.tensor_scalar(wscale[0:q, m, 0:k], wmax[0:q, m, 0:k], 1.0 / FP8_MAX, None, ALU.mult)
                link(V.tensor_scalar(winv[0:q, m, 0:k], winv[0:q, m, 0:k], FP8_MAX, None, ALU.mult))
                link(V.tensor_tensor(r3, r3, winv[0:q, m, 0:k].rearrange("p (k a) -> p k a", a=1).to_broadcast([q, k, n]), ALU.mult))
                if m >= 1:
                    dve.wait_ge(s["rqT_done"], m)
                    dve.wait_ge(s["diag_used"], m)
                round_e4m3(rq[0:q, 0:k * n], r, grid[0:q, 0:k * n]).then_inc(s["rq_ready"], 1)
                g = gat[0:q, 0:k * q].rearrange("p (k n) -> p k n", k=k)
                V.tensor_tensor(g, ident[0:q, 0:q].rearrange("p (a n) -> p a n", a=1).to_broadcast([q, k, q]),
                                wscale[0:q, m, 0:k].rearrange("p (k a) -> p k a", a=1).to_broadcast([q, k, q]), ALU.mult)\
                    .then_inc(s["diag_ready"], 1)

            def silu(n, part):
                lo, hi = (0, FA) if part == 0 else (FA, FF)
                a, b = (pb[0][:, 0:FA], pb[1][:, 0:FA]) if part == 0 else (sc2[:, 0, 0:FB], sc2[:, 1, 0:FB])
                done = s["silua_done" if part == 0 else "silub_done"]
                dve.wait_ge(s["expa_done" if part == 0 else "expb_done"], n + 1)
                k = n * 6 + 3 * part
                V.tensor_scalar(eh[:, lo:hi], eh[:, lo:hi], 1.0, None, ALU.add).then_inc(s["moe_link"], 1)
                dve.wait_ge(s["moe_link"], k + 1)
                V.reciprocal(eh[:, lo:hi], eh[:, lo:hi]).then_inc(s["moe_link"], 1)
                dve.wait_ge(s["moe_link"], k + 2)
                V.tensor_tensor(eh[:, lo:hi], eh[:, lo:hi], a, ALU.mult).then_inc(s["moe_link"], 1)
                dve.wait_ge(s["moe_link"], k + 3)
                if part == 0 and (not isinstance(n, int) or n >= 1):
                    dve.wait_ge(s["hT_done"], n)
                V.tensor_tensor(hh[:, lo:hi], eh[:, lo:hi], b, ALU.mult).then_inc(done, 1)

            for part in range(2):
                silu(0, part)
            with dve.Fori(1, MT) as n:
                for part in range(2):
                    silu(n, part)

            def mixed_rows(i):
                k = i % 2
                if i == 0:
                    dve.wait_ge(s["hT_done"], MT)
                dve.wait_ge(s_g[k], 32 * (i // 2 + 1))
                r = xq
                link(V.scalar_tensor_tensor(x1[:, i, :], y1[:, k, :], gts[:, i, 3:4], x0[:, i, :], ALU.mult, ALU.add))
                link(V.scalar_tensor_tensor(x1[:, i, :], y2[:, k, :], gts[:, i, 4:5], x1[:, i, :], ALU.mult, ALU.add))
                V.tensor_tensor(x1[:, i, :], x1[:, i, :], x_in[:, i // TT, (i % TT) * D:(i % TT + 1) * D], ALU.add).then_inc(s["x1_ready"], 1)
                dve.wait_ge(s["sgx_ready"], i + 1)
                link(V.tensor_scalar(r[:, 0, :], r[:, 0, :], 1.0, None, ALU.add))
                link(V.reciprocal(r[:, 1, :], r[:, 0, :]))
                link(V.tensor_tensor(r[:, 2, :], r[:, 1, :], ratio1[:, i, :], ALU.mult))
                link(V.tensor_reduce(out=rs[:, 0, i:i + 1], in_=r[:, 2, :], axis=AX.X, op=ALU.max, apply_absolute_value=True))
                link(V.reciprocal(rs[:, 1, i:i + 1], rs[:, 0, i:i + 1]))
                V.tensor_scalar(rs[:, 3, i:i + 1], rs[:, 0, i:i + 1], 1.0 / FP8_MAX, None, ALU.mult)
                V.tensor_scalar(rs[:, 4, i:i + 1], rs[:, 0, i:i + 1], -1.0 / FP8_MAX, None, ALU.mult)
                link(V.tensor_scalar(rs[:, 2, i:i + 1], rs[:, 1, i:i + 1], FP8_MAX, None, ALU.mult))
                link(V.tensor_tensor(rs[:, 5, i:i + 1], rs[:, 3, i:i + 1], rs[:, 3, i:i + 1], ALU.mult))
                link(V.tensor_scalar(r[:, 3, :], r[:, 2, :], rs[:, 2, i:i + 1], None, ALU.mult))
                if i >= 1:
                    dve.wait_ge(s["qxT_done"], i)
                round_e4m3(qx[:, :], r[:, 3, :], r[:, 4, :]).then_inc(s["qx_ready"], 1)

            def inner_rows(i):
                dve.wait_ge(s["gu_done"], i + 1)
                def halves(x):
                    return x.rearrange("p (k n) -> p k n", k=2)
                for k in range(2):
                    V.tensor_tensor(gw[:, 0, k * IH:(k + 1) * IH], pb[k][:, 0:IH], srow[:, k * IH:(k + 1) * IH], ALU.mult)
                V.tensor_tensor(halves(gw[:, 1, :]), sc2[:, :, 0:IH], halves(srow[:, INTER:2 * INTER]), ALU.mult).then_inc(s["g1_ready"], 1)
                dve.wait_ge(s["ge1_ready"], i + 1)
                link(V.tensor_scalar(gw[:, 2, :], gw[:, 2, :], 1.0, None, ALU.add))
                link(V.reciprocal(gw[:, 2, :], gw[:, 2, :]))
                link(V.tensor_tensor(gw[:, 3, :], gw[:, 0, :], gw[:, 2, :], ALU.mult))
                link(V.scalar_tensor_tensor(gw[:, 3, :], gw[:, 3, :], rs[:, 5, i:i + 1], gw[:, 1, :], ALU.mult, ALU.mult))
                link(V.tensor_reduce(out=rs[:, 6, i:i + 1], in_=gw[:, 3, :], axis=AX.X, op=ALU.max, apply_absolute_value=True))
                link(V.reciprocal(rs[:, 7, i:i + 1], rs[:, 6, i:i + 1]))
                V.tensor_scalar(rs[:, 9, i:i + 1], rs[:, 6, i:i + 1], 1.0 / FP8_MAX, None, ALU.mult)
                link(V.tensor_scalar(rs[:, 8, i:i + 1], rs[:, 7, i:i + 1], FP8_MAX, None, ALU.mult))
                link(V.tensor_scalar(gw[:, 3, :], gw[:, 3, :], rs[:, 8, i:i + 1], None, ALU.mult))
                if i >= 1:
                    dve.wait_ge(s["qtT_done"], i)
                round_e4m3(qt[:, :], gw[:, 3, :], gw[:, 4, :]).then_inc(s["qt_ready"], 1)

            def output_rows(i):
                k = i % 2
                dve.wait_ge(s["dn_done"], i + 1)
                if i >= 2:
                    dve.wait_ge(s_o[k], 16 * (i // 2))
                V.scalar_tensor_tensor(yo[:, k, :], pw[:, 0:D], rs[:, 9, i:i + 1], srow[:, 2 * INTER:], ALU.mult, ALU.mult)\
                    .then_inc(s["yo_read"], 1)
                dve.wait_ge(s["yo_read"], i + 1)
                V.tensor_tensor(yo[:, k, :], yo[:, k, :], x1[:, i, :], ALU.add).then_inc(s["yo_ready"], 1)

            for i in range(NT + 2):
                if i < NT:
                    mixed_rows(i)
                if 1 <= i <= NT:
                    inner_rows(i - 1)
                if i >= 2:
                    output_rows(i - 2)

        @block.gpsimd
        def _(pool):
            G = nc.gpsimd
            links = [0]

            def link(ins):
                links[0] += 1
                ins.then_inc(s["pool_link"], 1)
                pool.wait_ge(s["pool_link"], links[0])

            G.memset(t2[:, :], 0.0).then_inc(s["ms_done"], 1)
            link(G.memset(nhalf[:, :], -0.5))
            pool.wait_ge(s["par_in"], 16 * 8)

            def rstd(first, count, done):
                link(G.tensor_scalar(ssq[:, 1, first:first + count], ssq[:, 0, first:first + count], 1.0 / D, EPS, ALU.mult, ALU.add))
                G.tensor_tensor(ssq[:, 2, first:first + count], ssq[:, 1, first:first + count], nhalf[:, 0:count], ALU.pow).then_inc(done, 1)

            for n in range(2 * B):
                l, b = n // B, n % B
                pool.wait_ge(s["fT_copied"], b + 1)
                if n >= 1:
                    pool.wait_ge(s["u_used"], n)
                for c in range(C):
                    last = G.tensor_scalar(U[:, 1, c * S:(c + 1) * S], fT[:, b, c * S:(c + 1) * S], wu[:, 2 * l + 1, c:c + 1], 30.0,
                                           ALU.add, ALU.min)
                last.then_inc(s["ku_ready"], 1)
                pool.wait_ge(s["uexp_ready"], n + 1)
                G.tensor_tensor(U[:, 0, :], U[:, 1, :], fT[:, b, :], ALU.mult).then_inc(s["u_ready"], 1)
                if n < B:
                    pool.wait_ge(s["ssq_ready"], n + 1)
                    rstd(TT * b, TT, s["rstd_ready"])

            def rope_sum(n, parity, k):
                pool.wait_ge(s["rope_done"], n + 1)
                if not isinstance(n, int) or n >= 2:
                    pool.wait_ge(s["qhi_done"], n - 1)
                G.tensor_tensor(qr[:, parity, :], t1[:, :], t2[:, :], ALU.add).then_inc(s["radd_done"], 1)
                pool.wait_ge(s["radd_done"], n + 1)
                pool.wait_ge(s["qhi_done"], n + 1)
                if k is None:
                    G.tensor_tensor(q16[:, parity, 1, :], qr[:, parity, :], q16[:, parity, 0, :], ALU.subtract).then_inc(s["qlo_done"], 1)
                else:
                    at = slice(k // KVH * PAIR, (k // KVH + 1) * PAIR)
                    G.tensor_tensor(kT[:, 1, k % KVH, at], qr[:, parity, :], kT[:, 0, k % KVH, at], ALU.subtract).then_inc(s["qlo_done"], 1)

            for n in range(KU):
                rope_sum(n, n % 2, n)

            def normalise(u, parity):
                pool.wait_ge(s["recip_done"], u + 1)
                pool.sem_inc(s["pool_paused"], 1)
                for b in range(2):
                    for qb in range(2):
                        o, w = (0, P) if qb == 0 else (P, 2 * P)
                        k = 2 * b + qb
                        last = G.tensor_scalar(pr[:, parity, b, o:o + w], pr[:, parity, b, o:o + w], sums[:, parity, 1, k:k + 1], None, ALU.mult)
                last.then_inc(s["norm_done"], 1)

            def step(u, parity):
                fixed = isinstance(u, int)
                if not fixed or 2 <= u < QU + 2:
                    normalise(u - 2, parity)
                if not fixed or u < QU:
                    rope_sum(KU + u, parity, None)

            attention_steps(pool, step, lambda: None)

            pool.wait_ge(s["wo_done"], NT)
            pool.wait_ge(s["didx_in"], 16)

            def gather_rows(name):
                for c in range(NI):
                    G.indirect_dma_start(out=rows[0:IQ, c * D:(c + 1) * D], out_offset=None, in_=t[name],
                                         in_offset=bass.IndirectOffsetOnAxis(ap=didx[:, c:c + 1], axis=0)).then_inc(s["rows_in"], 16)

            gather_rows("L1_ffn_w_gate")
            for i in range(NT):
                pool.wait_ge(s["ssq2_ready"], i + 1)
                rstd(i, 1, s["rstd2_ready"])
            pool.wait_ge(s["slots_ready"], 1)
            pool.wait_ge(s["zero_out"], 16)
            for i in range(NT):
                for k in range(2):
                    G.indirect_dma_start(out=xs_dram[:, :], out_offset=bass.IndirectOffsetOnAxis(ap=sloti[:, k, i:i + 1], axis=0),
                                         in_=h2[:, i, :], in_offset=None).then_inc(s["scatter_out"], 16)
            pool.wait_ge(s["rq_ready"], 1)
            gather_rows("L1_ffn_w_up")
            pool.wait_ge(s["rq_ready"], 2)
            G.dma_start(rows[:, 0:C * INTER].rearrange("p (c n) -> p c n", c=C),
                        t["L1_ffn_w_down"].rearrange("(c p) n -> p c n", p=P)).then_inc(s["rows_in"], 16)
            pool.wait_ge(s_y[0], 16 * ((MT + 1) // 2))
            pool.wait_ge(s_y[1], 16 * (MT // 2))
            for i in range(NT):
                if i >= 2:
                    pool.wait_ge(s["x1_ready"], i - 1)
                for k, y in enumerate((y1, y2)):
                    G.indirect_dma_start(out=y[:, i % 2, :], out_offset=None, in_=ys_dram[:, :],
                                         in_offset=bass.IndirectOffsetOnAxis(ap=sloti[:, k, i:i + 1], axis=0)).then_inc(s_g[i % 2], 16)


INPUTS = ["x", "fside_BxSxS_0", "cond_512", "L0_cond_w", "L0_cond_u", "L0_ffn_ln_w", "L0_ffn_ff_ln_w", "L0_ffn_wq", "L0_ffn_wk",
          "L0_ffn_wv", "L0_ffn_wo", "L0_ffn_gate_w", "L0_ffn_w1", "L0_ffn_w3", "L0_ffn_w2", "L1_cond_w", "L1_cond_u",
          "L1_ffn_w_gate", "L1_ffn_w_up", "L1_ffn_w_down", "L1_ffn_down_reorder_index"]


def kernel(**inputs):
    import concourse.bacc as bacc
    from concourse.bass_utils import run_bass_kernel_spmd as run

    nc = bacc.Bacc("TRN2", target_bir_lowering=False, num_devices=1)
    arrays, t = {}, {}
    for name in INPUTS:
        arrays[f"in_{name}"] = np.ascontiguousarray(inputs[name])
    arrays["in_consts"] = constants()
    for name, a in arrays.items():
        t[name[3:]] = nc.dram_tensor(name, a.shape, mybir.dt.from_np(a.dtype), kind="ExternalInput").ap()
    out = nc.dram_tensor("out_dram", (B, S, D), F32, kind="ExternalOutput").ap()
    build(nc, t, out)
    return run(nc, [arrays], core_ids=[0]).results[0]["out_dram"]
```

```python
import numpy as np
import concourse.bass as bass
from concourse import mybir
from contextlib import ExitStack

F32 = mybir.dt.float32
F16 = mybir.dt.float16
BF16 = mybir.dt.bfloat16
I32 = mybir.dt.int32
U32 = mybir.dt.uint32
ALU = mybir.AluOpType
ACT = mybir.ActivationFunctionType
AX = mybir.AxisListType

P = 128
B, S, D = 4, 256, 256
TT = S // P
NT = B * TT
C = D // P
H, KVH, HD = 16, 4, 128
NE, FF = 8, 896
FC = FF // P
FA, FB = 4 * P, FF - 4 * P
MT = 2 * B * S // P + NE - 1
SLOTS = MT * P
WEXP = C * FF * 2 + FC * D
RING = 3
INTER = 704
IQ = 88
NI = INTER // IQ
IH = INTER // 2
WS = 64.0
EPS = 1e-5
QKV = (H + 2 * KVH) * HD
PAIR = 2 * S
KU = 2 * KVH
QU = 2 * H
ROUND = 6
LAG = 5
SCALE = float(HD) ** -0.5
BLK = 3 * P
FP8_MAX = 448.0
MAGIC = 1.5 * 2.0 ** 20
FP8_LEAST = 2.0 ** -6


def constants():
    pos = np.arange(S, dtype=np.float32)
    inv = np.float32(1e6) ** (-np.arange(0, HD, 2, dtype=np.float32) / np.float32(HD))
    ang = (pos[:, None] * inv[None, :].astype(np.float32)).astype(np.float32)
    cos, sin = np.cos(ang).T, np.sin(ang).T
    rope = np.stack([np.concatenate([cos, cos]), np.concatenate([-sin, sin])], 1) / WS
    diag = np.where(np.arange(P)[None, :] > np.arange(P)[:, None], -1e38, 0.0)
    mask = np.concatenate([diag, np.zeros((P, P)), diag], 1)
    before = (np.arange(P)[:, None] < np.arange(P)[None, :]).astype(np.float32)
    iota = np.tile(np.arange(NE, dtype=np.float32), (P, 1))
    tiles = np.tile(np.arange(MT, dtype=np.float32), (P, 1))
    consts = np.concatenate([np.eye(P), mask, before, np.ones((P, P)), iota, tiles, rope.reshape(P, -1)], 1)
    return np.ascontiguousarray(consts, dtype=np.float32)


def build(nc, t, out, dbg=None):
    ctx = ExitStack()
    with ctx:
        def sb(name, shape, dt=F32):
            return ctx.enter_context(nc.sbuf_tensor(name, shape, dt))

        def sem(name):
            return ctx.enter_context(nc.semaphore(name))

        def cut(region, offset, count, dt=F32):
            v = region[:, offset:offset + count]
            return v if dt == F32 else v.bitcast(dt)

        CN = P + BLK + P + P + NE + MT + 2 * S
        con = sb("con", [P, CN])
        ident = con[:, 0:P]
        mask = con[:, P:P + BLK]
        before = con[:, P + BLK:2 * P + BLK]
        ones = con[:, 2 * P + BLK:3 * P + BLK]
        o = 3 * P + BLK
        iota_e = con[:, o:o + NE]
        iota_t = con[:, o + NE:o + NE + MT]
        o += NE + MT
        rope_cos = con[:, o:o + S]
        rope_sin = con[:, o + S:o + 2 * S]

        stage_words = C * QKV
        wreg = sb("wreg", [P, RING * WEXP + 512])
        stage = cut(wreg, 0, stage_words).rearrange("p (c n) -> p c n", c=C)
        stage_wo = cut(wreg, 0, H * D).rearrange("p (h n) -> p h n", h=H)
        qkv16 = cut(wreg, stage_words, C * QKV, F16).rearrange("p (s c n) -> p s c n", s=2, c=C)
        wo16 = cut(wreg, 2 * stage_words, H * D, F16).rearrange("p (s h n) -> p s h n", s=2, h=H)

        AW = 4096 + 4096 + 2048 + 8192
        areg = sb("areg", [P, AW])
        kT = cut(areg, 0, 4096).rearrange("p (h n) -> p h n", h=KVH)
        v16 = cut(areg, 4096, 4096, F16).rearrange("p (s i n) -> p s i n", s=2, i=NT)
        hT = cut(areg, 8192, 2048, F16).rearrange("p (s c n) -> p s c n", s=2, c=C)
        oT = cut(areg, 10240, 8192, F16).rearrange("p (s h n) -> p s h n", s=2, h=H)
        f_tok = cut(areg, 0, 2048).rearrange("p (b i n) -> p b i n", b=B, i=TT)
        xn = cut(areg, 2048, 512)
        sg = cut(areg, 2560, 2048).rearrange("p (b n) -> p b n", b=B)

        def two_rows(offset, sets=1):
            v = cut(areg, offset, sets * 1024)
            return v.rearrange("p (q k n) -> p q k n", q=sets, k=2) if sets > 1 else v.rearrange("p (k n) -> p k n", k=2)

        def recurrence_buffers(base):
            return (two_rows(base, 2), two_rows(base + 2048, 2), two_rows(base + 4096), two_rows(base + 5120),
                    cut(areg, base + 6144, 512))

        cond_buf = (recurrence_buffers(10240), recurrence_buffers(6784))
        x_in = sb("x_in", [P, B, TT * D])
        xs = cut(areg, 0, 2 * D).rearrange("p (k n) -> p k n", k=2)
        xsT = cut(areg, 512, 2 * D).rearrange("p (k n) -> p k n", k=2)
        eh = cut(areg, 1024, FF)
        hh = cut(areg, 1920, FF)
        hhT = cut(areg, 2816, FF).rearrange("p (c n) -> p c n", c=FC)
        ysb = cut(areg, 3712, 2 * D).rearrange("p (k n) -> p k n", k=2)
        h2 = cut(areg, 4224, NT * D).rearrange("p (i n) -> p i n", i=NT)
        h2T = cut(areg, 6272, 2 * D).rearrange("p (k n) -> p k n", k=2)
        y1 = cut(areg, 6784, 2 * D).rearrange("p (k n) -> p k n", k=2)
        y2 = cut(areg, 7296, 2 * D).rearrange("p (k n) -> p k n", k=2)
        xq = cut(areg, 7808, 5 * D).rearrange("p (k n) -> p k n", k=5)
        qx = cut(areg, 9088, D // 2, BF16)
        qxT = cut(areg, 9216, D // 2, BF16).rearrange("p (c n) -> p c n", c=C)
        gw = cut(areg, 9344, 5 * INTER).rearrange("p (k n) -> p k n", k=5)
        qt = cut(areg, 12864, INTER // 2, BF16)
        qtT = cut(areg, 13216, NI * P // 2, BF16).rearrange("p (c n) -> p c n", c=NI)
        yo = cut(areg, 13728, 2 * D).rearrange("p (k n) -> p k n", k=2)

        x0 = sb("x0", [P, NT, D])
        ratio1 = sb("ratio1", [P, NT, D])
        fT = ratio1[:, :, :].rearrange("p (b i) n -> p b (i n)", b=B)
        x1 = x0
        wln = sb("wln", [P, C])
        ffln = sb("ffln", [P, D])
        wu = sb("wu", [P, 4, C])
        cond = sb("cond", [P, B, 64])
        tf = sb("tf", [P, 8, B])
        dec = sb("dec", [P, 3, 2, C])
        decay = sb("decay", [P, 2, C, B])
        gate_w = sb("gate_w", [P, C, NE])
        cond1 = sb("cond1", [P, B, C + 1])
        cond1b = sb("cond1b", [P, 2, C + 1])

        breg = sb("breg", [P, 3 * 2 * PAIR + 2 * 4 * BLK])
        t1, t2, qr = (cut(breg, k * 2 * PAIR, 2 * PAIR).rearrange("p (k n) -> p k n", k=2) for k in range(3))
        pr = cut(breg, 6 * PAIR, 4 * BLK).rearrange("p (k b n) -> p k b n", k=2, b=2)
        pT = cut(breg, 6 * PAIR + 4 * BLK, 4 * BLK, F16).rearrange("p (k s b n) -> p k s b n", k=2, s=2, b=2)
        mx = sb("mx", [P, 2, 2, 4])
        sums = sb("sums", [P, 2, 2, 4])
        nhalf = sb("nhalf", [P, 4])
        ssq = sb("ssq", [P, 4, NT])

        srow = cut(areg, 14240, 2 * INTER + D)
        q1w = cut(areg, 15904, C * INTER, BF16).rearrange("p (m c n) -> p m c n", m=2, c=C)
        q1d = cut(areg, 17312, NI * D // 2, BF16).rearrange("p (c n) -> p c n", c=NI)
        rows = cut(breg, 0, 2048)
        grid = cut(breg, 2048, 2048)
        rq = cut(breg, 4096, 1024, BF16)
        wmax = sb("wmax", [P, NI])
        winv = sb("winv", [P, NI])
        wscale = sb("wscale", [P, 3, NI])
        didx = sb("didx", [IQ, NI], I32)

        pb = [ctx.enter_context(nc.psum_tensor(f"pb{i}", [P, 512], F32)) for i in range(2)]
        sc2 = ctx.enter_context(nc.psum_tensor("sc2", [P, 2, 512], F32))
        pt2 = ctx.enter_context(nc.psum_tensor("pt2", [P, 2, 512], F32))
        po = ctx.enter_context(nc.psum_tensor("po", [P, 512], F32))
        pw = ctx.enter_context(nc.psum_tensor("pw", [P, 512], F32))

        rt = sb("rt", [P, 14, NT * NE])
        lg, M1, M2, MK, tots, pos, prod = (rt[:, k, :] for k in range(7))
        m8 = rt[:, 7, :]
        i8 = rt[:, 8, :].bitcast(U32)
        car = rt[:, 9:11, :].rearrange("p a n -> p (a n)")[:, 0:(NT + 1) * NE]
        idf = rt[:, 11, 0:2 * NT]
        gts = rt[:, 12, :].rearrange("p (k n) -> p k n", n=NT)
        ex8 = rt[:, 13, :].rearrange("p (k n) -> p k n", n=NE)
        exi = sb("exi", [P, 2, NE], I32)
        slotf = sb("slotf", [P, 2, NT])
        sloti = sb("sloti", [P, 2, NT], I32)
        cmp = sb("cmp", [P, MT * NE])
        tmap = sb("tmap", [P, 2, MT])
        tmi = sb("tmi", [1, MT], I32)
        endi = sb("endi", [1, NE], I32)
        identb = sb("identb", [P, P], BF16)
        rs = sb("rs", [P, 10, NT])

        xs_dram = nc.dram_tensor("xs_dram", (SLOTS, D), F32).ap()
        scale_dram = nc.dram_tensor("scale_dram", (2 * INTER + D,), F32).ap()
        ys_dram = nc.dram_tensor("ys_dram", (SLOTS, D), F32).ap()

        names = """con_in par_in qkv_in wo_in didx_in gatew_in upw_in downw_in zero_out scatter_out
            fT_done fT_copied kmin_ready tfsum tf_exp dec_exp sg_exp ku_ready uexp_ready u_ready u_used
            ratT_ready rat_done x0_ready ssq_ready rstd_ready xn_ready hTp_done hi_done hlo_done ms_done act_link dve_link pool_link
            qkvhi_done qkvlo_done wohi_done wolo_done
            swap_done sin_done proj_done rope_done radd_done v_done vhi_done vlo_done
            score_done max_done nmax_done exp_done recip_done norm_done pT_done pThi_done pTlo_done
            av_done ohi_done olo_done wo_done x1a_done
            ssq2_ready rstd2_ready h2_ready h2T_done h2T_copied gate_done lg_ready d_ready ge_ready mk_ready rank_done slots_ready tmap_ready
            rq_ready rqT_done rq_copied ratio1_copied scale_out scale_in side_link wscale_ready
            w_ready tiles_done xs_free xT_done xT_copied upa_done upb_done expa_done expb_done silua_done silub_done
            hT_done hT_copied down_done y_copied moe_link
            comb_in x1_ready sgx_ready qx_ready qxT_done qxT_copied gu_done g_ready ge1_ready gu_read qt_ready qtT_done qtT_copied dn_done yo_ready out_done
            dve_paused identb_ready rows_in gate_tile yo_read sx_ready act2_link g1_ready""".split()
        s = {n: sem(n) for n in names}
        s_f = [sem(f"f_in{b}") for b in range(B)]
        s_x = [sem(f"x_in{b}") for b in range(B)]
        s_w = [sem(f"w_in{k}") for k in range(RING)]
        s_xs = [sem(f"xs_in{k}") for k in range(2)]
        s_y = [sem(f"y_out{k}") for k in range(2)]
        s_g = [sem(f"gather_in{k}") for k in range(2)]
        s_o = [sem(f"out_out{k}") for k in range(2)]

        block = ctx.enter_context(nc.Block())

        def tokens(a, b):
            return a[b].rearrange("(i p) d -> p i d", p=P)

        def load_expert(eng, e):
            base = (e % RING) * WEXP
            n = C * FF
            eng.dma_start(wreg[:, base:base + n].rearrange("p (c n) -> p c n", c=C),
                          t["L0_ffn_w1"][e].rearrange("(c p) n -> p c n", p=P)).then_inc(s_w[e % RING], 16)
            eng.dma_start(wreg[:, base + n:base + 2 * n].rearrange("p (c n) -> p c n", c=C),
                          t["L0_ffn_w3"][e].rearrange("(c p) n -> p c n", p=P)).then_inc(s_w[e % RING], 16)
            eng.dma_start(wreg[:, base + 2 * n:base + WEXP].rearrange("p (c n) -> p c n", c=FC),
                          t["L0_ffn_w2"][e].rearrange("(c p) n -> p c n", p=P)).then_inc(s_w[e % RING], 16)

        @block.sync
        def _(sp):
            sp.dma_start(con[:, :], t["consts"]).then_inc(s["con_in"], 16)
            for b in range(B):
                sp.dma_start(f_tok[:, b], tokens(t["fside_BxSxS_0"], b)).then_inc(s_f[b], 16)
            with nc.allow_non_contiguous_dma(reason="short vectors, one element a partition"):
                for k, n in enumerate(("L0_cond_w", "L0_cond_u", "L1_cond_w", "L1_cond_u")):
                    sp.dma_start(wu[:, k], t[n].rearrange("(c p) -> p c", p=P)).then_inc(s["par_in"], 16)
                sp.dma_start(wln[:, :], t["L0_ffn_ln_w"].rearrange("(c p) -> p c", p=P)).then_inc(s["par_in"], 16)
                sp.dma_start(didx[:, :], t["L1_ffn_down_reorder_index"].rearrange("(c p) -> p c", p=IQ))\
                    .then_inc(s["didx_in"], 16)
            sp.dma_start(cond[:, :, :], t["cond_512"].rearrange("(a b) n -> a b n", a=1).to_broadcast([P, B, 64]))\
                .then_inc(s["par_in"], 16)
            sp.dma_start(ffln[:, :], t["L0_ffn_ff_ln_w"].rearrange("(a n) -> a n", a=1).to_broadcast([P, D]))\
                .then_inc(s["par_in"], 16)
            sp.dma_start(gate_w[:, :, :], t["L0_ffn_gate_w"].rearrange("(c p) n -> p c n", p=P))\
                .then_inc(s["par_in"], 16)
            for b in range(B):
                sp.dma_start(x_in[:, b].rearrange("p (i d) -> p i d", i=TT), tokens(t["x"], b)).then_inc(s_x[b], 16)
            at = 0
            for n, w in (("L0_ffn_wq", H * HD), ("L0_ffn_wk", KVH * HD), ("L0_ffn_wv", KVH * HD)):
                sp.dma_start(stage[:, :, at:at + w], t[n].rearrange("(c p) n -> p c n", p=P)).then_inc(s["qkv_in"], 16)
                at += w
            sp.wait_ge(s["ms_done"], 1)
            sp.dma_start(xs_dram.rearrange("(t p) n -> p t n", p=P),
                         t2[:, 0, 0:D].rearrange("p (a n) -> p a n", a=1).to_broadcast([P, MT, D])).then_inc(s["zero_out"], 16)
            sp.wait_ge(s["qkvhi_done"], 1)
            sp.wait_ge(s["qkvlo_done"], 1)
            sp.dma_start(stage_wo, t["L0_ffn_wo"].rearrange("(h p) n -> p h n", p=P)).then_inc(s["wo_in"], 16)
            sp.wait_ge(s["wohi_done"], 1)
            sp.wait_ge(s["wolo_done"], 1)
            load_expert(sp, 0)
            sp.wait_ge(s["wo_done"], NT)
            load_expert(sp, 1)
            load_expert(sp, 2)
            sp.wait_ge(s["tmap_ready"], 1)
            for e in range(NE):
                if e >= RING:
                    last = sp.value_load(endi[0:1, e - RING:e - RING + 1], min_val=1, max_val=MT + 1)
                    sp.wait_ge(s["down_done"], last)
                    load_expert(sp, e)
                sp.wait_ge(s_w[e % RING], 48 * (e // RING + 1))
                sp.sem_inc(s["w_ready"], 1)
            for i in range(NT):
                sp.wait_ge(s["yo_ready"], i + 1)
                sp.dma_start(out.rearrange("b s d -> (b s) d")[i * P:(i + 1) * P, :], yo[:, i % 2]).then_inc(s_o[i % 2], 16)
            for k in range(2):
                sp.wait_ge(s_o[k], 16 * NT // 2)

        def attention_steps(eng, step, middle):
            for u in range(LAG):
                step(u, u % 2)
            with eng.Fori(0, H // 2) as i:
                step(i * 2 + LAG, LAG % 2)
                step(i * 2 + LAG + 1, 1 - LAG % 2)
            middle()
            with eng.Fori(0, (H - LAG) // 2) as i:
                step(i * 2 + H + LAG, LAG % 2)
                step(i * 2 + H + LAG + 1, 1 - LAG % 2)
            for u in range(H + LAG + (H - LAG) // 2 * 2, QU + LAG):
                step(u, u % 2)

        def expert_steps(eng, step, ratio_piece, weight_piece, down_piece):
            def bound(f, *a):
                return lambda bank: f(*a, bank)
            step(0, 0)
            with eng.Fori(0, 2) as i:
                for k in range(ROUND):
                    pieces = {2: [bound(weight_piece, i, 0, h) for h in range(2)],
                              3: [bound(weight_piece, i, 1, h) for h in range(2)],
                              4: [bound(ratio_piece, i * 2, h) for h in range(2)],
                              5: [bound(ratio_piece, i * 2 + 1, h) for h in range(2)]}.get(k, (None, None))
                    step(i * ROUND + (k + 1), (k + 1) % 2, pieces, (i, k))
            first = 2 * ROUND + 1
            step(first, 1)
            step(first + 1, 0)
            for k in range(2):
                step(first + 2 + k, 1 - k, [bound(down_piece, k, h) for h in range(2)])
            with eng.Fori(0, (MT - 2 - first - 4) // 2) as i:
                step(i * 2 + first + 4, 1)
                step(i * 2 + first + 5, 0)
            for n in range(MT - 2, MT + 1):
                step(n, n % 2)

        def within(u, lag):
            return not isinstance(u, int) or lag <= u < QU + lag

        @block.tensor
        def _(pe):
            pe.wait_ge(s["con_in"], 16)
            for b in range(B):
                pe.wait_ge(s_f[b], 16)
                if b >= 2:
                    pe.wait_ge(s["fT_copied"], b - 1)
                for c in range(C):
                    for i in range(TT):
                        last = nc.tensor.transpose(pb[b % 2][:, c * S + i * P:c * S + (i + 1) * P],
                                                   f_tok[:, b, i, c * P:(c + 1) * P], ident)
                last.then_inc(s["fT_done"], 1)

            def ratio_transposes(n):
                pe.wait_ge(s["ratT_ready"], n + 1)
                if n >= 2:
                    pe.wait_ge(s["x0_ready"], n - 1)
                for i in range(TT):
                    for c in range(C):
                        last = nc.tensor.transpose(sc2[:, n % 2, i * D + c * P:i * D + (c + 1) * P],
                                                   cond_buf[0][4][:, c * S + i * P:c * S + (i + 1) * P], ident)
                last.then_inc(s["rat_done"], 1)

            def hidden_transposes(b):
                pe.wait_ge(s["xn_ready"], b + 1)
                if b >= 2:
                    pe.wait_ge(s["hlo_done"], b - 1)
                for c in range(C):
                    for i in range(TT):
                        last = nc.tensor.transpose(pt2[:, b % 2, c * S + i * P:c * S + (i + 1) * P],
                                                   xn[:, i * D + c * P:i * D + (c + 1) * P], ident)
                last.then_inc(s["hTp_done"], 1)

            for b in range(B):
                ratio_transposes(b)
                if b >= 1:
                    hidden_transposes(b - 1)
            hidden_transposes(B - 1)

            def split_products(bank, w, m, first=True, final=True):
                order = ((0, 0), (0, 1), (1, 0))
                for k, (a, b) in enumerate(order):
                    last = nc.tensor.matmul(bank, w(a), m(b), start=first and k == 0, stop=final and k == 2)
                return last

            def proj(n, bank, col, pair):
                for c in range(C):
                    last = split_products(bank[:, :], lambda a: qkv16[:, a, c, bass.ds(col, HD)],
                                          lambda a: hT[:, a, c, bass.ds(pair * PAIR, PAIR)], c == 0, c == C - 1)
                last.then_inc(s["proj_done"], 1)

            pe.wait_ge(s["hlo_done"], B)
            pe.wait_ge(s["hi_done"], B)
            pe.wait_ge(s["qkvhi_done"], 1)
            pe.wait_ge(s["qkvlo_done"], 1)
            pe.wait_ge(s["fT_copied"], B)
            for n in range(KU):
                if n >= 2:
                    pe.wait_ge(s["swap_done"], n - 1)
                proj(n, pb[n % 2], H * HD + (n % KVH) * HD, n // KVH)
            for i in range(NT):
                bank = (po, pw)[i % 2]
                if i >= 2:
                    pe.wait_ge(s["vlo_done"], i - 1)
                for c in range(C):
                    last = split_products(bank[:, :], lambda a: hT[:, a, c, i * P:(i + 1) * P],
                                          lambda a: qkv16[:, a, c, (H + KVH) * HD:QKV], c == 0, c == C - 1)
                last.then_inc(s["v_done"], 1)

            def scores(u, buf):
                pe.wait_ge(s["radd_done"], KU + u + 1)
                if not isinstance(u, int) or u >= 1:
                    pe.wait_ge(s["max_done"], u)
                kv, pair = (u % H) // (H // KVH), u // H
                for b in range(2):
                    for qb in range(2):
                        o, w = (0, P) if qb == 0 else (P, 2 * P)
                        last = nc.tensor.matmul(sc2[:, b, o:o + w], qr[:, buf, b * S + qb * P:b * S + (qb + 1) * P],
                                                kT[:, bass.ds(kv, 1), bass.ds(pair * PAIR + b * S, w)]
                                                .rearrange("p a n -> p (a n)"), start=True, stop=True)
                last.then_inc(s["score_done"], 1)

            def prob_transposes(u, buf):
                pe.wait_ge(s["norm_done"], u + 1)
                if not isinstance(u, int) or u >= 1:
                    pe.wait_ge(s["pTlo_done"], u)
                for b in range(2):
                    for k in range(3):
                        last = nc.tensor.transpose(pt2[:, b, k * P:(k + 1) * P], pr[:, buf, b, k * P:(k + 1) * P], ident)
                last.then_inc(s["pT_done"], 1)

            def weighted_values(u, buf):
                pe.wait_ge(s["pTlo_done"], u + 1)
                if not isinstance(u, int) or u >= 1:
                    pe.wait_ge(s["olo_done"], u)
                kv, pair = (u % H) // (H // KVH), u // H
                for b in range(2):
                    for kb in range(2):
                        o, w = (0, S) if kb == 0 else (2 * P, P)
                        last = split_products(po[:, b * S + kb * P:b * S + kb * P + w],
                                              lambda a: v16[:, a, bass.ds(pair * 4 + b * TT + kb, 1), bass.ds(kv * HD, HD)]
                                              .rearrange("p a n -> p (a n)"),
                                              lambda a: pT[:, buf, a, b, o:o + w], kb == 0, kb == 1)
                last.then_inc(s["av_done"], 1)

            def route(i):
                pe.wait_ge(s["h2_ready"], i + 1)
                if i >= 2:
                    pe.wait_ge(s["h2T_copied"], i - 1)
                for c in range(C):
                    last = nc.tensor.transpose(pb[i % 2][:, c * P:(c + 1) * P], h2[:, i, c * P:(c + 1) * P], ident)
                last.then_inc(s["h2T_done"], 1)
                pe.wait_ge(s["h2T_copied"], i + 1)
                for c in range(C):
                    last = nc.tensor.matmul(po[:, i * NE:(i + 1) * NE], h2T[:, i % 2, c * P:(c + 1) * P], gate_w[:, c, :],
                                            start=c == 0, stop=c == C - 1)
                last.then_inc(s["gate_tile"], 1)

            def project_out(pair):
                pe.wait_ge(s["olo_done"], (pair + 1) * H)
                pe.wait_ge(s["wohi_done"], 1)
                pe.wait_ge(s["wolo_done"], 1)
                for i in range(4):
                    n = 4 * pair + i
                    if n >= 1:
                        pe.wait_ge(s["x1a_done"], n)
                    for h in range(H):
                        last = split_products(pw[:, 0:D], lambda a: oT[:, a, h, i * P:(i + 1) * P],
                                              lambda a: wo16[:, a, h, :], h == 0, h == H - 1)
                    last.then_inc(s["wo_done"], 1)
                    if pair == 1 and i < 3:
                        for j in ((0, 1), (2, 3), (4,))[i]:
                            route(j)

            def step(u, parity):
                if within(u, 0):
                    pe.wait_ge(s["swap_done"], KU + u - 1)
                    proj(None, pb[parity], (u % H) * HD, u // H)
                if within(u, 2):
                    scores(u - 2, parity)
                if within(u, 4):
                    prob_transposes(u - 4, parity)
                if within(u, 5):
                    weighted_values(u - 5, 1 - parity)

            pe.wait_ge(s["vlo_done"], NT)
            pe.wait_ge(s["x0_ready"], B)
            attention_steps(pe, step, lambda: project_out(0))
            project_out(1)

            for i in range(5, NT):
                route(i)
            pe.wait_ge(s["mk_ready"], 1)
            nc.tensor.matmul(po[:, 128:128 + NT * NE], before, MK, start=True, stop=True)
            nc.tensor.matmul(po[:, 256:256 + NT * NE], ones, MK, start=True, stop=True).then_inc(s["rank_done"], 1)

            def ratio_piece(b, i, bank):
                pe.wait_ge(s["ratT_ready"], B + b + 1)
                for c in range(C):
                    last = nc.tensor.transpose(bank[:, D + c * P:D + (c + 1) * P],
                                               cond_buf[1][4][:, c * S + i * P:c * S + (i + 1) * P], ident)
                if i == TT - 1:
                    last.then_inc(s["rat_done"], 1)

            def weight_piece(m, kc, half, bank):
                pe.wait_ge(s["rq_ready"], m + 1)
                for j in range(NI // 2):
                    c = half * (NI // 2) + j
                    last = nc.tensor.transpose(bank[:, D:].bitcast(BF16)[:, j * IQ:(j + 1) * IQ],
                                               rq[0:IQ, c * D + kc * P:c * D + (kc + 1) * P], identb[0:IQ, 0:IQ])
                if (kc, half) == (1, 1):
                    last.then_inc(s["rqT_done"], 1)

            def down_piece(hc, half, bank):
                pe.wait_ge(s["rq_ready"], 3)
                for j in range(NI // 2):
                    c = half * (NI // 2) + j
                    last = nc.tensor.transpose(bank[0:IQ, D:].bitcast(BF16)[:, j * P:(j + 1) * P],
                                               rq[:, hc * INTER + c * IQ:hc * INTER + (c + 1) * IQ], identb[:, :])

            def x_transposes(n, parity, piece=None):
                pe.wait_ge(s_xs[parity], 16 * (n // 2 + 1))
                if not isinstance(n, int) or n >= 1:
                    pe.wait_ge(s["xT_copied"], n)
                if piece:
                    piece(po)
                for c in range(C):
                    last = nc.tensor.transpose(po[:, c * P:(c + 1) * P], xs[:, parity, c * P:(c + 1) * P], ident)
                last.then_inc(s["xT_done"], 1)

            def up(n, parity, base, part):
                lo, w = (0, FA) if part == 0 else (FA, FB)
                for m in range(2):
                    bank = (pb[m] if part == 0 else sc2[:, m])[:, 0:w]
                    for c in range(C):
                        last = nc.tensor.matmul(bank, xsT[:, parity, c * P:(c + 1) * P],
                                                wreg[:, bass.ds(base + (m * C + c) * FF + lo, w)], start=c == 0, stop=c == C - 1)
                last.then_inc(s["upa_done" if part == 0 else "upb_done"], 1)

            def h_transposes(n):
                pe.wait_ge(s["silub_done"], n + 1)
                if not isinstance(n, int) or n >= 1:
                    pe.wait_ge(s["hT_copied"], n)
                for c in range(FC):
                    last = nc.tensor.transpose(pt2[:, c // 4, c % 4 * P:(c % 4 + 1) * P], hh[:, c * P:(c + 1) * P], ident)
                last.then_inc(s["hT_done"], 1)

            def down(n, base, piece=None):
                pe.wait_ge(s["hT_copied"], n + 1)
                if not isinstance(n, int) or n >= 1:
                    pe.wait_ge(s["y_copied"], n)
                if piece:
                    piece(pw)
                for c in range(FC):
                    last = nc.tensor.matmul(pw[:, 0:D], hhT[:, c, :], wreg[:, bass.ds(base + 2 * C * FF + c * D, D)],
                                            start=c == 0, stop=c == FC - 1)
                last.then_inc(s["down_done"], 1)

            pe.wait_ge(s["tmap_ready"], 1)
            pe.wait_ge(s["identb_ready"], 1)
            pe.sem_inc(s["down_done"], 1)
            x_transposes(0, 0)

            def tile_base(n):
                e = pe.value_load(tmi[0:1, bass.ds(n, 1)], min_val=0, max_val=NE - 1)
                return e, (e % RING) * WEXP

            def tile_step(n, parity, pieces=(None, None), place=None):
                fixed = isinstance(n, int)
                if not fixed or n < MT:
                    e, base = tile_base(n)
                    pe.wait_ge(s["w_ready"], e + 1)
                    pe.wait_ge(s["xT_copied"], n + 1)
                    if not fixed or n >= 1:
                        pe.wait_ge(s["silua_done"], n)
                    up(n, parity, base, 0)
                if not fixed or n >= 1:
                    h_transposes(n - 1)
                if not fixed or n < MT:
                    if not fixed or n + 1 < MT:
                        x_transposes(n + 1, 1 - parity, pieces[0])
                    up(n, parity, base, 1)
                if not fixed or n >= 1:
                    down(n - 1, tile_base(n - 1)[1], pieces[1])

            expert_steps(pe, tile_step, ratio_piece, weight_piece, down_piece)

            def quantised_transposes(i):
                pe.wait_ge(s["qx_ready"], i + 1)
                if i >= 1:
                    pe.wait_ge(s["qxT_copied"], i)
                else:
                    pe.wait_ge(s["xT_copied"], MT)
                for c in range(C):
                    last = nc.tensor.transpose(po[:, :].bitcast(BF16)[:, c * P:(c + 1) * P], qx[:, c * P:(c + 1) * P], identb[:, :])
                last.then_inc(s["qxT_done"], 1)

            def gate_up(i):
                pe.wait_ge(s["qxT_copied"], i + 1)
                if i >= 1:
                    pe.wait_ge(s["g1_ready"], i)
                else:
                    pe.wait_ge(s["silub_done"], MT)
                for m in range(2):
                    for k in range(2):
                        bank = (pb[k] if m == 0 else sc2[:, k])[:, 0:IH]
                        for c in range(C):
                            last = nc.tensor.matmul(bank, qxT[:, c, :], q1w[:, m, c, k * IH:(k + 1) * IH],
                                                    start=c == 0, stop=c == C - 1)
                last.then_inc(s["gu_done"], 1)

            def inner_transposes(i):
                pe.wait_ge(s["qt_ready"], i + 1)
                if i >= 1:
                    pe.wait_ge(s["qtT_copied"], i)
                else:
                    pe.wait_ge(s["hT_copied"], MT)
                for c in range(NI):
                    last = nc.tensor.transpose(pt2[0:IQ, 0, :].bitcast(BF16)[:, c * P:(c + 1) * P], qt[:, c * IQ:(c + 1) * IQ], identb[:, :])
                last.then_inc(s["qtT_done"], 1)

            def down_quantised(i):
                pe.wait_ge(s["qtT_copied"], i + 1)
                if i >= 1:
                    pe.wait_ge(s["yo_read"], i)
                else:
                    pe.wait_ge(s["y_copied"], MT)
                for c in range(NI):
                    last = nc.tensor.matmul(pw[:, 0:D], qtT[0:IQ, c, :], q1d[0:IQ, c, :], start=c == 0, stop=c == NI - 1)
                last.then_inc(s["dn_done"], 1)

            pe.wait_ge(s["rq_copied"], 3)
            for i in range(NT + 1):
                if i < NT:
                    quantised_transposes(i)
                    gate_up(i)
                if i >= 1:
                    inner_transposes(i - 1)
                    down_quantised(i - 1)

        @block.scalar
        def _(act):
            links = [0]

            def link(ins):
                links[0] += 1
                ins.then_inc(s["act_link"], 1)
                act.wait_ge(s["act_link"], links[0])

            for b in range(B):
                act.wait_ge(s_x[b], 16)
                nc.scalar.activation(sg[:, b, :], x_in[:, b, :], ACT.Sigmoid).then_inc(s["sg_exp"], 1)
            act.wait_ge(s["tfsum"], 1)
            nc.scalar.activation(tf[:, 1, :], tf[:, 0, :], ACT.Exp, scale=-1.0).then_inc(s["tf_exp"], 1)
            link(nc.scalar.activation(dec[:, 0, :, :], wu[:, 0:4:2, :], ACT.Exp))
            nc.scalar.activation(dec[:, 1, :, :], dec[:, 0, :, :], ACT.Exp, scale=-1.0).then_inc(s["dec_exp"], 1)
            for b in range(B):
                act.wait_ge(s["fT_done"], b + 1)
                nc.scalar.copy(fT[:, b, :], pb[b % 2][:, :]).then_inc(s["fT_copied"], 1)

            def exponentials_of_batch(n, parity, bufs):
                E, U = bufs[0][:, parity], bufs[1][:, parity]
                if isinstance(n, int) and n < B:
                    act.wait_ge(s["kmin_ready"], n + 1)
                act.wait_ge(s["ku_ready"], n + 1)
                nc.scalar.activation(E[:, 1, :], E[:, 1, :], ACT.Exp)
                nc.scalar.activation(U[:, 1, :], U[:, 1, :], ACT.Exp).then_inc(s["uexp_ready"], 1)

            exponentials_of_batch(0, 0, cond_buf[0])
            exponentials_of_batch(1, 1, cond_buf[0])
            act.wait_ge(s["qkv_in"], 48)
            for c in range(C):
                for q in range(2):
                    nc.scalar.activation(qkv16[:, 0, c, 0:20 * HD].rearrange("p (h q i) -> p h q i", q=2, i=HD // 2)[:, :, q, :],
                                         stage[:, c, q:20 * HD:2].rearrange("p (h i) -> p h i", i=HD // 2), ACT.Copy, scale=WS)
            nc.scalar.activation(qkv16[:, 0, :, 20 * HD:], stage[:, :, 20 * HD:], ACT.Copy, scale=WS).then_inc(s["qkvhi_done"], 1)

            def squares(b):
                act.wait_ge(s["x0_ready"], b + 1)
                for i in range(TT):
                    last = nc.scalar.activation(t1[:, b % 2, i * D:(i + 1) * D], x0[:, b * TT + i, :], ACT.Square,
                                                accum_out=ssq[:, 0, b * TT + i:b * TT + i + 1])
                last.then_inc(s["ssq_ready"], 1)

            def hidden_high(b):
                act.wait_ge(s["hTp_done"], b + 1)
                for c in range(C):
                    last = nc.scalar.activation(hT[:, 0, c, b * S:(b + 1) * S], pt2[:, b % 2, c * S:(c + 1) * S],
                                                ACT.Copy, scale=wln[:, c:c + 1])
                last.then_inc(s["hi_done"], 1)

            act.wait_ge(s["par_in"], 16 * 8)
            for b in range(B):
                squares(b)
                if b >= 1:
                    hidden_high(b - 1)
                if b + 2 < B:
                    exponentials_of_batch(b + 2, b % 2, cond_buf[0])
            hidden_high(B - 1)
            act.wait_ge(s["wo_in"], 16)
            nc.scalar.activation(wo16[:, 0], stage_wo, ACT.Copy, scale=WS).then_inc(s["wohi_done"], 1)

            HH = HD // 2

            def swap_halves(n, parity):
                act.wait_ge(s["rope_done"], n + 1)
                if not isinstance(n, int) or n >= 2:
                    act.wait_ge(s["radd_done"], n - 1)
                nc.scalar.copy(t2[0:HH, parity, :], pb[parity][HH:HD, :])
                nc.scalar.copy(t2[HH:HD, parity, :], pb[parity][0:HH, :]).then_inc(s["swap_done"], 1)

            def exponentials(u, parity):
                act.wait_ge(s["nmax_done"], u + 1)
                for b in range(2):
                    for qb in range(2):
                        o, w = (0, P) if qb == 0 else (P, 2 * P)
                        k = 2 * b + qb
                        last = nc.scalar.activation(pr[:, parity, b, o:o + w], pr[:, parity, b, o:o + w], ACT.Exp,
                                                    bias=mx[:, parity, 1, k:k + 1], scale=SCALE,
                                                    accum_out=sums[:, parity, 0, k:k + 1])
                last.then_inc(s["exp_done"], 1)

            def pT_high(u, parity):
                act.wait_ge(s["pT_done"], u + 1)
                if not isinstance(u, int) or u >= 2:
                    act.wait_ge(s["av_done"], u - 1)
                nc.scalar.copy(pT[:, parity, 0], pt2[:, :, 0:BLK]).then_inc(s["pThi_done"], 1)

            def o_high(u):
                act.wait_ge(s["av_done"], u + 1)
                nc.scalar.copy(oT[:, 0, bass.ds(u % H, 1), :].rearrange("p a n -> p (a n)"), po[:, :]).then_inc(s["ohi_done"], 1)

            act.wait_ge(s["zero_out"], 16)
            for n in range(KU):
                swap_halves(n, n % 2)
            for i in range(NT):
                act.wait_ge(s["v_done"], i + 1)
                nc.scalar.copy(v16[:, 0, i, :], (po, pw)[i % 2][:, :]).then_inc(s["vhi_done"], 1)

            def step(u, parity):
                if within(u, 3):
                    exponentials(u - 3, 1 - parity)
                if within(u, 0):
                    swap_halves(KU + u, parity)
                if within(u, 4):
                    pT_high(u - 4, parity)
                if within(u, 5):
                    o_high(u - 5)

            attention_steps(act, step, lambda: act.wait_ge(s["wo_done"], NT // 2))

            act.wait_ge(s["av_done"], QU)
            act.wait_ge(s["olo_done"], QU)

            def squares_of_tile(i):
                act.wait_ge(s["x1a_done"], i + 1)
                nc.scalar.activation(h2[:, i, :], x0[:, i, :], ACT.Square, accum_out=ssq[:, 0, i:i + 1]).then_inc(s["ssq2_ready"], 1)

            def copy_h2T(i):
                act.wait_ge(s["h2T_done"], i + 1)
                if i >= 2:
                    act.wait_ge(s["gate_tile"], i - 1)
                nc.scalar.copy(h2T[:, i % 2, :], pb[i % 2][:, 0:D]).then_inc(s["h2T_copied"], 1)

            for tiles, copies in ((range(4), (0, 1)), ((4,), (2, 3)), ((5,), (4,)), ((6, 7), (5, 6, 7))):
                for i in tiles:
                    squares_of_tile(i)
                for i in copies:
                    copy_h2T(i)
            act.wait_ge(s["d_ready"], 1)
            nc.scalar.activation(gts[:, :, 1], gts[:, :, 0], ACT.Exp).then_inc(s["ge_ready"], 1)

            def ratio_piece(b, i, bank):
                last = nc.scalar.copy(ratio1[:, bass.ds(b * TT + i, 1), :], bank[:, D:].rearrange("p (a n) -> p a n", a=1))
                if i == TT - 1:
                    last.then_inc(s["ratio1_copied"], 1)

            def weight_piece(m, kc, half, bank):
                w = INTER // 2
                last = nc.scalar.copy(q1w[:, bass.ds(m, 1), kc, half * w:(half + 1) * w],
                                      bank[:, D:D + w // 2].bitcast(BF16).rearrange("p (a n) -> p a n", a=1))
                if (kc, half) == (1, 1):
                    last.then_inc(s["rq_copied"], 1)

            def down_piece(hc, half, bank):
                last = nc.scalar.copy(q1d[0:IQ, half * (NI // 2):(half + 1) * (NI // 2), hc * P:(hc + 1) * P],
                                      bank[0:IQ, D:].bitcast(BF16).rearrange("p (c n) -> p c n", c=NI // 2))
                if (hc, half) == (1, 1):
                    last.then_inc(s["rq_copied"], 1)

            def load_rows(n, parity):
                act.dma_start(xs[:, parity, :], xs_dram[bass.ds(n * P, P), :]).then_inc(s_xs[parity], 16)

            def copy_xT(n, parity, piece=None):
                act.wait_ge(s["xT_done"], n + 1)
                if piece:
                    piece(po)
                if not isinstance(n, int) or n >= 2:
                    act.wait_ge(s["upb_done"], n - 1)
                nc.scalar.copy(xsT[:, parity, :], po[:, 0:D]).then_inc(s["xT_copied"], 1)

            act.wait_ge(s["scatter_out"], 16 * 2 * NT)
            load_rows(0, 0)
            load_rows(1, 1)
            copy_xT(0, 0)

            for k in range(2):
                act.sem_inc(s_y[k], 16)

            def tile_step(n, parity, pieces=(None, None), place=None):
                fixed = isinstance(n, int)
                if place and place[1] in (0, 2):
                    k = place[1] // 2
                    exponentials_of_batch(place[0] * 2 + (B + k), k, cond_buf[1])
                if not fixed or n < MT:
                    act.wait_ge(s["upa_done"], n + 1)
                    if not fixed or n >= 1:
                        act.wait_ge(s["silub_done"], n)
                    nc.scalar.activation(eh[:, 0:FA], pb[0][:, :], ACT.Silu).then_inc(s["expa_done"], 1)
                if not fixed or n >= 1:
                    act.wait_ge(s["hT_done"], n)
                    if not fixed or n >= 2:
                        act.wait_ge(s["down_done"], n)
                    nc.scalar.copy(hhT[:, 0:4, :], pt2[:, 0, :].rearrange("p (c n) -> p c n", c=4))
                    nc.scalar.copy(hhT[:, 4:FC, :], pt2[:, 1, 0:FB].rearrange("p (c n) -> p c n", c=FC - 4)).then_inc(s["hT_copied"], 1)
                if not fixed or n + 1 < MT:
                    copy_xT(n + 1, 1 - parity, pieces[0])
                if not fixed or n + 2 < MT:
                    load_rows(n + 2, parity)
                if not fixed or n < MT:
                    act.wait_ge(s["upb_done"], n + 1)
                    nc.scalar.activation(eh[:, FA:FF], sc2[:, 0, 0:FB], ACT.Silu).then_inc(s["expb_done"], 1)
                if not fixed or n >= 1:
                    act.wait_ge(s["down_done"], n + 1)
                    if pieces[1]:
                        pieces[1](pw)
                    act.wait_ge(s_y[1 - parity], 16 * ((n + 1) // 2))
                    nc.scalar.copy(ysb[:, 1 - parity, :], pw[:, 0:D]).then_inc(s["y_copied"], 1)
                    act.wait_ge(s["y_copied"], n)
                    act.dma_start(ys_dram[bass.ds((n - 1) * P, P), :], ysb[:, 1 - parity, :]).then_inc(s_y[1 - parity], 16)

            expert_steps(act, tile_step, ratio_piece, weight_piece, down_piece)

            for i in range(NT + 1):
                if i < NT:
                    act.wait_ge(s["x1_ready"], i + 1)
                    nc.scalar.activation(xq[:, 0, :], x1[:, i, :], ACT.Sigmoid).then_inc(s["sgx_ready"], 1)
                    act.wait_ge(s["qxT_done"], i + 1)
                    if i >= 1:
                        act.wait_ge(s["gu_done"], i)
                    nc.scalar.copy(qxT[:, :, :], po[:, 0:P].bitcast(BF16).rearrange("p (c n) -> p c n", c=C)).then_inc(s["qxT_copied"], 1)
                if i >= 1:
                    act.wait_ge(s["g1_ready"], i)
                    nc.scalar.activation(gw[:, 2, :], gw[:, 0, :], ACT.Sigmoid, scale=rs[:, 3, i - 1:i]).then_inc(s["ge1_ready"], 1)
                    act.wait_ge(s["qtT_done"], i)
                    if i >= 2:
                        act.wait_ge(s["dn_done"], i - 1)
                    nc.scalar.copy(qtT[0:IQ, :, :], pt2[0:IQ, 0, :].bitcast(BF16).rearrange("p (c n) -> p c n", c=NI)).then_inc(s["qtT_copied"], 1)

        @block.vector
        def _(dve):
            links = [0]
            V = nc.vector

            def link(ins):
                links[0] += 1
                ins.then_inc(s["dve_link"], 1)
                dve.wait_ge(s["dve_link"], links[0])

            dve.wait_ge(s["par_in"], 16 * 8)
            V.tensor_reduce(out=tf[:, 0, :], in_=cond[:, :, :], axis=AX.X, op=ALU.add).then_inc(s["tfsum"], 1)
            dve.wait_ge(s["tf_exp"], 1)
            link(V.tensor_scalar(tf[:, 2, :], tf[:, 1, :], 1.0, None, ALU.add))
            link(V.reciprocal(tf[:, 3, :], tf[:, 2, :]))
            V.tensor_scalar(tf[:, 4, :], tf[:, 3, :], 0.5, 0.5, ALU.mult, ALU.add)
            link(V.tensor_scalar(tf[:, 5, :], tf[:, 3, :], 0.2, 0.8, ALU.mult, ALU.add))
            dve.wait_ge(s["dec_exp"], 1)
            for l in range(2):
                for c in range(C):
                    last = V.tensor_scalar(decay[:, l, c, :], tf[:, 4, :], dec[:, 1, l, c:c + 1], None, ALU.mult)
            link(last)
            for c in range(C):
                V.tensor_copy(cond1[:, :, c], decay[:, 1, c, :])
            V.tensor_copy(cond1[:, :, C], tf[:, 5, :])

            def clamp_keys(b):
                dve.wait_ge(s["fT_copied"], b + 1)
                if b >= 2:
                    dve.wait_ge(s["u_used"], b - 1)
                V.tensor_scalar(cond_buf[0][0][:, b % 2, 1, :], fT[:, b, :], 30.0, None, ALU.min).then_inc(s["kmin_ready"], 1)

            def scans(E, fwd, bwd, decay_of):
                for c in range(C):
                    a = decay_of(c).to_broadcast([P, S])
                    for k in range(2):
                        src = E[:, k, c * S:(c + 1) * S]
                        V.tensor_tensor_scan(out=fwd[:, k, c * S:(c + 1) * S], data0=a, data1=src, initial=0.0,
                                             op0=ALU.mult, op1=ALU.add)
                        last = V.tensor_tensor_scan(out=bwd[:, k, c * S:(c + 1) * S][:, ::-1], data0=a, data1=src[:, ::-1],
                                                    initial=0.0, op0=ALU.mult, op1=ALU.add)
                return last

            def mixing_ratio(b):
                E2, U2, fwd, bwd, rat = cond_buf[0]
                dve.wait_ge(s["u_ready"], b + 1)
                link(scans(E2[:, b % 2], fwd, bwd, lambda c: decay[:, 0, c, b:b + 1]))
                link(V.tensor_tensor(fwd[:, :, :], fwd[:, :, :], bwd[:, :, :], ALU.add))
                V.tensor_tensor(fwd[:, :, :], fwd[:, :, :], U2[:, b % 2], ALU.add).then_inc(s["u_used"], 1)
                dve.wait_ge(s["u_used"], b + 1)
                link(V.tensor_scalar(fwd[:, 1, :], fwd[:, 1, :], 1e-8, None, ALU.max))
                link(V.reciprocal(bwd[:, 1, :], fwd[:, 1, :]))
                if b >= 1:
                    dve.wait_ge(s["rat_done"], b)
                V.scalar_tensor_tensor(rat, fwd[:, 0, :], tf[:, 5, b:b + 1], bwd[:, 1, :], ALU.mult, ALU.mult)\
                    .then_inc(s["ratT_ready"], 1)

            def first_input(b):
                dve.wait_ge(s["sg_exp"], b + 1)
                dve.wait_ge(s["rat_done"], b + 1)
                V.tensor_tensor(x0[:, TT * b:TT * (b + 1), :].rearrange("p i n -> p (i n)"), sc2[:, b % 2, :], sg[:, b, :], ALU.mult)\
                    .then_inc(s["x0_ready"], 1)

            def normalise_rows(b):
                dve.wait_ge(s["rstd_ready"], b + 1)
                if b >= 1:
                    dve.wait_ge(s["hTp_done"], b)
                for i in range(TT):
                    k = b * TT + i
                    last = V.tensor_scalar(xn[:, i * D:(i + 1) * D], x0[:, k, :], ssq[:, 2, k:k + 1], None, ALU.mult)
                last.then_inc(s["xn_ready"], 1)

            def hidden_low(b):
                dve.wait_ge(s["hi_done"], b + 1)
                for c in range(C):
                    last = V.scalar_tensor_tensor(hT[:, 1, c, b * S:(b + 1) * S], pt2[:, b % 2, c * S:(c + 1) * S], wln[:, c:c + 1],
                                                  hT[:, 0, c, b * S:(b + 1) * S], ALU.mult, ALU.subtract)
                last.then_inc(s["hlo_done"], 1)

            clamp_keys(0)
            clamp_keys(1)
            for b in range(B):
                mixing_ratio(b)
                if b + 2 < B:
                    clamp_keys(b + 2)
                if b >= 2:
                    hidden_low(b - 2)
                if b >= 1:
                    normalise_rows(b - 1)
                first_input(b)
            hidden_low(B - 2)
            normalise_rows(B - 1)
            dve.wait_ge(s["qkvhi_done"], 1)
            for c in range(C):
                for q in range(2):
                    def lanes(a):
                        return qkv16[:, a, c, 0:20 * HD].rearrange("p (h q i) -> p h q i", q=2, i=HD // 2)[:, :, q, :]
                    V.scalar_tensor_tensor(lanes(1), stage[:, c, q:20 * HD:2].rearrange("p (h i) -> p h i", i=HD // 2), WS,
                                           lanes(0), ALU.mult, ALU.subtract)
            V.scalar_tensor_tensor(qkv16[:, 1, :, 20 * HD:], stage[:, :, 20 * HD:], WS, qkv16[:, 0, :, 20 * HD:],
                                   ALU.mult, ALU.subtract).then_inc(s["qkvlo_done"], 1)
            hidden_low(B - 1)
            dve.wait_ge(s["wohi_done"], 1)
            V.scalar_tensor_tensor(wo16[:, 1], stage_wo, WS, wo16[:, 0], ALU.mult, ALU.subtract).then_inc(s["wolo_done"], 1)

            def rope(n, parity):
                dve.wait_ge(s["proj_done"], n + 1)
                if not isinstance(n, int) or n >= 2:
                    dve.wait_ge(s["radd_done"], n - 1)
                bank = pb[parity][:, :].rearrange("p (b n) -> p b n", b=2)
                V.tensor_tensor(t1[:, parity, :].rearrange("p (b n) -> p b n", b=2), bank,
                                rope_cos.rearrange("p (a n) -> p a n", a=1).to_broadcast([P, 2, S]), ALU.mult)\
                    .then_inc(s["rope_done"], 1)

            for n in range(KU):
                rope(n, n % 2)
            for i in range(NT):
                dve.wait_ge(s["vhi_done"], i + 1)
                V.tensor_tensor(v16[:, 1, i, :], (po, pw)[i % 2][:, :], v16[:, 0, i, :], ALU.subtract).then_inc(s["vlo_done"], 1)

            def normalise(u, parity):
                dve.wait_ge(s["exp_done"], u + 1)
                V.reciprocal(sums[:, parity, 1, :], sums[:, parity, 0, :]).then_inc(s["recip_done"], 1)
                dve.wait_ge(s["recip_done"], u + 1)
                for b in range(2):
                    for qb in range(2):
                        o, w = (0, P) if qb == 0 else (P, 2 * P)
                        k = 2 * b + qb
                        last = V.tensor_scalar(pr[:, parity, b, o:o + w], pr[:, parity, b, o:o + w], sums[:, parity, 1, k:k + 1],
                                               None, ALU.mult)
                last.then_inc(s["norm_done"], 1)

            def row_max(u, parity):
                dve.wait_ge(s["score_done"], u + 1)
                if not isinstance(u, int) or u >= 2:
                    dve.wait_ge(s["pT_done"], u - 1)
                dve.sem_inc(s["dve_paused"], 1)
                for b in range(2):
                    for qb in range(2):
                        o, w = (0, P) if qb == 0 else (P, 2 * P)
                        k = 2 * b + qb
                        last = V.tensor_tensor_reduce(out=pr[:, parity, b, o:o + w], in0=sc2[:, b, o:o + w], in1=mask[:, o:o + w],
                                                      scale=1.0, scalar=-3e38, op0=ALU.add, op1=ALU.max,
                                                      accum_out=mx[:, parity, 0, k:k + 1])
                last.then_inc(s["max_done"], 1)
                dve.wait_ge(s["max_done"], u + 1)
                V.tensor_scalar(mx[:, parity, 1, :], mx[:, parity, 0, :], -SCALE, None, ALU.mult).then_inc(s["nmax_done"], 1)

            def pT_low(u, parity):
                dve.wait_ge(s["pThi_done"], u + 1)
                V.tensor_tensor(pT[:, parity, 1], pt2[:, :, 0:BLK], pT[:, parity, 0], ALU.subtract).then_inc(s["pTlo_done"], 1)

            def o_low(u):
                dve.wait_ge(s["ohi_done"], u + 1)
                V.tensor_tensor(oT[:, 1, bass.ds(u % H, 1), :].rearrange("p a n -> p (a n)"), po[:, :],
                                oT[:, 0, bass.ds(u % H, 1), :].rearrange("p a n -> p (a n)"), ALU.subtract).then_inc(s["olo_done"], 1)

            def step(u, parity):
                if within(u, 0):
                    rope(KU + u, parity)
                if within(u, 2):
                    row_max(u - 2, parity)
                if within(u, 3):
                    normalise(u - 3, 1 - parity)
                if within(u, 4):
                    pT_low(u - 4, parity)
                if within(u, 5):
                    o_low(u - 5)

            def residual(n):
                dve.wait_ge(s["wo_done"], n + 1)
                V.scalar_tensor_tensor(x0[:, n, :], pw[:, 0:D], 1.0 / (WS * WS), x0[:, n, :],
                                       ALU.mult, ALU.add).then_inc(s["x1a_done"], 1)

            attention_steps(dve, step, lambda: [residual(n) for n in range(4)])

            def second_norm(i):
                dve.wait_ge(s["rstd2_ready"], i + 1)
                V.scalar_tensor_tensor(h2[:, i, :], x0[:, i, :], ssq[:, 2, i:i + 1], ffln[:, :], ALU.mult, ALU.mult)\
                    .then_inc(s["h2_ready"], 1)

            for n, norms in ((4, (0, 1)), (5, (2, 3)), (6, (4,)), (7, (5,))):
                for i in norms:
                    second_norm(i)
                residual(n)
            second_norm(6)
            second_norm(7)
            dve.wait_ge(s["gate_tile"], NT)
            link(V.tensor_copy(lg, po[:, 0:NT * NE]))
            for i in range(NT):
                last = V.max(m8[:, i * NE:(i + 1) * NE], lg[:, i * NE:(i + 1) * NE])
            link(last)
            for i in range(NT):
                last = V.max_index(i8[:, i * NE:(i + 1) * NE], m8[:, i * NE:(i + 1) * NE], lg[:, i * NE:(i + 1) * NE])
            link(last)

            def te(x):
                return x.rearrange("p (i e) -> p i e", e=NE)

            m8v = te(m8)
            idfv = idf.rearrange("p (i k) -> p i k", k=2)
            iota = iota_e.rearrange("p (a e) -> p a e", a=1).to_broadcast([P, NT, NE])
            link(V.tensor_copy(idfv, i8.rearrange("p (i e) -> p i e", e=NE)[:, :, 0:2]))
            V.tensor_tensor(te(M1), iota, idfv[:, :, 0:1].to_broadcast([P, NT, NE]), ALU.is_equal)
            V.tensor_tensor(te(M2), iota, idfv[:, :, 1:2].to_broadcast([P, NT, NE]), ALU.is_equal)
            link(V.tensor_tensor(gts[:, :, 0], m8v[:, :, 1], m8v[:, :, 0], ALU.subtract))
            V.tensor_tensor(MK, M1, M2, ALU.add).then_inc(s["mk_ready"], 1)
            V.memset(car[:, 0:NE], 0.0).then_inc(s["d_ready"], 1)
            dve.wait_ge(s["ge_ready"], 1)
            link(V.tensor_scalar(gts[:, :, 2], gts[:, :, 1], 1.0, None, ALU.add))
            link(V.reciprocal(gts[:, :, 3], gts[:, :, 2]))
            link(V.tensor_tensor(gts[:, :, 4], gts[:, :, 3], gts[:, :, 1], ALU.mult))
            dve.wait_ge(s["rank_done"], 1)
            link(V.tensor_copy(tots, po[:, 256:256 + NT * NE]))
            for i in range(NT):
                link(V.tensor_tensor(car[:, (i + 1) * NE:(i + 2) * NE], car[:, i * NE:(i + 1) * NE], tots[:, i * NE:(i + 1) * NE], ALU.add))
            link(V.tensor_scalar(exi[:, 0, :], car[:, NT * NE:], float(P - 1), None, ALU.add))
            link(V.tensor_scalar(exi[:, 1, :], exi[:, 0, :], 7, None, ALU.logical_shift_right))
            link(V.tensor_copy(ex8[:, 1, :], exi[:, 1, :]))
            link(V.tensor_tensor_scan(out=ex8[:, 2, :], data0=ones[:, 0:NE], data1=ex8[:, 1, :], initial=0.0, op0=ALU.mult, op1=ALU.add))
            link(V.tensor_tensor(ex8[:, 3, :], ex8[:, 2, :], ex8[:, 1, :], ALU.subtract))
            link(V.tensor_scalar(ex8[:, 4, :], ex8[:, 3, :], float(P), None, ALU.mult))
            link(V.tensor_tensor(pos, po[:, 128:128 + NT * NE], car[:, 0:NT * NE], ALU.add))
            link(V.tensor_tensor(te(pos), te(pos), ex8[:, 4:5, :].to_broadcast([P, NT, NE]), ALU.add))
            for k, M in enumerate((M1, M2)):
                link(V.tensor_tensor(prod, pos, M, ALU.mult))
                link(V.tensor_reduce(out=slotf[:, k, :], in_=te(prod), axis=AX.X, op=ALU.add))
            V.tensor_copy(sloti[:, :, :], slotf[:, :, :]).then_inc(s["slots_ready"], 1)
            cmpv = cmp[:, :].rearrange("p (t e) -> p t e", e=NE)
            link(V.tensor_tensor(cmpv, ex8[:, 2:3, :].to_broadcast([P, MT, NE]),
                                 iota_t.rearrange("p (t a) -> p t a", a=1).to_broadcast([P, MT, NE]), ALU.is_le))
            link(V.tensor_reduce(out=tmap[:, 0, :], in_=cmpv, axis=AX.X, op=ALU.add))
            link(V.tensor_scalar(tmi[0:1, :], tmap[0:1, 0, :], float(NE - 1), None, ALU.min))
            V.tensor_scalar(endi[0:1, :], ex8[0:1, 2, :], 1.0, None, ALU.add).then_inc(s["tmap_ready"], 1)

            V.tensor_copy(identb[:, :], ident).then_inc(s["identb_ready"], 1)

            def round_e4m3(link, dst, v, g):
                link(V.tensor_scalar(g.bitcast(I32), v.bitcast(I32), 0x7F800000, None, ALU.bitwise_and))
                link(V.tensor_scalar(g, g, FP8_LEAST, MAGIC, ALU.max, ALU.mult))
                link(V.tensor_tensor(v, v, g, ALU.add))
                return V.tensor_tensor(dst, v, g, ALU.subtract)

            def recurrence_pieces(b, parity, link):
                E2, U2, fwd, bwd, rat = cond_buf[1]
                n = B + b

                def recur():
                    link(V.tensor_copy(cond1b[:, parity, :], cond1[:, bass.ds(b, 1), :].rearrange("p a n -> p (a n)")))
                    dve.wait_ge(s["u_ready"], n + 1)
                    dve.sem_inc(s["dve_paused"], 1)
                    link(scans(E2[:, parity], fwd, bwd, lambda c: cond1b[:, parity, c:c + 1]))

                def add():
                    link(V.tensor_tensor(fwd[:, :, :], fwd[:, :, :], bwd[:, :, :], ALU.add))
                    V.tensor_tensor(fwd[:, :, :], fwd[:, :, :], U2[:, parity], ALU.add).then_inc(s["u_used"], 1)
                    dve.wait_ge(s["u_used"], n + 1)
                    link(V.tensor_scalar(fwd[:, 1, :], fwd[:, 1, :], 1e-8, None, ALU.max))

                def divide():
                    link(V.reciprocal(bwd[:, 1, :], fwd[:, 1, :]))
                    dve.wait_ge(s["rat_done"], n)
                    V.scalar_tensor_tensor(rat, fwd[:, 0, :], cond1b[:, parity, C:C + 1], bwd[:, 1, :], ALU.mult, ALU.mult)\
                        .then_inc(s["ratT_ready"], 1)

                return [recur, add, divide]

            def weight_pieces(m, link):
                down = isinstance(m, int)
                q, k, n = (P, C, INTER) if down else (IQ, NI, D)
                r, g = rows[0:q, 0:k * n], grid[0:q, 0:k * n]
                r3 = r.rearrange("p (k n) -> p k n", k=k)
                wm, wi = (w[0:q, 0:k] for w in (wmax, winv))

                def scale():
                    dve.wait_ge(s["rows_in"], 32 * NI + 16 if down else m * (16 * NI) + 16 * NI)
                    link(V.tensor_reduce(out=wm, in_=r3, axis=AX.X, op=ALU.max, apply_absolute_value=True))
                    link(V.reciprocal(wi, wm))
                    ws = wscale[0:q, 2, 0:k] if down else wscale[0:q, bass.ds(m, 1), 0:k].rearrange("p a k -> p (a k)")
                    V.tensor_scalar(ws, wm, 1.0 / FP8_MAX, None, ALU.mult).then_inc(s["wscale_ready"], 1)
                    link(V.tensor_scalar(wi, wi, FP8_MAX, None, ALU.mult))
                    link(V.tensor_tensor(r3, r3, wi.rearrange("p (k a) -> p k a", a=1).to_broadcast([q, k, n]), ALU.mult))

                def grids():
                    link(V.tensor_scalar(g.bitcast(I32), r.bitcast(I32), 0x7F800000, None, ALU.bitwise_and))
                    link(V.tensor_scalar(g, g, FP8_LEAST, MAGIC, ALU.max, ALU.mult))

                def round_up():
                    link(V.tensor_tensor(r, r, g, ALU.add))

                def round_down():
                    if down:
                        dve.wait_ge(s["rqT_done"], 2)
                    V.tensor_tensor(rq[0:q, 0:k * n], r, g, ALU.subtract).then_inc(s["rq_ready"], 1)

                return [scale, grids, round_up, round_down]

            def silu(n, part):
                lo, hi = (0, FA) if part == 0 else (FA, FF)
                b = pb[1][:, 0:FA] if part == 0 else sc2[:, 1, 0:FB]
                done = s["silua_done" if part == 0 else "silub_done"]
                dve.wait_ge(s["expa_done" if part == 0 else "expb_done"], n + 1)
                if part == 0 and (not isinstance(n, int) or n >= 1):
                    dve.wait_ge(s["hT_done"], n)
                V.tensor_tensor(hh[:, lo:hi], eh[:, lo:hi], b, ALU.mult).then_inc(done, 1)

            def tile(n, pieces=()):
                for part in range(2):
                    silu(n, part)
                    if part < len(pieces) and pieces[part]:
                        pieces[part]()

            tile(0)
            LINKS = 17
            with dve.Fori(0, 2) as i:
                round_links = [0]

                def round_link(ins):
                    round_links[0] += 1
                    ins.then_inc(s["side_link"], 1)
                    dve.wait_ge(s["side_link"], i * LINKS + round_links[0])

                w = weight_pieces(i, round_link)
                r0 = recurrence_pieces(i * 2, 0, round_link)
                r1 = recurrence_pieces(i * 2 + 1, 1, round_link)
                order = w + r0 + r1
                for k in range(ROUND):
                    tile(i * ROUND + (k + 1), order[2 * k:2 * k + 2])
                assert round_links[0] == LINKS, round_links
            w = weight_pieces(2, link)
            tile(2 * ROUND + 1, w[0:2])
            tile(2 * ROUND + 2, w[2:4])
            with dve.Fori(2 * ROUND + 3, MT) as n:
                tile(n)

            def mixed_rows(i):
                k = i % 2
                if i == 0:
                    dve.wait_ge(s["hT_done"], MT)
                    dve.wait_ge(s["rat_done"], 2 * B)
                dve.wait_ge(s_g[k], 32 * (i // 2 + 1))
                r = xq
                link(V.scalar_tensor_tensor(x1[:, i, :], y1[:, k, :], gts[:, i, 3:4], x0[:, i, :], ALU.mult, ALU.add))
                link(V.scalar_tensor_tensor(x1[:, i, :], y2[:, k, :], gts[:, i, 4:5], x1[:, i, :], ALU.mult, ALU.add))
                V.tensor_tensor(x1[:, i, :], x1[:, i, :], x_in[:, i // TT, (i % TT) * D:(i % TT + 1) * D], ALU.add).then_inc(s["x1_ready"], 1)
                dve.wait_ge(s["sgx_ready"], i + 1)
                if i == 0:
                    dve.wait_ge(s["ratio1_copied"], B)
                    dve.wait_ge(s["scale_in"], 16)
                link(V.tensor_tensor(r[:, 2, :], r[:, 0, :], ratio1[:, i, :], ALU.mult))
                link(V.tensor_reduce(out=rs[:, 0, i:i + 1], in_=r[:, 2, :], axis=AX.X, op=ALU.max, apply_absolute_value=True))
                link(V.reciprocal(rs[:, 1, i:i + 1], rs[:, 0, i:i + 1]))
                V.tensor_scalar(rs[:, 3, i:i + 1], rs[:, 0, i:i + 1], 1.0 / FP8_MAX, None, ALU.mult)
                link(V.tensor_scalar(rs[:, 2, i:i + 1], rs[:, 1, i:i + 1], FP8_MAX, None, ALU.mult))
                link(V.tensor_tensor(rs[:, 5, i:i + 1], rs[:, 3, i:i + 1], rs[:, 3, i:i + 1], ALU.mult))
                link(V.tensor_scalar(r[:, 3, :], r[:, 2, :], rs[:, 2, i:i + 1], None, ALU.mult))
                if i >= 1:
                    dve.wait_ge(s["qxT_done"], i)
                round_e4m3(link, qx[:, :], r[:, 3, :], r[:, 4, :]).then_inc(s["qx_ready"], 1)

            def inner_rows(i):
                dve.wait_ge(s["gu_done"], i + 1)
                def halves(x):
                    return x.rearrange("p (k n) -> p k n", k=2)
                for k in range(2):
                    V.tensor_tensor(gw[:, 0, k * IH:(k + 1) * IH], pb[k][:, 0:IH], srow[:, k * IH:(k + 1) * IH], ALU.mult)
                V.tensor_tensor(halves(gw[:, 1, :]), sc2[:, :, 0:IH], halves(srow[:, INTER:2 * INTER]), ALU.mult).then_inc(s["g1_ready"], 1)
                dve.wait_ge(s["ge1_ready"], i + 1)
                link(V.tensor_tensor(gw[:, 3, :], gw[:, 0, :], gw[:, 2, :], ALU.mult))
                link(V.scalar_tensor_tensor(gw[:, 3, :], gw[:, 3, :], rs[:, 5, i:i + 1], gw[:, 1, :], ALU.mult, ALU.mult))
                link(V.tensor_reduce(out=rs[:, 6, i:i + 1], in_=gw[:, 3, :], axis=AX.X, op=ALU.max, apply_absolute_value=True))
                link(V.reciprocal(rs[:, 7, i:i + 1], rs[:, 6, i:i + 1]))
                V.tensor_scalar(rs[:, 9, i:i + 1], rs[:, 6, i:i + 1], 1.0 / FP8_MAX, None, ALU.mult)
                link(V.tensor_scalar(rs[:, 8, i:i + 1], rs[:, 7, i:i + 1], FP8_MAX, None, ALU.mult))
                link(V.tensor_scalar(gw[:, 3, :], gw[:, 3, :], rs[:, 8, i:i + 1], None, ALU.mult))
                if i >= 1:
                    dve.wait_ge(s["qtT_done"], i)
                round_e4m3(link, qt[:, :], gw[:, 3, :], gw[:, 4, :]).then_inc(s["qt_ready"], 1)

            def output_rows(i):
                k = i % 2
                dve.wait_ge(s["dn_done"], i + 1)
                if i >= 2:
                    dve.wait_ge(s_o[k], 16 * (i // 2))
                V.scalar_tensor_tensor(yo[:, k, :], pw[:, 0:D], rs[:, 9, i:i + 1], srow[:, 2 * INTER:], ALU.mult, ALU.mult)\
                    .then_inc(s["yo_read"], 1)
                dve.wait_ge(s["yo_read"], i + 1)
                V.tensor_tensor(yo[:, k, :], yo[:, k, :], x1[:, i, :], ALU.add).then_inc(s["yo_ready"], 1)

            for i in range(NT + 2):
                if i < NT:
                    mixed_rows(i)
                if 1 <= i <= NT:
                    inner_rows(i - 1)
                if i >= 2:
                    output_rows(i - 2)

        @block.gpsimd
        def _(pool):
            G = nc.gpsimd
            links = [0]

            def link(ins):
                links[0] += 1
                ins.then_inc(s["pool_link"], 1)
                pool.wait_ge(s["pool_link"], links[0])

            G.memset(t2[:, 0, :], 0.0).then_inc(s["ms_done"], 1)
            link(G.memset(nhalf[:, :], -0.5))
            pool.wait_ge(s["par_in"], 16 * 8)

            def rstd(first, count, done):
                link(G.tensor_scalar(ssq[:, 1, first:first + count], ssq[:, 0, first:first + count], 1.0 / D, EPS, ALU.mult, ALU.add))
                G.tensor_tensor(ssq[:, 2, first:first + count], ssq[:, 1, first:first + count], nhalf[:, 0:count], ALU.pow).then_inc(done, 1)

            def recurrence_inputs(l, b):
                n = l * B + b
                E, U = cond_buf[l][0][:, b % 2], cond_buf[l][1][:, b % 2]
                if l == 0:
                    pool.wait_ge(s["fT_copied"], b + 1)
                if n >= 2:
                    pool.wait_ge(s["u_used"], n - 1)
                if l == 1:
                    G.tensor_scalar(E[:, 1, :], fT[:, b, :], 30.0, None, ALU.min)
                for c in range(C):
                    last = G.tensor_scalar(U[:, 1, c * S:(c + 1) * S], fT[:, b, c * S:(c + 1) * S], wu[:, 2 * l + 1, c:c + 1], 30.0,
                                           ALU.add, ALU.min)
                last.then_inc(s["ku_ready"], 1)
                pool.wait_ge(s["uexp_ready"], n + 1)
                G.tensor_tensor(U[:, 0, :], U[:, 1, :], fT[:, b, :], ALU.mult)
                link(G.tensor_tensor(E[:, 0, :], E[:, 1, :], fT[:, b, :], ALU.mult))
                G.tensor_tensor(U, U, E, ALU.subtract).then_inc(s["u_ready"], 1)

            recurrence_inputs(0, 0)
            for b in range(B):
                if b + 1 < B:
                    recurrence_inputs(0, b + 1)
                pool.wait_ge(s["ssq_ready"], b + 1)
                rstd(TT * b, TT, s["rstd_ready"])

            def rope_sum(n, parity, k):
                pool.wait_ge(s["swap_done"], n + 1)
                G.tensor_tensor(t2[:, parity, :].rearrange("p (b n) -> p b n", b=2), t2[:, parity, :].rearrange("p (b n) -> p b n", b=2),
                                rope_sin.rearrange("p (a n) -> p a n", a=1).to_broadcast([P, 2, S]), ALU.mult).then_inc(s["sin_done"], 1)
                pool.wait_ge(s["sin_done"], n + 1)
                if k is None:
                    if not isinstance(n, int) or n >= KU + 2:
                        pool.wait_ge(s["score_done"], n - KU - 1)
                    dst = qr[:, parity, :]
                else:
                    dst = kT[:, k % KVH, k // KVH * PAIR:(k // KVH + 1) * PAIR]
                G.tensor_tensor(dst, t1[:, parity, :], t2[:, parity, :], ALU.add).then_inc(s["radd_done"], 1)

            for n in range(KU):
                rope_sum(n, n % 2, n)

            def step(u, parity):
                if within(u, 0):
                    rope_sum(KU + u, parity, None)

            attention_steps(pool, step, lambda: None)

            pool.wait_ge(s["av_done"], QU)
            pool.wait_ge(s["didx_in"], 16)

            def gather_rows(name):
                for c in range(NI):
                    G.indirect_dma_start(out=rows[0:IQ, c * D:(c + 1) * D], out_offset=None, in_=t[name],
                                         in_offset=bass.IndirectOffsetOnAxis(ap=didx[:, c:c + 1], axis=0)).then_inc(s["rows_in"], 16)

            for i in range(NT):
                pool.wait_ge(s["ssq2_ready"], i + 1)
                rstd(i, 1, s["rstd2_ready"])
            gather_rows("L1_ffn_w_gate")
            pool.wait_ge(s["slots_ready"], 1)
            pool.wait_ge(s["zero_out"], 16)
            for i in range(NT):
                for k in range(2):
                    G.indirect_dma_start(out=xs_dram[:, :], out_offset=bass.IndirectOffsetOnAxis(ap=sloti[:, k, i:i + 1], axis=0),
                                         in_=h2[:, i, :], in_offset=None).then_inc(s["scatter_out"], 16)
            for b in range(2):
                recurrence_inputs(1, b)

            def send_scales(m):
                q, k, at = (IQ, NI, m * INTER) if m < 2 else (P, C, 2 * INTER)
                pool.wait_ge(s["wscale_ready"], m + 1)
                with nc.allow_non_contiguous_dma(reason="a scale of each partition"):
                    G.dma_start(scale_dram[at:at + q * k].rearrange("(k p) -> p k", p=q), wscale[0:q, m, 0:k]).then_inc(s["scale_out"], 16)

            pool.wait_ge(s["rq_ready"], 1)
            gather_rows("L1_ffn_w_up")
            send_scales(0)
            recurrence_inputs(1, 2)
            recurrence_inputs(1, 3)
            pool.wait_ge(s["rq_ready"], 2)
            G.dma_start(rows[:, 0:C * INTER].rearrange("p (c n) -> p c n", c=C),
                        t["L1_ffn_w_down"].rearrange("(c p) n -> p c n", p=P)).then_inc(s["rows_in"], 16)
            send_scales(1)
            send_scales(2)
            pool.wait_ge(s["scale_out"], 48)
            G.dma_start(srow[:, :], scale_dram.rearrange("(a n) -> a n", a=1).to_broadcast([P, 2 * INTER + D])).then_inc(s["scale_in"], 16)
            pool.wait_ge(s["u_used"], 2 * B)
            pool.wait_ge(s_y[0], 16 * ((MT + 1) // 2 + 1))
            pool.wait_ge(s_y[1], 16 * (MT // 2 + 1))
            for i in range(NT):
                if i >= 2:
                    pool.wait_ge(s["x1_ready"], i - 1)
                for k, y in enumerate((y1, y2)):
                    G.indirect_dma_start(out=y[:, i % 2, :], out_offset=None, in_=ys_dram[:, :],
                                         in_offset=bass.IndirectOffsetOnAxis(ap=sloti[:, k, i:i + 1], axis=0)).then_inc(s_g[i % 2], 16)


INPUTS = ["x", "fside_BxSxS_0", "cond_512", "L0_cond_w", "L0_cond_u", "L0_ffn_ln_w", "L0_ffn_ff_ln_w", "L0_ffn_wq", "L0_ffn_wk",
          "L0_ffn_wv", "L0_ffn_wo", "L0_ffn_gate_w", "L0_ffn_w1", "L0_ffn_w3", "L0_ffn_w2", "L1_cond_w", "L1_cond_u",
          "L1_ffn_w_gate", "L1_ffn_w_up", "L1_ffn_w_down", "L1_ffn_down_reorder_index"]


def kernel(**inputs):
    import concourse.bacc as bacc
    from concourse.bass_utils import run_bass_kernel_spmd as run

    nc = bacc.Bacc("TRN2", target_bir_lowering=False, num_devices=1)
    arrays, t = {}, {}
    for name in INPUTS:
        arrays[f"in_{name}"] = np.ascontiguousarray(inputs[name])
    arrays["in_consts"] = constants()
    for name, a in arrays.items():
        t[name[3:]] = nc.dram_tensor(name, a.shape, mybir.dt.from_np(a.dtype), kind="ExternalInput").ap()
    out = nc.dram_tensor("out_dram", (B, S, D), F32, kind="ExternalOutput").ap()
    build(nc, t, out)
    return run(nc, [arrays], core_ids=[0]).results[0]["out_dram"]
```

```python
import numpy as np
import concourse.bass as bass
from concourse import mybir
from contextlib import ExitStack

F32 = mybir.dt.float32
F16 = mybir.dt.float16
BF16 = mybir.dt.bfloat16
I32 = mybir.dt.int32
U32 = mybir.dt.uint32
ALU = mybir.AluOpType
ACT = mybir.ActivationFunctionType
AX = mybir.AxisListType

P = 128
B, S, D = 4, 256, 256
TT = S // P
NT = B * TT
C = D // P
H, KVH, HD = 16, 4, 128
NE, FF = 8, 896
FC = FF // P
FA, FB = 4 * P, FF - 4 * P
MT = 2 * B * S // P + NE - 1
SLOTS = MT * P
WEXP = C * FF * 2 + FC * D
RING = 3
INTER = 704
IQ = 88
NI = INTER // IQ
IH = INTER // 2
WS = 64.0
EPS = 1e-5
QKV = (H + 2 * KVH) * HD
PAIR = 2 * S
KU = 2 * KVH
QU = 2 * H
ROUND = 8
LAG = 5
SCALE = float(HD) ** -0.5
BLK = 3 * P
FP8_MAX = 448.0
MAGIC = 1.5 * 2.0 ** 20
FP8_LEAST = 2.0 ** -6


def constants():
    pos = np.arange(S, dtype=np.float32)
    inv = np.float32(1e6) ** (-np.arange(0, HD, 2, dtype=np.float32) / np.float32(HD))
    ang = (pos[:, None] * inv[None, :].astype(np.float32)).astype(np.float32)
    cos, sin = np.cos(ang).T, np.sin(ang).T
    rope = np.stack([np.concatenate([cos, cos]), np.concatenate([-sin, sin])], 1) / WS
    diag = np.where(np.arange(P)[None, :] > np.arange(P)[:, None], -1e38, 0.0)
    mask = np.concatenate([diag, np.zeros((P, P)), diag], 1)
    before = (np.arange(P)[:, None] < np.arange(P)[None, :]).astype(np.float32)
    iota = np.tile(np.arange(NE, dtype=np.float32), (P, 1))
    tiles = np.tile(np.arange(MT, dtype=np.float32), (P, 1))
    lane = np.tile(np.arange(P, dtype=np.float32), (P, 1))
    token = np.arange(NT)[None, :] * P + np.arange(P)[:, None]
    consts = np.concatenate([np.eye(P), mask, before, np.ones((P, P)), iota, tiles, lane, token, rope.reshape(P, -1)], 1)
    return np.ascontiguousarray(consts, dtype=np.float32)


def build(nc, t, out):
    ctx = ExitStack()
    with ctx:
        def sb(name, shape, dt=F32):
            return ctx.enter_context(nc.sbuf_tensor(name, shape, dt))

        def sem(name):
            return ctx.enter_context(nc.semaphore(name))

        def cut(region, offset, count, dt=F32):
            v = region[:, offset:offset + count]
            return v if dt == F32 else v.bitcast(dt)

        CN = P + BLK + P + P + NE + MT + P + NT + 2 * S
        con = sb("con", [P, CN])
        ident = con[:, 0:P]
        mask = con[:, P:P + BLK]
        before = con[:, P + BLK:2 * P + BLK]
        ones = con[:, 2 * P + BLK:3 * P + BLK]
        o = 3 * P + BLK
        iota_e = con[:, o:o + NE]
        iota_t = con[:, o + NE:o + NE + MT]
        o += NE + MT
        iota_p = con[:, o:o + P]
        token_id = con[:, o + P:o + P + NT]
        o += P + NT
        rope_cos = con[:, o:o + S]
        rope_sin = con[:, o + S:o + 2 * S]

        stage_words = C * QKV
        wreg = sb("wreg", [P, RING * WEXP + 512])
        stage = cut(wreg, 0, stage_words).rearrange("p (c n) -> p c n", c=C)
        stage_wo = cut(wreg, 0, H * D).rearrange("p (h n) -> p h n", h=H)
        qkv16 = cut(wreg, stage_words, C * QKV, F16).rearrange("p (s c n) -> p s c n", s=2, c=C)
        wo16 = cut(wreg, 2 * stage_words, H * D, F16).rearrange("p (s h n) -> p s h n", s=2, h=H)

        breg = sb("breg", [P, 3 * 2 * PAIR + 2 * 4 * BLK])
        t1, t2, qr = (cut(breg, k * 2 * PAIR, 2 * PAIR).rearrange("p (k n) -> p k n", k=2) for k in range(3))
        pr = cut(breg, 6 * PAIR, 4 * BLK).rearrange("p (k b n) -> p k b n", k=2, b=2)
        pT = cut(breg, 6 * PAIR + 4 * BLK, 4 * BLK, F16).rearrange("p (k s b n) -> p k s b n", k=2, s=2, b=2)
        areg = sb("areg", [P, 4096 + 4096 + 2048 + 8192])
        kT = cut(areg, 0, 4096).rearrange("p (h n) -> p h n", h=KVH)
        v16 = cut(areg, 4096, 4096, F16).rearrange("p (s i n) -> p s i n", s=2, i=NT)
        hT = cut(areg, 8192, 2048, F16).rearrange("p (s c n) -> p s c n", s=2, c=C)
        oT = cut(areg, 10240, 8192, F16).rearrange("p (s h n) -> p s h n", s=2, h=H)
        f_tok = cut(areg, 0, 2048).rearrange("p (b i n) -> p b i n", b=B, i=TT)
        xn = cut(areg, 2048, 512)
        sg = cut(areg, 2560, 2048).rearrange("p (b n) -> p b n", b=B)

        def two_rows(offset, sets=1):
            v = cut(areg, offset, sets * 1024)
            return v.rearrange("p (q k n) -> p q k n", q=sets, k=2) if sets > 1 else v.rearrange("p (k n) -> p k n", k=2)

        def recurrence_buffers(base):
            return (two_rows(base, 2), two_rows(base + 2048, 2), two_rows(base + 4096), two_rows(base + 5120),
                    cut(areg, base + 6144, 512))

        cond_buf = (recurrence_buffers(10240), recurrence_buffers(6912))
        x_in = sb("x_in", [P, B, TT * D])
        xs = [cut(areg, at, D) for at in (0, D, 13568, 13568 + D)]
        xsT = cut(areg, 512, 2 * D).rearrange("p (k n) -> p k n", k=2)
        silu_out = cut(areg, 1024, FF)
        hh = cut(areg, 1920, FF)
        hhT = cut(areg, 2816, FF, F16).rearrange("p (s c n) -> p s c n", s=2, c=FC)
        w2s = [[cut(region, at, FC * D // 2, F16).rearrange("p (c n) -> p c n", c=FC) for region, at in parts]
               for parts in (((areg, 4224), (areg, 5120)), ((areg, 6016), (breg, 5120)))]
        ysb = cut(areg, 3712, 2 * D).rearrange("p (k n) -> p k n", k=2)
        h2 = cut(areg, 4224, NT * D).rearrange("p (i n) -> p i n", i=NT)
        h2T = cut(areg, 6272, 2 * D).rearrange("p (k n) -> p k n", k=2)
        y12 = cut(areg, 0, 2 * NT * D).rearrange("p (k i n) -> p k i n", k=2, i=NT)
        qx = cut(areg, 4224, 2 * D, BF16).rearrange("p (k i n) -> p k i n", k=2, i=2)
        qxT = cut(areg, 4736, D // 2, BF16).rearrange("p (c n) -> p c n", c=C)
        qt = cut(areg, 4864, INTER // 2, BF16)
        qtT = cut(areg, 5216, NI * P // 2, BF16).rearrange("p (c n) -> p c n", c=NI)
        yo = cut(areg, 5728, 2 * D).rearrange("p (k n) -> p k n", k=2)
        xsig, xmix, xval, xgrid = (cut(breg, k * 2 * D, 2 * D) for k in range(4))
        gate, gsig, tval, tscaled, tgrid, gprod0, gprod1 = (cut(areg, 8832 + k * INTER, INTER) for k in range(7))
        upv0, upv1 = (cut(breg, 2048 + k * INTER, INTER) for k in range(2))
        gprods, upvs = (gprod0, gprod1), (upv0, upv1)

        x0 = sb("x0", [P, NT, D])
        ratio1 = sb("ratio1", [P, NT, D])
        fT = ratio1[:, :, :].rearrange("p (b i) n -> p b (i n)", b=B)
        x1 = x0
        wln = sb("wln", [P, C])
        ffln = sb("ffln", [P, D])
        wu = sb("wu", [P, 4, C])
        cond = sb("cond", [P, B, 64])
        tf = sb("tf", [P, 6, B])
        dec = sb("dec", [P, 2, 2, C])
        decay = sb("decay", [P, 2, C, B])
        gate_w = sb("gate_w", [P, C, NE])
        cond1 = sb("cond1", [P, B, C + 1])
        cond1b = sb("cond1b", [P, 2, C + 1])

        mx = sb("mx", [P, 2, 2, 4])
        sums = sb("sums", [P, 2, 2, 4])
        nhalf = sb("nhalf", [P, 4])
        ssq = sb("ssq", [P, 3, NT])

        srow = cut(areg, 14240, 2 * INTER + D)
        q1w = cut(areg, 15904, C * INTER, BF16).rearrange("p (m c n) -> p m c n", m=2, c=C)
        q1d = cut(areg, 17312, NI * D // 2, BF16).rearrange("p (c n) -> p c n", c=NI)
        hot_place = cut(breg, 2048, NT * P, F16).rearrange("p (k n) -> p k n", n=P)
        hot_tile = cut(breg, 4096, NT * MT, F16).rearrange("p (k n) -> p k n", n=MT)
        rows = cut(breg, 0, 2048)
        grid = cut(breg, 2048, 2048)
        rq = cut(breg, 4096, 1024, BF16)
        wmax = sb("wmax", [P, NI])
        winv = sb("winv", [P, NI])
        wscale = sb("wscale", [P, 3, NI])
        didx = sb("didx", [IQ, NI], I32)

        pb = [ctx.enter_context(nc.psum_tensor(f"pb{i}", [P, 512], F32)) for i in range(2)]
        sc2 = ctx.enter_context(nc.psum_tensor("sc2", [P, 2, 512], F32))
        pt2 = ctx.enter_context(nc.psum_tensor("pt2", [P, 2, 512], F32))
        po = ctx.enter_context(nc.psum_tensor("po", [P, 512], F32))
        pw = ctx.enter_context(nc.psum_tensor("pw", [P, 512], F32))

        rt = sb("rt", [P, 14, NT * NE])
        lg, M1, M2, MK, tots, pos, prod = (rt[:, k, :] for k in range(7))
        m8 = rt[:, 7, :]
        i8 = rt[:, 8, :].bitcast(U32)
        car = rt[:, 9:11, :].rearrange("p a n -> p (a n)")[:, 0:(NT + 1) * NE]
        idf = rt[:, 11, 0:2 * NT]
        gts = rt[:, 12, :].rearrange("p (k n) -> p k n", n=NT)
        ex8 = rt[:, 13, :].rearrange("p (k n) -> p k n", n=NE)
        exi = sb("exi", [P, 2, NE], I32)
        slotf = sb("slotf", [P, 2, NT])
        sloti = sb("sloti", [P, 2, NT], I32)
        cmp = sb("cmp", [P, MT * NE])
        tmap = sb("tmap", [P, 1, MT])
        tmi = sb("tmi", [1, MT], I32)
        endi = sb("endi", [1, NE], I32)
        identb = sb("identb", [P, P], BF16)
        rs = sb("rs", [P, 10, NT])

        place = sb("place", [P, 2, 2 * NT], I32)
        placef = sb("placef", [P, 2, 2 * NT])
        row_ids = sb("row_ids", [P, MT], I32)
        h2_dram = nc.dram_tensor("h2_dram", (NT * P, D), F32).ap()
        scale_dram = nc.dram_tensor("scale_dram", (2 * INTER + D,), F32).ap()
        ys_dram = nc.dram_tensor("ys_dram", (SLOTS, D), F32).ap()

        names = (
            "ident_in con_in par_in norm_in qkv_in wo_in didx_in rows_in h2_out scale_out scale_in "
            "act_link dve_link pool_link side_link dve_paused "
            "fT_done fT_copied kmin_ready ek_ready e_ready tfsum tf_exp dec_exp sg_exp ku_ready uexp_ready u_ready u_used "
            "ratT_ready rat_done x0_ready ssq_ready rstd_ready xn_ready hTp_done hi_done hlo_done "
            "qkvhi_done qkvlo_done wohi_done wolo_done proj_done rope_done swap_done sin_done radd_done v_done vhi_done vlo_done "
            "score_done max_done nmax_done exp_done recip_done norm_done norm2_done pT_done pThi_done pTlo_done "
            "av_done ohi_done olo_done wo_done x1a_done "
            "ssq2_ready rstd2_ready h2_ready h2T_done h2T_copied gate_tile d_ready ge_ready mk_ready rank_done tmap_ready "
            "hot_ready ids_done ids_ready identb_ready "
            "rq_ready rqT_done rq_copied ratio1_copied wscale_ready xsum_ready "
            "w_ready xT_done xT_copied upa_done upb_done silu_a_done silu_b_done inner_a_done inner_b_done "
            "hT_done hT_copied hTlo_done w2hi_done w2lo_done down_done y_copied "
            "x1_ready sgx_ready qx_ready qxT_done qxT_copied gatep_done upp_done gate_ready gsig_ready up_ready p_ready "
            "inv_ready scaled_ready qt_ready qtT_done qtT_copied dn_done yo_read yo_ready").split()
        s = {n: sem(n) for n in names}
        s_f = [sem(f"f_in{b}") for b in range(B)]
        s_x = [sem(f"x_in{b}") for b in range(B)]
        s_w = [sem(f"w_in{k}") for k in range(RING)]
        s_xs = [sem(f"xs_in{k}") for k in range(4)]
        s_y = [sem(f"y_out{k}") for k in range(2)]
        s_g = [sem(f"gather_in{k}") for k in range(2)]
        s_o = [sem(f"out_out{k}") for k in range(2)]

        block = ctx.enter_context(nc.Block())

        def tokens(a, b):
            return a[b].rearrange("(i p) d -> p i d", p=P)

        def load_expert(eng, e):
            base = (e % RING) * WEXP
            n = C * FF
            eng.dma_start(wreg[:, base:base + n].rearrange("p (c n) -> p c n", c=C),
                          t["L0_ffn_w1"][e].rearrange("(c p) n -> p c n", p=P)).then_inc(s_w[e % RING], 16)
            eng.dma_start(wreg[:, base + n:base + 2 * n].rearrange("p (c n) -> p c n", c=C),
                          t["L0_ffn_w3"][e].rearrange("(c p) n -> p c n", p=P)).then_inc(s_w[e % RING], 16)
            eng.dma_start(wreg[:, base + 2 * n:base + WEXP].rearrange("p (c n) -> p c n", c=FC),
                          t["L0_ffn_w2"][e].rearrange("(c p) n -> p c n", p=P)).then_inc(s_w[e % RING], 16)

        def shifted_keys(engine, U, l, b):
            for c in range(C):
                last = engine.tensor_scalar(U[:, 1, c * S:(c + 1) * S], fT[:, b, c * S:(c + 1) * S], wu[:, 2 * l + 1, c:c + 1], 30.0,
                                            ALU.add, ALU.min)
            last.then_inc(s["ku_ready"], 1)

        @block.sync
        def _(sp):
            sp.dma_start(ident, t["consts"][:, 0:P]).then_inc(s["ident_in"], 16)
            sp.dma_start(cond[:, :, :], t["cond_512"].rearrange("(a b) n -> a b n", a=1).to_broadcast([P, B, 64]))\
                .then_inc(s["par_in"], 16)
            with nc.allow_non_contiguous_dma(reason="short vectors, one element a partition"):
                for k, n in enumerate(("L0_cond_w", "L0_cond_u", "L1_cond_w", "L1_cond_u")):
                    sp.dma_start(wu[:, k], t[n].rearrange("(c p) -> p c", p=P)).then_inc(s["par_in"], 16)
            sp.dma_start(con[:, P:], t["consts"][:, P:]).then_inc(s["con_in"], 16)
            with nc.allow_non_contiguous_dma(reason="short vectors, one element a partition"):
                sp.dma_start(wln[:, :], t["L0_ffn_ln_w"].rearrange("(c p) -> p c", p=P)).then_inc(s["norm_in"], 16)
                sp.dma_start(didx[:, :], t["L1_ffn_down_reorder_index"].rearrange("(c p) -> p c", p=IQ))\
                    .then_inc(s["didx_in"], 16)
            sp.dma_start(ffln[:, :], t["L0_ffn_ff_ln_w"].rearrange("(a n) -> a n", a=1).to_broadcast([P, D]))\
                .then_inc(s["norm_in"], 16)
            sp.dma_start(gate_w[:, :, :], t["L0_ffn_gate_w"].rearrange("(c p) n -> p c n", p=P))\
                .then_inc(s["norm_in"], 16)
            for b in range(B):
                sp.dma_start(x_in[:, b].rearrange("p (i d) -> p i d", i=TT), tokens(t["x"], b)).then_inc(s_x[b], 16)
            at = 0
            for n, w in (("L0_ffn_wq", H * HD), ("L0_ffn_wk", KVH * HD), ("L0_ffn_wv", KVH * HD)):
                sp.dma_start(stage[:, :, at:at + w], t[n].rearrange("(c p) n -> p c n", p=P)).then_inc(s["qkv_in"], 16)
                at += w
            sp.wait_ge(s["qkvhi_done"], 1)
            sp.wait_ge(s["qkvlo_done"], 2)
            sp.dma_start(stage_wo, t["L0_ffn_wo"].rearrange("(h p) n -> p h n", p=P)).then_inc(s["wo_in"], 16)
            sp.wait_ge(s["wolo_done"], 4)
            load_expert(sp, 0)
            for i in range(NT):
                sp.wait_ge(s["h2_ready"], i + 1)
                sp.dma_start(h2_dram[i * P:(i + 1) * P, :], h2[:, i, :]).then_inc(s["h2_out"], 16)
            sp.wait_ge(s["wo_done"], NT)
            load_expert(sp, 1)
            load_expert(sp, 2)
            sp.wait_ge(s["tmap_ready"], 1)
            for e in range(NE):
                if e >= RING:
                    last = sp.value_load(endi[0:1, e - RING:e - RING + 1], min_val=1, max_val=MT + 1)
                    sp.wait_ge(s["down_done"], last)
                    load_expert(sp, e)
                sp.wait_ge(s_w[e % RING], 48 * (e // RING + 1))
                sp.sem_inc(s["w_ready"], 1)
            for i in range(NT):
                sp.wait_ge(s["yo_ready"], i + 1)
                sp.dma_start(out.rearrange("b s d -> (b s) d")[i * P:(i + 1) * P, :], yo[:, i % 2]).then_inc(s_o[i % 2], 16)
            for k in range(2):
                sp.wait_ge(s_o[k], 16 * NT // 2)

        def wo_bank(n):
            return pw[:, 0:D] if n % 2 else po[:, 0:D] if n < 4 else pt2[:, 0, 0:D]

        def attention_steps(eng, step, middle, beside=None):
            for u in range(LAG):
                step(u, u % 2)
                if beside and u < 4:
                    beside(u)
            with eng.Fori(0, H // 2) as i:
                step(i * 2 + LAG, LAG % 2)
                step(i * 2 + LAG + 1, 1 - LAG % 2)
            middle()
            with eng.Fori(0, (H - LAG) // 2) as i:
                step(i * 2 + H + LAG, LAG % 2)
                step(i * 2 + H + LAG + 1, 1 - LAG % 2)
            for u in range(H + LAG + (H - LAG) // 2 * 2, QU + LAG):
                step(u, u % 2)

        def expert_steps(eng, step, ratio_piece, weight_piece, down_piece):
            def bound(f, *a):
                return lambda bank: f(*a, bank)
            step(0, 0)
            with eng.Fori(0, 2) as i:
                for k in range(ROUND):
                    pieces = {4: [bound(ratio_piece, i * 2, h) for h in range(2)],
                              5: [bound(weight_piece, i, 0, h) for h in range(2)],
                              6: [bound(weight_piece, i, 1, h) for h in range(2)],
                              7: [bound(ratio_piece, i * 2 + 1, h) for h in range(2)]}.get(k, (None, None))
                    step(i * ROUND + (k + 1), (k + 1) % 2, pieces, (i, k))
            first = 2 * ROUND + 1
            step(first, 1)
            step(first + 1, 0)
            for k in range(2):
                step(first + 2 + k, 1 - k, [bound(down_piece, k, h) for h in range(2)])
            for n in range(first + 4, MT + 1):
                step(n, n % 2)

        def within(u, lag):
            return not isinstance(u, int) or lag <= u < QU + lag

        @block.tensor
        def _(pe):
            pe.wait_ge(s["ident_in"], 16)
            for b in range(B):
                pe.wait_ge(s_f[b], 16)
                if b >= 2:
                    pe.wait_ge(s["fT_copied"], b - 1)
                for c in range(C):
                    for i in range(TT):
                        last = nc.tensor.transpose(pb[b % 2][:, c * S + i * P:c * S + (i + 1) * P],
                                                   f_tok[:, b, i, c * P:(c + 1) * P], ident)
                last.then_inc(s["fT_done"], 1)

            def ratio_transposes(n):
                pe.wait_ge(s["ratT_ready"], n + 1)
                if n >= 2:
                    pe.wait_ge(s["x0_ready"], n - 1)
                for i in range(TT):
                    for c in range(C):
                        last = nc.tensor.transpose(sc2[:, n % 2, i * D + c * P:i * D + (c + 1) * P],
                                                   cond_buf[0][4][:, c * S + i * P:c * S + (i + 1) * P], ident)
                last.then_inc(s["rat_done"], 1)

            def hidden_transposes(b):
                pe.wait_ge(s["xn_ready"], b + 1)
                if b >= 2:
                    pe.wait_ge(s["hlo_done"], b - 1)
                for c in range(C):
                    for i in range(TT):
                        last = nc.tensor.transpose(pt2[:, b % 2, c * S + i * P:c * S + (i + 1) * P],
                                                   xn[:, i * D + c * P:i * D + (c + 1) * P], ident)
                last.then_inc(s["hTp_done"], 1)

            for b in range(B):
                ratio_transposes(b)
                hidden_transposes(b)

            def split_products(bank, w, m, first=True, final=True):
                order = ((0, 0), (0, 1), (1, 0))
                for k, (a, b) in enumerate(order):
                    last = nc.tensor.matmul(bank, w(a), m(b), start=first and k == 0, stop=final and k == 2)
                return last

            def proj(n, bank, col, pair):
                for c in range(C):
                    last = split_products(bank[:, :], lambda a: qkv16[:, a, c, bass.ds(col, HD)],
                                          lambda a: hT[:, a, c, bass.ds(pair * PAIR, PAIR)], c == 0, c == C - 1)
                last.then_inc(s["proj_done"], 1)

            pe.wait_ge(s["con_in"], 16)
            pe.wait_ge(s["norm_in"], 48)
            pe.wait_ge(s["hlo_done"], B)
            pe.wait_ge(s["hi_done"], B)
            pe.wait_ge(s["qkvhi_done"], 1)
            pe.wait_ge(s["qkvlo_done"], 1)
            pe.wait_ge(s["fT_copied"], B)
            for n in range(KU):
                if n >= 2:
                    pe.wait_ge(s["swap_done"], n - 1)
                proj(n, pb[n % 2], H * HD + (n % KVH) * HD, n // KVH)
                if n >= 2:
                    pe.wait_ge(s["vlo_done"], n - 1)
                for c in range(C):
                    last = split_products((po, pw)[n % 2][:, :], lambda a: hT[:, a, c, n * P:(n + 1) * P],
                                          lambda a: qkv16[:, a, c, (H + KVH) * HD:QKV], c == 0, c == C - 1)
                last.then_inc(s["v_done"], 1)
            pe.wait_ge(s["qkvlo_done"], 2)

            def scores(u, buf):
                pe.wait_ge(s["radd_done"], KU + u + 1)
                if not isinstance(u, int) or u >= 1:
                    pe.wait_ge(s["max_done"], u)
                kv, pair = (u % H) // (H // KVH), u // H
                for b in range(2):
                    for qb in range(2):
                        o, w = (0, P) if qb == 0 else (P, 2 * P)
                        last = nc.tensor.matmul(sc2[:, b, o:o + w], qr[:, buf, b * S + qb * P:b * S + (qb + 1) * P],
                                                kT[:, bass.ds(kv, 1), bass.ds(pair * PAIR + b * S, w)]
                                                .rearrange("p a n -> p (a n)"), start=True, stop=True)
                last.then_inc(s["score_done"], 1)

            def prob_transposes(u, buf):
                pe.wait_ge(s["norm_done"], u + 1)
                pe.wait_ge(s["norm2_done"], u + 1)
                if not isinstance(u, int) or u >= 1:
                    pe.wait_ge(s["pTlo_done"], u)
                for b in range(2):
                    for k in range(3):
                        last = nc.tensor.transpose(pt2[:, b, k * P:(k + 1) * P], pr[:, buf, b, k * P:(k + 1) * P], ident)
                last.then_inc(s["pT_done"], 1)

            def weighted_values(u, buf):
                pe.wait_ge(s["pTlo_done"], u + 1)
                if not isinstance(u, int) or u >= 1:
                    pe.wait_ge(s["olo_done"], u)
                kv, pair = (u % H) // (H // KVH), u // H
                for b in range(2):
                    for kb in range(2):
                        o, w = (0, S) if kb == 0 else (2 * P, P)
                        last = split_products(po[:, b * S + kb * P:b * S + kb * P + w],
                                              lambda a: v16[:, a, bass.ds(pair * 4 + b * TT + kb, 1), bass.ds(kv * HD, HD)]
                                              .rearrange("p a n -> p (a n)"),
                                              lambda a: pT[:, buf, a, b, o:o + w], kb == 0, kb == 1)
                last.then_inc(s["av_done"], 1)

            def route(i):
                pe.wait_ge(s["h2_ready"], i + 1)
                if i >= 2:
                    pe.wait_ge(s["h2T_copied"], i - 1)
                for c in range(C):
                    last = nc.tensor.transpose(pb[i % 2][:, c * P:(c + 1) * P], h2[:, i, c * P:(c + 1) * P], ident)
                last.then_inc(s["h2T_done"], 1)
                pe.wait_ge(s["h2T_copied"], i + 1)
                for c in range(C):
                    last = nc.tensor.matmul(po[:, i * NE:(i + 1) * NE], h2T[:, i % 2, c * P:(c + 1) * P], gate_w[:, c, :],
                                            start=c == 0, stop=c == C - 1)
                last.then_inc(s["gate_tile"], 1)

            def project_out(pair):
                pe.wait_ge(s["olo_done"], (pair + 1) * H)
                pe.wait_ge(s["wolo_done"], 4)
                for i in range(4):
                    n = 4 * pair + i
                    if n >= 2:
                        pe.wait_ge(s["x1a_done"], n - 1)
                    for h in range(H):
                        last = split_products(wo_bank(n), lambda a: oT[:, a, h, i * P:(i + 1) * P],
                                              lambda a: wo16[:, a, h, :], h == 0, h == H - 1)
                    last.then_inc(s["wo_done"], 1)
                    if pair == 1 and i < 3:
                        for j in ((0, 1), (2, 3), (4,))[i]:
                            route(j)
                if pair == 0:
                    pe.wait_ge(s["x1a_done"], 4)

            def step(u, parity):
                if within(u, 0):
                    pe.wait_ge(s["swap_done"], KU + u - 1)
                    proj(None, pb[parity], (u % H) * HD, u // H)
                if within(u, 2):
                    scores(u - 2, parity)
                if within(u, 4):
                    prob_transposes(u - 4, parity)
                if within(u, 5):
                    weighted_values(u - 5, 1 - parity)

            pe.wait_ge(s["vlo_done"], NT)
            pe.wait_ge(s["x0_ready"], B)
            attention_steps(pe, step, lambda: project_out(0))
            project_out(1)

            for i in range(5, NT):
                route(i)
            pe.wait_ge(s["mk_ready"], 1)
            nc.tensor.matmul(po[:, 128:128 + NT * NE], before, MK, start=True, stop=True)
            nc.tensor.matmul(po[:, 256:256 + NT * NE], ones, MK, start=True, stop=True).then_inc(s["rank_done"], 1)

            for k in range(2 * NT):
                if k % NT == 0:
                    pe.wait_ge(s["hot_ready"], k // NT + 1)
                last = nc.tensor.matmul(pw[:, 0:MT], hot_place[:, k, :], hot_tile[:, k, :], start=k == 0, stop=k == 2 * NT - 1)
            last.then_inc(s["ids_done"], 1)

            def ratio_piece(b, i, bank):
                pe.wait_ge(s["ratT_ready"], B + b + 1)
                for c in range(C):
                    last = nc.tensor.transpose(bank[:, D + c * P:D + (c + 1) * P],
                                               cond_buf[1][4][:, c * S + i * P:c * S + (i + 1) * P], ident)
                if i == TT - 1:
                    last.then_inc(s["rat_done"], 1)

            def weight_piece(m, kc, half, bank):
                pe.wait_ge(s["rq_ready"], m + 1)
                for j in range(NI // 2):
                    c = half * (NI // 2) + j
                    last = nc.tensor.transpose(bank[:, D:].bitcast(BF16)[:, j * IQ:(j + 1) * IQ],
                                               rq[0:IQ, c * D + kc * P:c * D + (kc + 1) * P], identb[0:IQ, 0:IQ])
                if (kc, half) == (1, 1):
                    last.then_inc(s["rqT_done"], 1)

            def down_piece(hc, half, bank):
                pe.wait_ge(s["rq_ready"], 3)
                for j in range(NI // 2):
                    c = half * (NI // 2) + j
                    last = nc.tensor.transpose(bank[0:IQ, D:].bitcast(BF16)[:, j * P:(j + 1) * P],
                                               rq[:, hc * INTER + c * IQ:hc * INTER + (c + 1) * IQ], identb[:, :])

            def x_transposes(n, k, piece=None):
                pe.wait_ge(s_xs[k], 16 * (n // 4 + 1))
                if not isinstance(n, int) or n >= 1:
                    pe.wait_ge(s["xT_copied"], n)
                if piece:
                    piece(po)
                for c in range(C):
                    last = nc.tensor.transpose(po[:, c * P:(c + 1) * P], xs[k][:, c * P:(c + 1) * P], ident)
                last.then_inc(s["xT_done"], 1)

            def up(n, parity, base, part):
                lo, w = (0, FA) if part == 0 else (FA, FB)
                for m in range(2):
                    bank = (pb[m] if part == 0 else sc2[:, m])[:, 0:w]
                    for c in range(C):
                        last = nc.tensor.matmul(bank, xsT[:, parity, c * P:(c + 1) * P],
                                                wreg[:, bass.ds(base + (m * C + c) * FF + lo, w)], start=c == 0, stop=c == C - 1)
                last.then_inc(s["upa_done" if part == 0 else "upb_done"], 1)

            def h_transposes(n):
                pe.wait_ge(s["inner_b_done"], n + 1)
                if not isinstance(n, int) or n >= 1:
                    pe.wait_ge(s["hTlo_done"], n)
                for c in range(FC):
                    last = nc.tensor.transpose(pt2[:, c // 4, c % 4 * P:(c % 4 + 1) * P], hh[:, c * P:(c + 1) * P], ident)
                last.then_inc(s["hT_done"], 1)

            def down(n, parity, piece=None):
                pe.wait_ge(s["hTlo_done"], n + 1)
                pe.wait_ge(s["w2lo_done"], n + 1)
                if not isinstance(n, int) or n >= 1:
                    pe.wait_ge(s["y_copied"], n)
                if piece:
                    piece(pw)
                for c in range(FC):
                    last = split_products(pw[:, 0:D], lambda a: hhT[:, a, c, :], lambda a: w2s[parity][a][:, c, :], c == 0, c == FC - 1)
                last.then_inc(s["down_done"], 1)

            pe.wait_ge(s["tmap_ready"], 1)
            pe.wait_ge(s["identb_ready"], 1)
            pe.sem_inc(s["down_done"], 1)
            x_transposes(0, 0)

            def tile_base(n):
                e = pe.value_load(tmi[0:1, bass.ds(n, 1)], min_val=0, max_val=NE - 1)
                return e, (e % RING) * WEXP

            def tile_step(n, parity, pieces=(None, None), place=None):
                fixed = isinstance(n, int)
                if not fixed or n < MT:
                    e, base = tile_base(n)
                    pe.wait_ge(s["w_ready"], e + 1)
                    pe.wait_ge(s["xT_copied"], n + 1)
                    if not fixed or n >= 1:
                        pe.wait_ge(s["inner_a_done"], n)
                    up(n, parity, base, 0)
                if not fixed or n >= 1:
                    h_transposes(n - 1)
                if not fixed or n < MT:
                    if not fixed or n + 1 < MT:
                        k = (n + 1) % 4 if fixed else (place[1] + 2) % 4
                        x_transposes(n + 1, k, pieces[0])
                    up(n, parity, base, 1)
                if not fixed or n >= 1:
                    down(n - 1, 1 - parity, pieces[1])

            expert_steps(pe, tile_step, ratio_piece, weight_piece, down_piece)

            def quantised_transposes(i):
                pe.wait_ge(s["qx_ready"], i // 2 + 1)
                if i >= 1:
                    pe.wait_ge(s["qxT_copied"], i)
                else:
                    pe.wait_ge(s["xT_copied"], MT)
                for c in range(C):
                    last = nc.tensor.transpose(po[:, :].bitcast(BF16)[:, c * P:(c + 1) * P], qx[:, i // 2 % 2, i % 2, c * P:(c + 1) * P], identb[:, :])
                last.then_inc(s["qxT_done"], 1)

            def gate_up(i):
                pe.wait_ge(s["qxT_copied"], i + 1)
                if i >= 1:
                    pe.wait_ge(s["gate_ready"], i)
                    pe.wait_ge(s["up_ready"], i)
                else:
                    pe.wait_ge(s["inner_b_done"], MT)
                for m in range(2):
                    for k in range(2):
                        bank = (pb[k] if m == 0 else sc2[:, k])[:, 0:IH]
                        for c in range(C):
                            last = nc.tensor.matmul(bank, qxT[:, c, :], q1w[:, m, c, k * IH:(k + 1) * IH],
                                                    start=c == 0, stop=c == C - 1)
                    last.then_inc(s["gatep_done" if m == 0 else "upp_done"], 1)

            def inner_transposes(i):
                pe.wait_ge(s["qt_ready"], i + 1)
                if i >= 1:
                    pe.wait_ge(s["qtT_copied"], i)
                else:
                    pe.wait_ge(s["hTlo_done"], MT)
                for c in range(NI):
                    last = nc.tensor.transpose(pt2[0:IQ, 0, :].bitcast(BF16)[:, c * P:(c + 1) * P], qt[:, c * IQ:(c + 1) * IQ], identb[:, :])
                last.then_inc(s["qtT_done"], 1)

            def down_quantised(i):
                pe.wait_ge(s["qtT_copied"], i + 1)
                if i >= 1:
                    pe.wait_ge(s["yo_read"], i)
                else:
                    pe.wait_ge(s["y_copied"], MT)
                for c in range(NI):
                    last = nc.tensor.matmul(pw[:, 0:D], qtT[0:IQ, c, :], q1d[0:IQ, c, :], start=c == 0, stop=c == NI - 1)
                last.then_inc(s["dn_done"], 1)

            pe.wait_ge(s["rq_copied"], 3)
            for i in range(NT + 2):
                if i < NT:
                    quantised_transposes(i)
                    gate_up(i)
                if i >= 2:
                    inner_transposes(i - 2)
                    down_quantised(i - 2)

        @block.scalar
        def _(act):
            links = [0]

            def link(ins):
                links[0] += 1
                ins.then_inc(s["act_link"], 1)
                act.wait_ge(s["act_link"], links[0])

            for b in range(B):
                act.dma_start(f_tok[:, b], tokens(t["fside_BxSxS_0"], b)).then_inc(s_f[b], 16)

            def copy_fT(b):
                act.wait_ge(s["fT_done"], b + 1)
                nc.scalar.copy(fT[:, b, :], pb[b % 2][:, :]).then_inc(s["fT_copied"], 1)

            def exponential_of_keys(n, parity, bufs):
                E = bufs[0][:, parity]
                first = bufs is cond_buf[0]
                act.wait_ge(s["kmin_ready" if first else "ku_ready"], n + 1)
                nc.scalar.activation(E[:, 1, :], E[:, 1, :], ACT.Exp).then_inc(s["ek_ready"], 1)

            def exponential_of_sums(n, parity, bufs):
                U = bufs[1][:, parity]
                act.wait_ge(s["ku_ready"], n + 1)
                nc.scalar.activation(U[:, 1, :], U[:, 1, :], ACT.Exp).then_inc(s["uexp_ready"], 1)

            def exponentials_of_batch(n, parity, bufs):
                exponential_of_keys(n, parity, bufs)
                exponential_of_sums(n, parity, bufs)

            copy_fT(0)
            exponential_of_keys(0, 0, cond_buf[0])
            copy_fT(1)
            act.wait_ge(s["tfsum"], 1)
            nc.scalar.activation(tf[:, 1, :], tf[:, 0, :], ACT.Exp, scale=-1.0).then_inc(s["tf_exp"], 1)
            link(nc.scalar.activation(dec[:, 0, :, :], wu[:, 0:4:2, :], ACT.Exp))
            nc.scalar.activation(dec[:, 1, :, :], dec[:, 0, :, :], ACT.Exp, scale=-1.0).then_inc(s["dec_exp"], 1)
            exponential_of_sums(0, 0, cond_buf[0])
            copy_fT(2)
            copy_fT(3)
            exponentials_of_batch(1, 1, cond_buf[0])
            for b in range(B):
                act.wait_ge(s_x[b], 16)
                nc.scalar.activation(sg[:, b, :], x_in[:, b, :], ACT.Sigmoid).then_inc(s["sg_exp"], 1)

            def split_high():
                act.wait_ge(s["qkv_in"], 48)
                for c in range(C):
                    for q in range(2):
                        nc.scalar.activation(qkv16[:, 0, c, 0:20 * HD].rearrange("p (h q i) -> p h q i", q=2, i=HD // 2)[:, :, q, :],
                                             stage[:, c, q:20 * HD:2].rearrange("p (h i) -> p h i", i=HD // 2), ACT.Copy, scale=WS)
                nc.scalar.activation(qkv16[:, 0, :, 20 * HD:], stage[:, :, 20 * HD:], ACT.Copy, scale=WS).then_inc(s["qkvhi_done"], 1)

            def squares(b):
                act.wait_ge(s["x0_ready"], b + 1)
                for i in range(TT):
                    last = nc.scalar.activation(t1[:, b % 2, i * D:(i + 1) * D], x0[:, b * TT + i, :], ACT.Square,
                                                accum_out=ssq[:, 0, b * TT + i:b * TT + i + 1])
                last.then_inc(s["ssq_ready"], 1)

            def normalise_rows(b):
                act.wait_ge(s["rstd_ready"], b + 1)
                if b >= 1:
                    act.wait_ge(s["hTp_done"], b)
                for i in range(TT):
                    k = b * TT + i
                    last = nc.scalar.activation(xn[:, i * D:(i + 1) * D], x0[:, k, :], ACT.Copy, scale=ssq[:, 2, k:k + 1])
                last.then_inc(s["xn_ready"], 1)

            def hidden_high(b):
                act.wait_ge(s["hTp_done"], b + 1)
                for c in range(C):
                    last = nc.scalar.activation(hT[:, 0, c, b * S:(b + 1) * S], pt2[:, b % 2, c * S:(c + 1) * S],
                                                ACT.Copy, scale=wln[:, c:c + 1])
                last.then_inc(s["hi_done"], 1)

            act.wait_ge(s["norm_in"], 48)
            for b in range(B):
                squares(b)
                if b >= 1:
                    hidden_high(b - 1)
                normalise_rows(b)
                if b + 2 < B:
                    exponentials_of_batch(b + 2, b % 2, cond_buf[0])
                if b == 1:
                    split_high()
            hidden_high(B - 1)

            HH = HD // 2

            def swap_halves(n, parity):
                act.wait_ge(s["rope_done"], n + 1)
                if not isinstance(n, int) or n >= 2:
                    act.wait_ge(s["radd_done"], n - 1)
                nc.scalar.copy(t2[0:HH, parity, :], pb[parity][HH:HD, :])
                nc.scalar.copy(t2[HH:HD, parity, :], pb[parity][0:HH, :]).then_inc(s["swap_done"], 1)

            def exponentials(u, parity):
                act.wait_ge(s["nmax_done"], u + 1)
                for b in range(2):
                    for qb in range(2):
                        o, w = (0, P) if qb == 0 else (P, 2 * P)
                        k = 2 * b + qb
                        last = nc.scalar.activation(pr[:, parity, b, o:o + w], pr[:, parity, b, o:o + w], ACT.Exp,
                                                    bias=mx[:, parity, 1, k:k + 1], scale=SCALE,
                                                    accum_out=sums[:, parity, 0, k:k + 1])
                last.then_inc(s["exp_done"], 1)

            def pT_high(u, parity):
                act.wait_ge(s["pT_done"], u + 1)
                if not isinstance(u, int) or u >= 2:
                    act.wait_ge(s["av_done"], u - 1)
                nc.scalar.copy(pT[:, parity, 0], pt2[:, :, 0:BLK]).then_inc(s["pThi_done"], 1)

            def o_high(u):
                act.wait_ge(s["av_done"], u + 1)
                nc.scalar.copy(oT[:, 0, bass.ds(u % H, 1), :].rearrange("p a n -> p (a n)"), po[:, :]).then_inc(s["ohi_done"], 1)

            for n in range(KU):
                swap_halves(n, n % 2)
                act.wait_ge(s["v_done"], n + 1)
                nc.scalar.copy(v16[:, 0, n, :], (po, pw)[n % 2][:, :]).then_inc(s["vhi_done"], 1)

            def step(u, parity):
                if within(u, 3):
                    exponentials(u - 3, 1 - parity)
                if within(u, 4):
                    pT_high(u - 4, parity)
                if within(u, 0):
                    swap_halves(KU + u, parity)
                if within(u, 5):
                    o_high(u - 5)

            def wo_high(u):
                hs = slice(u * 4, u * 4 + 4)
                act.wait_ge(s["wo_in"], 16)
                nc.scalar.activation(wo16[:, 0, hs], stage_wo[:, hs], ACT.Copy, scale=WS).then_inc(s["wohi_done"], 1)

            attention_steps(act, step, lambda: act.wait_ge(s["wo_done"], NT // 2), wo_high)

            act.wait_ge(s["av_done"], QU)
            act.wait_ge(s["olo_done"], QU)

            def squares_of_tile(i):
                act.wait_ge(s["x1a_done"], i + 1)
                nc.scalar.activation(h2[:, i, :], x0[:, i, :], ACT.Square, accum_out=ssq[:, 0, i:i + 1]).then_inc(s["ssq2_ready"], 1)

            def copy_h2T(i):
                act.wait_ge(s["h2T_done"], i + 1)
                if i >= 2:
                    act.wait_ge(s["gate_tile"], i - 1)
                nc.scalar.copy(h2T[:, i % 2, :], pb[i % 2][:, 0:D]).then_inc(s["h2T_copied"], 1)

            for tiles, copies in ((range(4), (0, 1)), ((4,), (2, 3)), ((5,), (4,)), ((6, 7), (5, 6, 7))):
                for i in tiles:
                    squares_of_tile(i)
                for i in copies:
                    copy_h2T(i)
            act.wait_ge(s["d_ready"], 1)
            nc.scalar.activation(gts[:, :, 1], gts[:, :, 0], ACT.Exp).then_inc(s["ge_ready"], 1)

            def ratio_piece(b, i, bank):
                last = nc.scalar.copy(ratio1[:, bass.ds(b * TT + i, 1), :], bank[:, D:].rearrange("p (a n) -> p a n", a=1))
                if i == TT - 1:
                    last.then_inc(s["ratio1_copied"], 1)

            def weight_piece(m, kc, half, bank):
                w = INTER // 2
                last = nc.scalar.copy(q1w[:, bass.ds(m, 1), kc, half * w:(half + 1) * w],
                                      bank[:, D:D + w // 2].bitcast(BF16).rearrange("p (a n) -> p a n", a=1))
                if (kc, half) == (1, 1):
                    last.then_inc(s["rq_copied"], 1)

            def down_piece(hc, half, bank):
                last = nc.scalar.copy(q1d[0:IQ, half * (NI // 2):(half + 1) * (NI // 2), hc * P:(hc + 1) * P],
                                      bank[0:IQ, D:].bitcast(BF16).rearrange("p (c n) -> p c n", c=NI // 2))
                if (hc, half) == (1, 1):
                    last.then_inc(s["rq_copied"], 1)

            def copy_xT(n, parity, piece=None):
                act.wait_ge(s["xT_done"], n + 1)
                if piece:
                    piece(po)
                if not isinstance(n, int) or n >= 2:
                    act.wait_ge(s["upb_done"], n - 1)
                nc.scalar.copy(xsT[:, parity, :], po[:, 0:D]).then_inc(s["xT_copied"], 1)

            act.wait_ge(s["tmap_ready"], 1)
            act.wait_ge(s["h2_out"], 16 * NT)
            copy_xT(0, 0)

            def w2_high(n, parity):
                e = act.value_load(tmi[0:1, bass.ds(n, 1)], min_val=0, max_val=NE - 1)
                act.wait_ge(s["w_ready"], e + 1)
                if not isinstance(n, int) or n >= 2:
                    act.wait_ge(s["down_done"], n)
                nc.scalar.activation(w2s[parity][0].rearrange("p c n -> p (c n)"),
                                     wreg[:, bass.ds((e % RING) * WEXP + 2 * C * FF, FC * D)], ACT.Copy, scale=WS).then_inc(s["w2hi_done"], 1)

            for k in range(2):
                act.sem_inc(s_y[k], 16)

            def tile_step(n, parity, pieces=(None, None), place=None):
                fixed = isinstance(n, int)
                if place and place[1] in (0, 3):
                    k = place[1] // 3
                    exponentials_of_batch(place[0] * 2 + (B + k), k, cond_buf[1])
                if not fixed or n < MT:
                    act.wait_ge(s["upa_done"], n + 1)
                    if not fixed or n >= 1:
                        act.wait_ge(s["inner_b_done"], n)
                    nc.scalar.activation(silu_out[:, 0:FA], pb[0][:, :], ACT.Silu).then_inc(s["silu_a_done"], 1)
                if not fixed or n >= 1:
                    act.wait_ge(s["hT_done"], n)
                    if not fixed or n >= 2:
                        act.wait_ge(s["down_done"], n)
                    nc.scalar.copy(hhT[:, 0, 0:4, :], pt2[:, 0, :].rearrange("p (c n) -> p c n", c=4))
                    nc.scalar.copy(hhT[:, 0, 4:FC, :], pt2[:, 1, 0:FB].rearrange("p (c n) -> p c n", c=FC - 4)).then_inc(s["hT_copied"], 1)
                if not fixed or n + 1 < MT:
                    copy_xT(n + 1, 1 - parity, pieces[0])
                if not fixed or n < MT:
                    w2_high(n, parity)
                    act.wait_ge(s["upb_done"], n + 1)
                    nc.scalar.activation(silu_out[:, FA:FF], sc2[:, 0, 0:FB], ACT.Silu).then_inc(s["silu_b_done"], 1)
                if not fixed or n >= 1:
                    act.wait_ge(s["down_done"], n + 1)
                    if pieces[1]:
                        pieces[1](pw)
                    act.wait_ge(s_y[1 - parity], 16 * ((n + 1) // 2))
                    nc.scalar.activation(ysb[:, 1 - parity, :], pw[:, 0:D], ACT.Copy, scale=1.0 / WS).then_inc(s["y_copied"], 1)
                    act.wait_ge(s["y_copied"], n)
                    act.dma_start(ys_dram[bass.ds((n - 1) * P, P), :], ysb[:, 1 - parity, :]).then_inc(s_y[1 - parity], 16)

            expert_steps(act, tile_step, ratio_piece, weight_piece, down_piece)

            def input_gate(p):
                act.wait_ge(s["x1_ready"], p + 1)
                if p >= 1:
                    act.wait_ge(s["qx_ready"], p)
                nc.scalar.activation(xsig, x1[:, 2 * p:2 * p + 2, :].rearrange("p i n -> p (i n)"), ACT.Sigmoid)\
                    .then_inc(s["sgx_ready"], 1)

            def copy_qxT(i):
                act.wait_ge(s["qxT_done"], i + 1)
                if i >= 1:
                    act.wait_ge(s["upp_done"], i)
                nc.scalar.copy(qxT[:, :, :], po[:, 0:P].bitcast(BF16).rearrange("p (c n) -> p c n", c=C)).then_inc(s["qxT_copied"], 1)

            def gate_of_tile(i):
                act.wait_ge(s["gate_ready"], i + 1)
                nc.scalar.activation(gsig, gate, ACT.Sigmoid, scale=rs[:, 3, i:i + 1]).then_inc(s["gsig_ready"], 1)
                act.wait_ge(s["upp_done"], i + 1)
                if i >= 2:
                    act.wait_ge(s["inv_ready"], i - 1)
                nc.scalar.copy(upvs[i % 2].rearrange("p (k n) -> p k n", k=2), sc2[:, :, 0:IH]).then_inc(s["up_ready"], 1)

            input_gate(0)
            copy_qxT(0)
            gate_of_tile(0)
            copy_qxT(1)
            input_gate(1)
            for i in range(NT):
                if i + 1 < NT:
                    gate_of_tile(i + 1)
                act.wait_ge(s["inv_ready"], i + 1)
                nc.scalar.activation(tscaled, tval, ACT.Copy, scale=rs[:, 8, i:i + 1]).then_inc(s["scaled_ready"], 1)
                if i % 2 == 1 and i + 3 < NT:
                    input_gate((i + 3) // 2)
                if i + 2 < NT:
                    copy_qxT(i + 2)
                act.wait_ge(s["qtT_done"], i + 1)
                if i >= 1:
                    act.wait_ge(s["dn_done"], i)
                nc.scalar.copy(qtT[0:IQ, :, :], pt2[0:IQ, 0, :].bitcast(BF16).rearrange("p (c n) -> p c n", c=NI)).then_inc(s["qtT_copied"], 1)

        @block.vector
        def _(dve):
            links = [0]
            V = nc.vector

            def link(ins):
                links[0] += 1
                ins.then_inc(s["dve_link"], 1)
                dve.wait_ge(s["dve_link"], links[0])

            def clamp_keys(b):
                dve.wait_ge(s["fT_copied"], b + 1)
                if b >= 2:
                    dve.wait_ge(s["u_used"], b - 1)
                V.tensor_scalar(cond_buf[0][0][:, b % 2, 1, :], fT[:, b, :], 30.0, None, ALU.min).then_inc(s["kmin_ready"], 1)

            clamp_keys(0)
            dve.wait_ge(s["par_in"], 16 * 5)
            shifted_keys(V, cond_buf[0][1][:, 0], 0, 0)
            V.tensor_reduce(out=tf[:, 0, :], in_=cond[:, :, :], axis=AX.X, op=ALU.add).then_inc(s["tfsum"], 1)
            dve.wait_ge(s["tf_exp"], 1)
            link(V.tensor_scalar(tf[:, 2, :], tf[:, 1, :], 1.0, None, ALU.add))
            link(V.reciprocal(tf[:, 3, :], tf[:, 2, :]))
            V.tensor_scalar(tf[:, 4, :], tf[:, 3, :], 0.5, 0.5, ALU.mult, ALU.add)
            link(V.tensor_scalar(tf[:, 5, :], tf[:, 3, :], 0.2, 0.8, ALU.mult, ALU.add))
            dve.wait_ge(s["dec_exp"], 1)
            for l in range(2):
                for c in range(C):
                    last = V.tensor_scalar(decay[:, l, c, :], tf[:, 4, :], dec[:, 1, l, c:c + 1], None, ALU.mult)
            link(last)
            clamp_keys(1)
            for c in range(C):
                V.tensor_copy(cond1[:, :, c], decay[:, 1, c, :])
            V.tensor_copy(cond1[:, :, C], tf[:, 5, :])

            def scans(E, fwd, bwd, decay_of):
                for c in range(C):
                    a = decay_of(c).to_broadcast([P, S])
                    for k in range(2):
                        src = E[:, k, c * S:(c + 1) * S]
                        V.tensor_tensor_scan(out=fwd[:, k, c * S:(c + 1) * S], data0=a, data1=src, initial=0.0,
                                             op0=ALU.mult, op1=ALU.add)
                        last = V.tensor_tensor_scan(out=bwd[:, k, c * S:(c + 1) * S][:, ::-1], data0=a, data1=src[:, ::-1],
                                                    initial=0.0, op0=ALU.mult, op1=ALU.add)
                return last

            def mixing_ratio(b):
                E2, U2, fwd, bwd, rat = cond_buf[0]
                dve.wait_ge(s["e_ready"], b + 1)
                link(scans(E2[:, b % 2], fwd, bwd, lambda c: decay[:, 0, c, b:b + 1]))
                link(V.tensor_tensor(fwd[:, :, :], fwd[:, :, :], bwd[:, :, :], ALU.add))
                dve.wait_ge(s["u_ready"], b + 1)
                V.tensor_tensor(fwd[:, :, :], fwd[:, :, :], U2[:, b % 2], ALU.add).then_inc(s["u_used"], 1)
                dve.wait_ge(s["u_used"], b + 1)
                link(V.tensor_scalar(fwd[:, 1, :], fwd[:, 1, :], 1e-8, None, ALU.max))
                link(V.reciprocal(bwd[:, 1, :], fwd[:, 1, :]))
                if b >= 1:
                    dve.wait_ge(s["rat_done"], b)
                V.scalar_tensor_tensor(rat, fwd[:, 0, :], tf[:, 5, b:b + 1], bwd[:, 1, :], ALU.mult, ALU.mult)\
                    .then_inc(s["ratT_ready"], 1)

            def first_input(b):
                dve.wait_ge(s["sg_exp"], b + 1)
                dve.wait_ge(s["rat_done"], b + 1)
                V.tensor_tensor(x0[:, TT * b:TT * (b + 1), :].rearrange("p i n -> p (i n)"), sc2[:, b % 2, :], sg[:, b, :], ALU.mult)\
                    .then_inc(s["x0_ready"], 1)

            def hidden_low(b):
                dve.wait_ge(s["hi_done"], b + 1)
                if b == 0:
                    dve.wait_ge(s["norm_in"], 48)
                for c in range(C):
                    last = V.scalar_tensor_tensor(hT[:, 1, c, b * S:(b + 1) * S], pt2[:, b % 2, c * S:(c + 1) * S], wln[:, c:c + 1],
                                                  hT[:, 0, c, b * S:(b + 1) * S], ALU.mult, ALU.subtract)
                last.then_inc(s["hlo_done"], 1)

            for b in range(B):
                mixing_ratio(b)
                if b + 2 < B:
                    clamp_keys(b + 2)
                if b >= 2:
                    hidden_low(b - 2)
                first_input(b)
            hidden_low(B - 2)
            dve.wait_ge(s["con_in"], 16)
            dve.wait_ge(s["qkvhi_done"], 1)

            def lanes(w, c, q, h0, h1):
                if w == 2:
                    return stage[:, c, h0 * HD + q:h1 * HD:2].rearrange("p (h i) -> p h i", i=HD // 2)
                return qkv16[:, w, c, h0 * HD:h1 * HD].rearrange("p (h q i) -> p h q i", q=2, i=HD // 2)[:, :, q, :]

            def low_lanes(c, q, h0, h1):
                return V.scalar_tensor_tensor(lanes(1, c, q, h0, h1), lanes(2, c, q, h0, h1), WS, lanes(0, c, q, h0, h1),
                                              ALU.mult, ALU.subtract)

            for c in range(C):
                for q in range(2):
                    low_lanes(c, q, H, H + KVH)
            V.scalar_tensor_tensor(qkv16[:, 1, :, (H + KVH) * HD:], stage[:, :, (H + KVH) * HD:], WS, qkv16[:, 0, :, (H + KVH) * HD:],
                                   ALU.mult, ALU.subtract).then_inc(s["qkvlo_done"], 1)
            hidden_low(B - 1)

            def rope(n, parity):
                dve.wait_ge(s["proj_done"], n + 1)
                if not isinstance(n, int) or n >= 2:
                    dve.wait_ge(s["radd_done"], n - 1)
                bank = pb[parity][:, :].rearrange("p (b n) -> p b n", b=2)
                V.tensor_tensor(t1[:, parity, :].rearrange("p (b n) -> p b n", b=2), bank,
                                rope_cos.rearrange("p (a n) -> p a n", a=1).to_broadcast([P, 2, S]), ALU.mult)\
                    .then_inc(s["rope_done"], 1)

            def batches_of(x):
                return x.rearrange("p (b n) -> p b n", b=2)

            def times_sin(n):
                dve.wait_ge(s["swap_done"], n + 1)
                V.tensor_tensor(batches_of(t2[:, n % 2, :]), batches_of(t2[:, n % 2, :]),
                                rope_sin.rearrange("p (a n) -> p a n", a=1).to_broadcast([P, 2, S]), ALU.mult).then_inc(s["sin_done"], 1)

            def v_low(i):
                dve.wait_ge(s["vhi_done"], i + 1)
                V.tensor_tensor(v16[:, 1, i, :], (po, pw)[i % 2][:, :], v16[:, 0, i, :], ALU.subtract).then_inc(s["vlo_done"], 1)

            for n in range(KU + 1):
                if n < KU:
                    rope(n, n % 2)
                if n >= 1:
                    times_sin(n - 1)
                    v_low(n - 1)
                if n < 2 * C:
                    last = low_lanes(n // 2, n % 2, 0, H)
                    if n == 2 * C - 1:
                        last.then_inc(s["qkvlo_done"], 1)

            def normalise(u, parity):
                dve.wait_ge(s["exp_done"], u + 1)
                V.reciprocal(sums[:, parity, 1, :], sums[:, parity, 0, :]).then_inc(s["recip_done"], 1)
                dve.wait_ge(s["recip_done"], u + 1)
                for qb in range(2):
                    o, w = (0, P) if qb == 0 else (P, 2 * P)
                    last = V.tensor_scalar(pr[:, parity, 0, o:o + w], pr[:, parity, 0, o:o + w], sums[:, parity, 1, qb:qb + 1],
                                           None, ALU.mult)
                last.then_inc(s["norm_done"], 1)

            def row_max(u, parity):
                dve.wait_ge(s["score_done"], u + 1)
                if not isinstance(u, int) or u >= 2:
                    dve.wait_ge(s["pT_done"], u - 1)
                dve.sem_inc(s["dve_paused"], 1)
                for b in range(2):
                    for qb in range(2):
                        o, w = (0, P) if qb == 0 else (P, 2 * P)
                        k = 2 * b + qb
                        last = V.tensor_tensor_reduce(out=pr[:, parity, b, o:o + w], in0=sc2[:, b, o:o + w], in1=mask[:, o:o + w],
                                                      scale=1.0, scalar=-3e38, op0=ALU.add, op1=ALU.max,
                                                      accum_out=mx[:, parity, 0, k:k + 1])
                last.then_inc(s["max_done"], 1)
                dve.wait_ge(s["max_done"], u + 1)
                V.tensor_scalar(mx[:, parity, 1, :], mx[:, parity, 0, :], -SCALE, None, ALU.mult).then_inc(s["nmax_done"], 1)

            def pT_low(u, parity):
                dve.wait_ge(s["pThi_done"], u + 1)
                V.tensor_tensor(pT[:, parity, 1], pt2[:, :, 0:BLK], pT[:, parity, 0], ALU.subtract).then_inc(s["pTlo_done"], 1)

            def o_low(u):
                dve.wait_ge(s["ohi_done"], u + 1)
                V.tensor_tensor(oT[:, 1, bass.ds(u % H, 1), :].rearrange("p a n -> p (a n)"), po[:, :],
                                oT[:, 0, bass.ds(u % H, 1), :].rearrange("p a n -> p (a n)"), ALU.subtract).then_inc(s["olo_done"], 1)

            def step(u, parity):
                if within(u, 0):
                    rope(KU + u, parity)
                if within(u, 3):
                    normalise(u - 3, 1 - parity)
                if within(u, 2):
                    row_max(u - 2, parity)
                if within(u, 4):
                    pT_low(u - 4, parity)
                if within(u, 5):
                    o_low(u - 5)

            def residual(n):
                dve.wait_ge(s["wo_done"], n + 1)
                V.scalar_tensor_tensor(x0[:, n, :], wo_bank(n), 1.0 / (WS * WS), x0[:, n, :],
                                       ALU.mult, ALU.add).then_inc(s["x1a_done"], 1)

            def wo_low(u):
                hs = slice(u * 4, u * 4 + 4)
                dve.wait_ge(s["wohi_done"], u + 1)
                V.scalar_tensor_tensor(wo16[:, 1, hs], stage_wo[:, hs], WS, wo16[:, 0, hs], ALU.mult, ALU.subtract).then_inc(s["wolo_done"], 1)

            attention_steps(dve, step, lambda: [residual(n) for n in range(4)], wo_low)

            def second_norm(i):
                dve.wait_ge(s["rstd2_ready"], i + 1)
                V.scalar_tensor_tensor(h2[:, i, :], x0[:, i, :], ssq[:, 2, i:i + 1], ffln[:, :], ALU.mult, ALU.mult)\
                    .then_inc(s["h2_ready"], 1)

            for n, norms in ((4, (0, 1)), (5, (2, 3)), (6, (4,)), (7, (5,))):
                for i in norms:
                    second_norm(i)
                residual(n)
            second_norm(6)
            second_norm(7)
            dve.wait_ge(s["gate_tile"], NT)
            link(V.tensor_copy(lg, po[:, 0:NT * NE]))
            for i in range(NT):
                last = V.max(m8[:, i * NE:(i + 1) * NE], lg[:, i * NE:(i + 1) * NE])
            link(last)
            for i in range(NT):
                last = V.max_index(i8[:, i * NE:(i + 1) * NE], m8[:, i * NE:(i + 1) * NE], lg[:, i * NE:(i + 1) * NE])
            link(last)

            def te(x):
                return x.rearrange("p (i e) -> p i e", e=NE)

            m8v = te(m8)
            idfv = idf.rearrange("p (i k) -> p i k", k=2)
            iota = iota_e.rearrange("p (a e) -> p a e", a=1).to_broadcast([P, NT, NE])
            link(V.tensor_copy(idfv, i8.rearrange("p (i e) -> p i e", e=NE)[:, :, 0:2]))
            V.tensor_tensor(te(M1), iota, idfv[:, :, 0:1].to_broadcast([P, NT, NE]), ALU.is_equal)
            V.tensor_tensor(te(M2), iota, idfv[:, :, 1:2].to_broadcast([P, NT, NE]), ALU.is_equal)
            link(V.tensor_tensor(gts[:, :, 0], m8v[:, :, 1], m8v[:, :, 0], ALU.subtract))
            V.tensor_tensor(MK, M1, M2, ALU.add).then_inc(s["mk_ready"], 1)
            V.memset(car[:, 0:NE], 0.0).then_inc(s["d_ready"], 1)
            dve.wait_ge(s["ge_ready"], 1)
            link(V.tensor_scalar(gts[:, :, 2], gts[:, :, 1], 1.0, None, ALU.add))
            link(V.reciprocal(gts[:, :, 3], gts[:, :, 2]))
            link(V.tensor_tensor(gts[:, :, 4], gts[:, :, 3], gts[:, :, 1], ALU.mult))
            dve.wait_ge(s["rank_done"], 1)
            link(V.tensor_copy(tots, po[:, 256:256 + NT * NE]))
            for i in range(NT):
                link(V.tensor_tensor(car[:, (i + 1) * NE:(i + 2) * NE], car[:, i * NE:(i + 1) * NE], tots[:, i * NE:(i + 1) * NE], ALU.add))
            link(V.tensor_scalar(exi[:, 0, :], car[:, NT * NE:], float(P - 1), None, ALU.add))
            link(V.tensor_scalar(exi[:, 1, :], exi[:, 0, :], 7, None, ALU.logical_shift_right))
            link(V.tensor_copy(ex8[:, 1, :], exi[:, 1, :]))
            link(V.tensor_tensor_scan(out=ex8[:, 2, :], data0=ones[:, 0:NE], data1=ex8[:, 1, :], initial=0.0, op0=ALU.mult, op1=ALU.add))
            link(V.tensor_tensor(ex8[:, 3, :], ex8[:, 2, :], ex8[:, 1, :], ALU.subtract))
            link(V.tensor_scalar(ex8[:, 4, :], ex8[:, 3, :], float(P), None, ALU.mult))
            link(V.tensor_tensor(pos, po[:, 128:128 + NT * NE], car[:, 0:NT * NE], ALU.add))
            link(V.tensor_tensor(te(pos), te(pos), ex8[:, 4:5, :].to_broadcast([P, NT, NE]), ALU.add))
            for k, M in enumerate((M1, M2)):
                link(V.tensor_tensor(prod, pos, M, ALU.mult))
                link(V.tensor_reduce(out=slotf[:, k, :], in_=te(prod), axis=AX.X, op=ALU.add))
            link(V.tensor_copy(sloti[:, :, :], slotf[:, :, :]))
            slots = sloti[:, :, :].rearrange("p k i -> p (k i)")
            V.tensor_scalar(place[:, 0, :], slots, 7, None, ALU.logical_shift_right)
            link(V.tensor_scalar(place[:, 1, :], slots, P - 1, None, ALU.bitwise_and))
            link(V.tensor_copy(placef[:, :, :], place[:, :, :]))

            def over(x, n):
                return x.rearrange("p (k a) -> p k a", a=1).to_broadcast([P, x.shape[1], n])

            link(V.tensor_tensor(hot_tile, iota_t.rearrange("p (a n) -> p a n", a=1).to_broadcast([P, 2 * NT, MT]),
                                 over(placef[:, 0, :], MT), ALU.is_equal))
            for k in range(2):
                V.tensor_tensor(hot_tile[:, k * NT:(k + 1) * NT], hot_tile[:, k * NT:(k + 1) * NT], over(token_id, MT), ALU.mult)
            for k in range(2):
                V.tensor_tensor(hot_place[:, k * NT:(k + 1) * NT], iota_p.rearrange("p (a n) -> p a n", a=1).to_broadcast([P, NT, P]),
                                over(placef[:, 1, k * NT:(k + 1) * NT], P), ALU.is_equal).then_inc(s["hot_ready"], 1)
            cmpv = cmp[:, :].rearrange("p (t e) -> p t e", e=NE)
            link(V.tensor_tensor(cmpv, ex8[:, 2:3, :].to_broadcast([P, MT, NE]),
                                 iota_t.rearrange("p (t a) -> p t a", a=1).to_broadcast([P, MT, NE]), ALU.is_le))
            link(V.tensor_reduce(out=tmap[:, 0, :], in_=cmpv, axis=AX.X, op=ALU.add))
            link(V.tensor_scalar(tmi[0:1, :], tmap[0:1, 0, :], float(NE - 1), None, ALU.min))
            dve.wait_ge(s["ids_done"], 1)
            V.tensor_copy(row_ids[:, :], pw[:, 0:MT]).then_inc(s["ids_ready"], 1)
            V.tensor_scalar(endi[0:1, :], ex8[0:1, 2, :], 1.0, None, ALU.add).then_inc(s["tmap_ready"], 1)

            V.tensor_copy(identb[:, :], ident).then_inc(s["identb_ready"], 1)

            def round_e4m3(link, dst, v, g):
                link(V.tensor_scalar(g.bitcast(I32), v.bitcast(I32), 0x7F800000, None, ALU.bitwise_and))
                link(V.tensor_scalar(g, g, FP8_LEAST, MAGIC, ALU.max, ALU.mult))
                link(V.tensor_tensor(v, v, g, ALU.add))
                return V.tensor_tensor(dst, v, g, ALU.subtract)

            def recurrence_pieces(b, parity, link):
                E2, U2, fwd, bwd, rat = cond_buf[1]
                n = B + b

                def recur():
                    link(V.tensor_copy(cond1b[:, parity, :], cond1[:, bass.ds(b, 1), :].rearrange("p a n -> p (a n)")))
                    dve.wait_ge(s["u_ready"], n + 1)
                    dve.sem_inc(s["dve_paused"], 1)
                    link(scans(E2[:, parity], fwd, bwd, lambda c: cond1b[:, parity, c:c + 1]))

                def add():
                    link(V.tensor_tensor(fwd[:, :, :], fwd[:, :, :], bwd[:, :, :], ALU.add))
                    V.tensor_tensor(fwd[:, :, :], fwd[:, :, :], U2[:, parity], ALU.add).then_inc(s["u_used"], 1)
                    dve.wait_ge(s["u_used"], n + 1)
                    link(V.tensor_scalar(fwd[:, 1, :], fwd[:, 1, :], 1e-8, None, ALU.max))

                def divide():
                    link(V.reciprocal(bwd[:, 1, :], fwd[:, 1, :]))
                    dve.wait_ge(s["rat_done"], n)
                    V.scalar_tensor_tensor(rat, fwd[:, 0, :], cond1b[:, parity, C:C + 1], bwd[:, 1, :], ALU.mult, ALU.mult)\
                        .then_inc(s["ratT_ready"], 1)

                return [recur, add, divide]

            def weight_pieces(m, link):
                down = isinstance(m, int)
                q, k, n = (P, C, INTER) if down else (IQ, NI, D)
                r, g = rows[0:q, 0:k * n], grid[0:q, 0:k * n]
                r3 = r.rearrange("p (k n) -> p k n", k=k)
                wm, wi = (w[0:q, 0:k] for w in (wmax, winv))

                def scale():
                    dve.wait_ge(s["rows_in"], 32 * NI + 16 if down else m * (16 * NI) + 16 * NI)
                    link(V.tensor_reduce(out=wm, in_=r3, axis=AX.X, op=ALU.max, apply_absolute_value=True))
                    link(V.reciprocal(wi, wm))
                    ws = wscale[0:q, 2, 0:k] if down else wscale[0:q, bass.ds(m, 1), 0:k].rearrange("p a k -> p (a k)")
                    V.tensor_scalar(ws, wm, 1.0 / FP8_MAX, None, ALU.mult).then_inc(s["wscale_ready"], 1)
                    link(V.tensor_scalar(wi, wi, FP8_MAX, None, ALU.mult))
                    link(V.tensor_tensor(r3, r3, wi.rearrange("p (k a) -> p k a", a=1).to_broadcast([q, k, n]), ALU.mult))

                def grids():
                    link(V.tensor_scalar(g.bitcast(I32), r.bitcast(I32), 0x7F800000, None, ALU.bitwise_and))
                    link(V.tensor_scalar(g, g, FP8_LEAST, MAGIC, ALU.max, ALU.mult))

                def round_up():
                    link(V.tensor_tensor(r, r, g, ALU.add))

                def round_down():
                    if down:
                        dve.wait_ge(s["rqT_done"], 2)
                    V.tensor_tensor(rq[0:q, 0:k * n], r, g, ALU.subtract).then_inc(s["rq_ready"], 1)

                return [scale, grids, round_up, round_down]

            def silu(n, part):
                lo, hi = (0, FA) if part == 0 else (FA, FF)
                b = pb[1][:, 0:FA] if part == 0 else sc2[:, 1, 0:FB]
                done = s["inner_a_done" if part == 0 else "inner_b_done"]
                dve.wait_ge(s["silu_a_done" if part == 0 else "silu_b_done"], n + 1)
                if part == 0 and (not isinstance(n, int) or n >= 1):
                    dve.wait_ge(s["hT_done"], n)
                V.tensor_tensor(hh[:, lo:hi], silu_out[:, lo:hi], b, ALU.mult).then_inc(done, 1)

            def w2_low(n, parity):
                e = dve.value_load(tmi[0:1, bass.ds(n, 1)], min_val=0, max_val=NE - 1)
                dve.wait_ge(s["w2hi_done"], n + 1)
                V.scalar_tensor_tensor(w2s[parity][1].rearrange("p c n -> p (c n)"),
                                       wreg[:, bass.ds((e % RING) * WEXP + 2 * C * FF, FC * D)], WS,
                                       w2s[parity][0].rearrange("p c n -> p (c n)"), ALU.mult, ALU.subtract).then_inc(s["w2lo_done"], 1)

            def hT_low(n):
                dve.wait_ge(s["hT_copied"], n + 1)
                V.tensor_tensor(hhT[:, 1, 0:4, :], pt2[:, 0, :].rearrange("p (c n) -> p c n", c=4), hhT[:, 0, 0:4, :], ALU.subtract)
                V.tensor_tensor(hhT[:, 1, 4:FC, :], pt2[:, 1, 0:FB].rearrange("p (c n) -> p c n", c=FC - 4), hhT[:, 0, 4:FC, :],
                                ALU.subtract).then_inc(s["hTlo_done"], 1)

            def tile(n, parity, pieces=()):
                for part in range(2):
                    silu(n, part)
                    if part == 0 and (not isinstance(n, int) or n >= 1):
                        hT_low(n - 1)
                    if part == 1:
                        w2_low(n, parity)
                    if part < len(pieces) and pieces[part]:
                        pieces[part]()

            tile(0, 0)
            LINKS = 17
            with dve.Fori(0, 2) as i:
                round_links = [0]

                def round_link(ins):
                    round_links[0] += 1
                    ins.then_inc(s["side_link"], 1)
                    dve.wait_ge(s["side_link"], i * LINKS + round_links[0])

                w = weight_pieces(i, round_link)
                r0 = recurrence_pieces(i * 2, 0, round_link)
                r1 = recurrence_pieces(i * 2 + 1, 1, round_link)
                order = [(w[0], None), (w[1], w[2]), (r0[0], r0[1]), (r0[2], None), (w[3], r1[0]), (r1[1], None), (r1[2], None), ()]
                for k in range(ROUND):
                    tile(i * ROUND + (k + 1), (k + 1) % 2, order[k])
                assert round_links[0] == LINKS, round_links
            w = weight_pieces(2, link)
            tile(2 * ROUND + 1, 1, w[0:2])
            tile(2 * ROUND + 2, 0, w[2:4])
            with dve.Fori(0, (MT - 2 * ROUND - 3) // 2) as i:
                for k in range(2):
                    tile(i * 2 + 2 * ROUND + 3 + k, 1 - k)
            hT_low(MT - 1)

            dve.wait_ge(s["xsum_ready"], 1)
            dve.wait_ge(s["ratio1_copied"], B)
            dve.wait_ge(s["scale_in"], 16)

            def combine(p):
                dve.wait_ge(s_g[p % 2], 64 * (p // 2 + 1))
                for k in range(2):
                    for i in (2 * p, 2 * p + 1):
                        last = V.scalar_tensor_tensor(x1[:, i, :], y12[:, k, i, :], gts[:, i, 3 + k:4 + k], x1[:, i, :], ALU.mult, ALU.add)
                    if k == 0:
                        link(last)
                last.then_inc(s["x1_ready"], 1)

            def scale_of_rows(at, value, i, n, done=None):
                r = [rs[:, at + k, i:i + n] for k in range(4)]
                link(V.tensor_reduce(out=r[0], in_=value, axis=AX.X, op=ALU.max, apply_absolute_value=True))
                link(V.reciprocal(r[3], r[0]))
                V.tensor_scalar(r[1], r[0], 1.0 / FP8_MAX, None, ALU.mult)
                last = V.tensor_scalar(r[2], r[3], FP8_MAX, None, ALU.mult)
                if done:
                    last.then_inc(done, 1)
                else:
                    link(last)

            def quantise_input(p):
                i = 2 * p
                dve.wait_ge(s["sgx_ready"], p + 1)
                link(V.tensor_tensor(xmix, xsig, ratio1[:, i:i + 2, :].rearrange("p i n -> p (i n)"), ALU.mult))
                scale_of_rows(2, xmix.rearrange("p (i n) -> p i n", i=2), i, 2)
                V.tensor_tensor(rs[:, 1, i:i + 2], rs[:, 3, i:i + 2], rs[:, 3, i:i + 2], ALU.mult)
                for k in range(2):
                    last = V.tensor_scalar(xval[:, k * D:(k + 1) * D], xmix[:, k * D:(k + 1) * D], rs[:, 4, i + k:i + k + 1], None, ALU.mult)
                link(last)
                if p >= 2:
                    dve.wait_ge(s["qxT_done"], i - 2)
                round_e4m3(link, qx[:, p % 2].rearrange("p i n -> p (i n)"), xval, xgrid).then_inc(s["qx_ready"], 1)

            def gate_rows(i):
                dve.wait_ge(s["gatep_done"], i + 1)
                if i >= 1:
                    dve.wait_ge(s["p_ready"], i)
                for k in range(2):
                    last = V.tensor_tensor(gate[:, k * IH:(k + 1) * IH], pb[k][:, 0:IH], srow[:, k * IH:(k + 1) * IH], ALU.mult)
                last.then_inc(s["gate_ready"], 1)

            def inner_rows(i):
                dve.wait_ge(s["p_ready"], i + 1)
                if i >= 1:
                    dve.wait_ge(s["scaled_ready"], i)
                link(V.scalar_tensor_tensor(tval, gprods[i % 2], rs[:, 1, i:i + 1], upvs[i % 2], ALU.mult, ALU.mult))
                scale_of_rows(6, tval, i, 1, s["inv_ready"])

            def round_inner(i):
                dve.wait_ge(s["scaled_ready"], i + 1)
                if i >= 1:
                    dve.wait_ge(s["qtT_done"], i)
                round_e4m3(link, qt[:, :], tscaled, tgrid).then_inc(s["qt_ready"], 1)

            def output_rows(i):
                k = i % 2
                dve.wait_ge(s["dn_done"], i + 1)
                if i >= 2:
                    dve.wait_ge(s_o[k], 16 * (i // 2))
                V.scalar_tensor_tensor(yo[:, k, :], pw[:, 0:D], rs[:, 7, i:i + 1], srow[:, 2 * INTER:], ALU.mult, ALU.mult)\
                    .then_inc(s["yo_read"], 1)

            combine(0)
            quantise_input(0)
            gate_rows(0)
            combine(1)
            for i in range(NT):
                if i + 1 < NT:
                    gate_rows(i + 1)
                inner_rows(i)
                if i % 2 == 1 and i + 3 < NT:
                    combine((i + 3) // 2)
                if i % 2 == 0 and i + 2 < NT:
                    quantise_input((i + 2) // 2)
                if i >= 1:
                    output_rows(i - 1)
                round_inner(i)
            output_rows(NT - 1)

        @block.gpsimd
        def _(pool):
            G = nc.gpsimd
            links = [0]

            def link(ins):
                links[0] += 1
                ins.then_inc(s["pool_link"], 1)
                pool.wait_ge(s["pool_link"], links[0])

            link(G.memset(nhalf[:, :], -0.5))

            def rstd(first, count, done):
                link(G.tensor_scalar(ssq[:, 1, first:first + count], ssq[:, 0, first:first + count], 1.0 / D, EPS, ALU.mult, ALU.add))
                G.tensor_tensor(ssq[:, 2, first:first + count], ssq[:, 1, first:first + count], nhalf[:, 0:count], ALU.pow).then_inc(done, 1)

            def recurrence_inputs(l, b):
                n = l * B + b
                E, U = cond_buf[l][0][:, b % 2], cond_buf[l][1][:, b % 2]
                if l == 0:
                    pool.wait_ge(s["fT_copied"], b + 1)
                if n >= 2:
                    pool.wait_ge(s["u_used"], n - 1)
                if l == 0:
                    pool.wait_ge(s["ek_ready"], b + 1)
                    G.tensor_tensor(E[:, 0, :], E[:, 1, :], fT[:, b, :], ALU.mult).then_inc(s["e_ready"], 1)
                else:
                    G.tensor_scalar(E[:, 1, :], fT[:, b, :], 30.0, None, ALU.min)
                if n >= 1:
                    if n == 1:
                        pool.wait_ge(s["ku_ready"], 1)
                    shifted_keys(G, U, l, b)
                pool.wait_ge(s["uexp_ready"], n + 1)
                if l == 1:
                    G.tensor_tensor(E[:, 0, :], E[:, 1, :], fT[:, b, :], ALU.mult)
                link(G.tensor_tensor(U[:, 0, :], U[:, 1, :], fT[:, b, :], ALU.mult))
                G.tensor_tensor(U, U, E, ALU.subtract).then_inc(s["u_ready"], 1)

            recurrence_inputs(0, 0)
            for b in range(B):
                if b + 1 < B:
                    recurrence_inputs(0, b + 1)
                pool.wait_ge(s["ssq_ready"], b + 1)
                rstd(TT * b, TT, s["rstd_ready"])

            def rotated(n, parity, dst):
                pool.wait_ge(s["sin_done"], n + 1)
                G.tensor_tensor(dst, t1[:, parity, :], t2[:, parity, :], ALU.add).then_inc(s["radd_done"], 1)

            def rope_sum(n, parity):
                pool.wait_ge(s["swap_done"], n + 1)
                G.tensor_tensor(t2[:, parity, :].rearrange("p (b n) -> p b n", b=2), t2[:, parity, :].rearrange("p (b n) -> p b n", b=2),
                                rope_sin.rearrange("p (a n) -> p a n", a=1).to_broadcast([P, 2, S]), ALU.mult).then_inc(s["sin_done"], 1)
                if not isinstance(n, int) or n >= KU + 2:
                    pool.wait_ge(s["score_done"], n - KU - 1)
                rotated(n, parity, qr[:, parity, :])

            pool.wait_ge(s["con_in"], 16)
            for n in range(KU):
                rotated(n, n % 2, kT[:, n % KVH, n // KVH * PAIR:(n // KVH + 1) * PAIR])

            def normalise_second(u, parity):
                pool.wait_ge(s["recip_done"], u + 1)
                for qb in range(2):
                    o, w = (0, P) if qb == 0 else (P, 2 * P)
                    last = G.tensor_tensor(pr[:, parity, 1, o:o + w], pr[:, parity, 1, o:o + w],
                                           sums[:, parity, 1, 2 + qb:3 + qb].to_broadcast([P, w]), ALU.mult)
                last.then_inc(s["norm2_done"], 1)

            def step(u, parity):
                if within(u, 3):
                    normalise_second(u - 3, 1 - parity)
                if within(u, 0):
                    rope_sum(KU + u, parity)

            attention_steps(pool, step, lambda: None)

            pool.wait_ge(s["av_done"], QU)
            pool.wait_ge(s["didx_in"], 16)

            def gather_rows(name):
                for c in range(NI):
                    G.indirect_dma_start(out=rows[0:IQ, c * D:(c + 1) * D], out_offset=None, in_=t[name],
                                         in_offset=bass.IndirectOffsetOnAxis(ap=didx[:, c:c + 1], axis=0)).then_inc(s["rows_in"], 16)

            for i in range(NT):
                pool.wait_ge(s["ssq2_ready"], i + 1)
                rstd(i, 1, s["rstd2_ready"])
            gather_rows("L1_ffn_w_gate")
            pool.wait_ge(s["h2_out"], 16 * NT)
            pool.wait_ge(s["ids_ready"], 1)

            def gather_tiles(*tiles):
                for n in tiles:
                    if n >= 4:
                        pool.wait_ge(s["xT_done"], n - 3)
                    G.indirect_dma_start(out=xs[n % 4], out_offset=None, in_=h2_dram[:, :],
                                         in_offset=bass.IndirectOffsetOnAxis(ap=row_ids[:, n:n + 1], axis=0)).then_inc(s_xs[n % 4], 16)

            def send_scales(m):
                q, k, at = (IQ, NI, m * INTER) if m < 2 else (P, C, 2 * INTER)
                pool.wait_ge(s["wscale_ready"], m + 1)
                with nc.allow_non_contiguous_dma(reason="a scale of each partition"):
                    G.dma_start(scale_dram[at:at + q * k].rearrange("(k p) -> p k", p=q), wscale[0:q, m, 0:k]).then_inc(s["scale_out"], 16)

            gather_tiles(0, 1, 2, 3)
            recurrence_inputs(1, 0)
            gather_tiles(4, 5, 6)
            recurrence_inputs(1, 1)
            gather_tiles(7, 8)
            pool.wait_ge(s["rq_ready"], 1)
            gather_rows("L1_ffn_w_up")
            gather_tiles(9, 10)
            send_scales(0)
            recurrence_inputs(1, 2)
            gather_tiles(11, 12, 13)
            recurrence_inputs(1, 3)
            gather_tiles(14, 15, 16)
            pool.wait_ge(s["rq_ready"], 2)
            G.dma_start(rows[:, 0:C * INTER].rearrange("p (c n) -> p c n", c=C),
                        t["L1_ffn_w_down"].rearrange("(c p) n -> p c n", p=P)).then_inc(s["rows_in"], 16)
            send_scales(1)
            gather_tiles(17, 18)
            G.tensor_tensor(x0[:, :, :].rearrange("p i n -> p (i n)"), x0[:, :, :].rearrange("p i n -> p (i n)"),
                            x_in[:, :, :].rearrange("p b n -> p (b n)"), ALU.add).then_inc(s["xsum_ready"], 1)
            gather_tiles(19, 20, 21, 22)
            send_scales(2)
            pool.wait_ge(s["scale_out"], 48)
            G.dma_start(srow[:, :], scale_dram.rearrange("(a n) -> a n", a=1).to_broadcast([P, 2 * INTER + D])).then_inc(s["scale_in"], 16)
            pool.wait_ge(s["u_used"], 2 * B)
            pool.wait_ge(s_y[0], 16 * ((MT + 1) // 2 + 1))
            pool.wait_ge(s_y[1], 16 * (MT // 2 + 1))
            def gather_pair(p):
                for i in (2 * p, 2 * p + 1):
                    for k in range(2):
                        G.indirect_dma_start(out=y12[:, k, i, :], out_offset=None, in_=ys_dram[:, :],
                                             in_offset=bass.IndirectOffsetOnAxis(ap=sloti[:, k, i:i + 1], axis=0)).then_inc(s_g[p % 2], 16)

            def add_input(i):
                pool.wait_ge(s["yo_read"], i + 1)
                G.tensor_tensor(yo[:, i % 2, :], yo[:, i % 2, :], x1[:, i, :], ALU.add).then_inc(s["yo_ready"], 1)

            def gate_times(i):
                pool.wait_ge(s["gsig_ready"], i + 1)
                G.tensor_tensor(gprods[i % 2], gate, gsig, ALU.mult)
                pool.wait_ge(s["up_ready"], i + 1)
                G.tensor_tensor(upvs[i % 2], upvs[i % 2], srow[:, INTER:2 * INTER], ALU.mult).then_inc(s["p_ready"], 1)

            gather_pair(0)
            gather_pair(1)
            gate_times(0)
            for i in range(NT):
                if i + 1 < NT:
                    gate_times(i + 1)
                if i < 2:
                    pool.wait_ge(s_g[i], 64)
                    gather_pair(i + 2)
                if i >= 1:
                    add_input(i - 1)
            add_input(NT - 1)


INPUTS = ["x", "fside_BxSxS_0", "cond_512", "L0_cond_w", "L0_cond_u", "L0_ffn_ln_w", "L0_ffn_ff_ln_w", "L0_ffn_wq", "L0_ffn_wk",
          "L0_ffn_wv", "L0_ffn_wo", "L0_ffn_gate_w", "L0_ffn_w1", "L0_ffn_w3", "L0_ffn_w2", "L1_cond_w", "L1_cond_u",
          "L1_ffn_w_gate", "L1_ffn_w_up", "L1_ffn_w_down", "L1_ffn_down_reorder_index"]


def kernel(**inputs):
    import concourse.bacc as bacc
    from concourse.bass_utils import run_bass_kernel_spmd as run

    nc = bacc.Bacc("TRN2", target_bir_lowering=False, num_devices=1)
    arrays, t = {}, {}
    for name in INPUTS:
        arrays[f"in_{name}"] = np.ascontiguousarray(inputs[name])
    arrays["in_consts"] = constants()
    for name, a in arrays.items():
        t[name[3:]] = nc.dram_tensor(name, a.shape, mybir.dt.from_np(a.dtype), kind="ExternalInput").ap()
    out = nc.dram_tensor("out_dram", (B, S, D), F32, kind="ExternalOutput").ap()
    build(nc, t, out)
    return run(nc, [arrays], core_ids=[0]).results[0]["out_dram"]
```
